# Optimizing a Trainium2 kernel written in Bass

```python
import numpy as np
import jax
import jax.numpy as jnp

def _softmax(x, axis=-1):
    return jax.nn.softmax(x, axis=axis)

def _gelu(x):
    return jax.nn.gelu(x, approximate=True)

def _silu(x):
    return jax.nn.silu(x)

def _sigmoid(x):
    return jax.nn.sigmoid(x)

def _layernorm(x, axis=-1, eps=1e-05):
    m = jnp.mean(x, axis=axis, keepdims=True)
    v = jnp.var(x, axis=axis, keepdims=True)
    return (x - m) / jnp.sqrt(v + eps)

def _scatter_add(tgt, idx, src, axis=0):
    return tgt.at[idx].add(src)

def _segment_sum(src, seg, n):
    return jax.ops.segment_sum(src, seg, n)
kernel_name = 'mk_decoder_postln_d1_seqx_r4_2d63ca'

def setup_inputs(seed: int=0):
    np.random.seed(seed)
    _w = jnp.asarray

    def _rec_inputs():
        import jax
        import jax.numpy as jnp
        _rk = jax.random.key(seed)
        x = 2.818e-05 + 1 * jax.random.normal(jax.random.fold_in(_rk, 1), (4, 512, 512), jnp.float32)
        _lenS = 512 - jax.random.randint(jax.random.fold_in(_rk, 7), (4,), 0, max(1, 512 // 4) + 1, jnp.int32)
        _lenS2 = 512 - jax.random.randint(jax.random.fold_in(_rk, 8), (4,), 0, max(1, 512 // 4) + 1, jnp.int32)
        _ctx_1024P = jax.random.normal(jax.random.fold_in(_rk, 11), (4, 16, 256), jnp.float32)
        _ctx_1024c = jax.random.dirichlet(jax.random.fold_in(_rk, 511), 0.3 * jnp.ones((16,), jnp.float32), (4, 512))
        _ctx_1024t = jnp.einsum('bsk,bkd->bsd', _ctx_1024c, _ctx_1024P)
        _ctx_1024t = _ctx_1024t * jax.lax.rsqrt(jnp.mean(jnp.square(_ctx_1024t)) + 1e-12) * 0.953939
        ctx_1024 = 7.22013e-05 + 1.00017 * (_ctx_1024t + 0.3 * jax.random.normal(jax.random.fold_in(_rk, 611), (4, 512, 256), jnp.float32))
        return (x, ctx_1024)
    x, ctx_1024 = _rec_inputs()

    def _L0_attn_setup():
        import jax, jax.numpy as jnp
        import numpy as np
        IN_FEATURES = 512
        HEAD_NUM = 64
        D = IN_FEATURES // HEAD_NUM
        SCALE = float(np.sqrt(D))
        key = jax.random.key(seed)
        ks = jax.random.split(key, 9)
        F = IN_FEATURES
        x = jax.random.normal(ks[0], (4, 256, F), dtype=jnp.float32)
        w = lambda k: jax.random.normal(k, (F, F), dtype=jnp.float32) * 0.02
        b = lambda k: jax.random.normal(k, (F,), dtype=jnp.float32) * 0.01
        return {'x': x, 'Wq': w(ks[1]), 'bq': b(ks[2]), 'Wk': w(ks[3]), 'bk': b(ks[4]), 'Wv': w(ks[5]), 'bv': b(ks[6]), 'Wo': w(ks[7]), 'bo': b(ks[8])}
    _L0_attn_all = _L0_attn_setup()
    _L0_attn_in = {k: v for k, v in _L0_attn_all.items() if k in ('Wq', 'bq', 'Wk', 'bk', 'Wv', 'bv', 'Wo', 'bo')}
    del _L0_attn_all

    def _L0_xattn_setup():
        import jax, jax.numpy as jnp
        import numpy as np
        B_, L_, D_MODEL = (4, 512, 256)
        D_STATE, D_CONV, EXPAND = (16, 4, 2)
        D_INNER = EXPAND * D_MODEL
        DT_RANK = (D_MODEL + 15) // 16

        def silu(x):
            return x * jax.nn.sigmoid(x)
        key = jax.random.key(seed)
        ks = jax.random.split(key, 10)
        f32 = jnp.float32
        hidden_states = jax.random.normal(ks[0], (B_, L_, D_MODEL), dtype=f32)
        z = jax.random.normal(ks[1], (B_, D_INNER, L_), dtype=f32)
        in_proj_w = jax.random.normal(ks[2], (D_INNER, D_MODEL), dtype=f32) * 0.02
        conv_w = jax.random.normal(ks[3], (D_INNER, 1, D_CONV), dtype=f32) * 0.1
        conv_b = jax.random.normal(ks[4], (D_INNER,), dtype=f32) * 0.02
        x_proj_w = jax.random.normal(ks[5], (DT_RANK + 2 * D_STATE, D_INNER), dtype=f32) * 0.02
        dt_proj_w = jax.random.uniform(ks[6], (D_INNER, DT_RANK), dtype=f32, minval=-DT_RANK ** (-0.5), maxval=DT_RANK ** (-0.5))
        dt = jnp.exp(jax.random.uniform(ks[7], (D_INNER,), dtype=f32, minval=np.log(0.001), maxval=np.log(0.1)))
        dt_proj_b = jnp.log(jnp.expm1(dt))
        A_log = jnp.log(jnp.broadcast_to(jnp.arange(1, D_STATE + 1, dtype=f32), (D_INNER, D_STATE)))
        D = jnp.ones((D_INNER,), f32)
        return {'hidden_states': hidden_states, 'z': z, 'in_proj_w': in_proj_w, 'conv_w': conv_w, 'conv_b': conv_b, 'x_proj_w': x_proj_w, 'dt_proj_w': dt_proj_w, 'dt_proj_b': dt_proj_b, 'A_log': A_log, 'D': D}
    _L0_xattn_all = _L0_xattn_setup()
    _L0_xattn_in = {k: v for k, v in _L0_xattn_all.items() if k in ('in_proj_w', 'conv_w', 'conv_b', 'x_proj_w', 'dt_proj_w', 'dt_proj_b', 'A_log', 'D')}
    del _L0_xattn_all

    def _L0_ffn_setup():
        import jax, jax.numpy as jnp
        import numpy as np
        ROPE_THETA = 1000000.0
        TOP_K = 2

        def rmsnorm(x, w, eps=1e-06):
            xf = x.astype(jnp.float32)
            n = jax.lax.rsqrt(jnp.mean(xf * xf, axis=-1, keepdims=True) + eps)
            return (xf * n).astype(x.dtype) * w

        def rope_tables(seq_len, head_dim):
            freqs = 1.0 / ROPE_THETA ** (jnp.arange(0, head_dim, 2, dtype=jnp.float32) / head_dim)
            t = jnp.arange(seq_len, dtype=jnp.float32)
            f = jnp.outer(t, freqs)
            return (jnp.cos(f), jnp.sin(f))

        def apply_rope(x, cos, sin):
            half = x.shape[-1] // 2
            x1, x2 = (x[..., :half], x[..., half:])
            c = cos[None, None]
            s = sin[None, None]
            return jnp.concatenate([x1 * c - x2 * s, x2 * c + x1 * s], axis=-1)
        key = jax.random.key(seed)
        ks = jax.random.split(key, 8)
        B, S, D = (2, 512, 512)
        Hq, Hkv, hd = (16, 4, 128)
        E, I = (8, 352)
        sc = 0.02
        return {'hidden': jax.random.normal(ks[0], (B, S, D), jnp.float32), 'attn_norm_w': jnp.ones((D,), jnp.float32), 'q_w': jax.random.normal(ks[1], (Hq * hd, D), jnp.float32) * sc, 'k_w': jax.random.normal(ks[2], (Hkv * hd, D), jnp.float32) * sc, 'v_w': jax.random.normal(ks[3], (Hkv * hd, D), jnp.float32) * sc, 'o_w': jax.random.normal(ks[4], (D, Hq * hd), jnp.float32) * sc, 'q_norm_w': jnp.ones((hd,), jnp.float32), 'k_norm_w': jnp.ones((hd,), jnp.float32), 'ffn_norm_w': jnp.ones((D,), jnp.float32), 'gate_w': jax.random.normal(ks[5], (E, D), jnp.float32) * sc, 'wg': jax.random.normal(ks[6], (E, I, D), jnp.float32) * sc, 'wu': jax.random.normal(ks[7], (E, I, D), jnp.float32) * sc, 'wd': jax.random.normal(jax.random.fold_in(key, 99), (E, D, I), jnp.float32) * sc}
    _L0_ffn_all = _L0_ffn_setup()
    _L0_ffn_in = {k: v for k, v in _L0_ffn_all.items() if k in ('attn_norm_w', 'q_w', 'k_w', 'v_w', 'o_w', 'q_norm_w', 'k_norm_w', 'ffn_norm_w', 'gate_w', 'wg', 'wu', 'wd')}
    del _L0_ffn_all
    return {'x': x, 'ctx_1024': ctx_1024, 'L0_attn_Wq': _L0_attn_in['Wq'], 'L0_attn_bq': _L0_attn_in['bq'], 'L0_attn_Wk': _L0_attn_in['Wk'], 'L0_attn_bk': _L0_attn_in['bk'], 'L0_attn_Wv': _L0_attn_in['Wv'], 'L0_attn_bv': _L0_attn_in['bv'], 'L0_attn_Wo': _L0_attn_in['Wo'], 'L0_attn_bo': _L0_attn_in['bo'], 'L0_xattn_in_proj_w': _L0_xattn_in['in_proj_w'], 'L0_xattn_conv_w': _L0_xattn_in['conv_w'], 'L0_xattn_conv_b': _L0_xattn_in['conv_b'], 'L0_xattn_x_proj_w': _L0_xattn_in['x_proj_w'], 'L0_xattn_dt_proj_w': _L0_xattn_in['dt_proj_w'], 'L0_xattn_dt_proj_b': _L0_xattn_in['dt_proj_b'], 'L0_xattn_A_log': _L0_xattn_in['A_log'], 'L0_xattn_D': _L0_xattn_in['D'], 'L0_ffn_attn_norm_w': _L0_ffn_in['attn_norm_w'], 'L0_ffn_q_w': _L0_ffn_in['q_w'], 'L0_ffn_k_w': _L0_ffn_in['k_w'], 'L0_ffn_v_w': _L0_ffn_in['v_w'], 'L0_ffn_o_w': _L0_ffn_in['o_w'], 'L0_ffn_q_norm_w': _L0_ffn_in['q_norm_w'], 'L0_ffn_k_norm_w': _L0_ffn_in['k_norm_w'], 'L0_ffn_ffn_norm_w': _L0_ffn_in['ffn_norm_w'], 'L0_ffn_gate_w': _L0_ffn_in['gate_w'], 'L0_ffn_wg': _L0_ffn_in['wg'], 'L0_ffn_wu': _L0_ffn_in['wu'], 'L0_ffn_wd': _L0_ffn_in['wd']}

def reference(x, ctx_1024, L0_attn_Wq, L0_attn_bq, L0_attn_Wk, L0_attn_bk, L0_attn_Wv, L0_attn_bv, L0_attn_Wo, L0_attn_bo, L0_xattn_in_proj_w, L0_xattn_conv_w, L0_xattn_conv_b, L0_xattn_x_proj_w, L0_xattn_dt_proj_w, L0_xattn_dt_proj_b, L0_xattn_A_log, L0_xattn_D, L0_ffn_attn_norm_w, L0_ffn_q_w, L0_ffn_k_w, L0_ffn_v_w, L0_ffn_o_w, L0_ffn_q_norm_w, L0_ffn_k_norm_w, L0_ffn_ffn_norm_w, L0_ffn_gate_w, L0_ffn_wg, L0_ffn_wu, L0_ffn_wd):
    import jax
    import jax.numpy as jnp

    def _L0_attn_ref(x, Wq, bq, Wk, bk, Wv, bv, Wo, bo):
        import jax, jax.numpy as jnp
        import numpy as np
        IN_FEATURES = 512
        HEAD_NUM = 64
        D = IN_FEATURES // HEAD_NUM
        SCALE = float(np.sqrt(D))
        B, S, F = x.shape
        d = D
        h = F // d
        q = x @ Wq + bq
        k = x @ Wk + bk
        v = x @ Wv + bv

        def to_heads(t):
            return t.reshape(B, S, d, h).transpose(0, 2, 1, 3)
        q, k, v = (to_heads(q), to_heads(k), to_heads(v))
        scores = jnp.einsum('bdsh,bdth->bdst', q, k) / SCALE
        weights = jax.nn.softmax(scores, axis=-1)
        feats = jnp.einsum('bdst,bdth->bdsh', weights, v)
        feats = feats.transpose(0, 2, 1, 3).reshape(B, S, F)
        return feats @ Wo + bo

    def _L0_xattn_ref(hidden_states, z, in_proj_w, conv_w, conv_b, x_proj_w, dt_proj_w, dt_proj_b, A_log, D):
        import jax, jax.numpy as jnp
        import numpy as np
        B_, L_, D_MODEL = (4, 512, 256)
        D_STATE, D_CONV, EXPAND = (16, 4, 2)
        D_INNER = EXPAND * D_MODEL
        DT_RANK = (D_MODEL + 15) // 16

        def silu(x):
            return x * jax.nn.sigmoid(x)
        Bsz, L, _ = hidden_states.shape
        d_inner, _, d_conv = conv_w.shape
        dt_rank = dt_proj_w.shape[1]
        d_state = A_log.shape[1]
        x = jnp.einsum('bld,ed->bel', hidden_states, in_proj_w)
        xc = jax.lax.conv_general_dilated(x, conv_w, window_strides=(1,), padding=[(d_conv - 1, 0)], feature_group_count=d_inner, dimension_numbers=('NCH', 'OIH', 'NCH'))
        x = silu(xc + conv_b[None, :, None])
        x_dbl = jnp.einsum('bdl,ed->bel', x, x_proj_w)
        dt_low, Bm, Cm = jnp.split(x_dbl, [dt_rank, dt_rank + d_state], axis=1)
        dt = jnp.einsum('brl,dr->bdl', dt_low, dt_proj_w)
        dt = jax.nn.softplus(dt + dt_proj_b[None, :, None])
        A = -jnp.exp(A_log)
        dt_t = jnp.moveaxis(dt, -1, 0)
        B_t = jnp.moveaxis(Bm, -1, 0)
        C_t = jnp.moveaxis(Cm, -1, 0)
        u_t = jnp.moveaxis(x, -1, 0)

        def step(state, inp):
            d, b, c, u = inp
            dA = jnp.exp(d[..., None] * A)
            state = state * dA + (d * u)[..., None] * b[:, None, :]
            y = jnp.einsum('bdn,bn->bd', state, c)
            return (state, y)
        state0 = jnp.zeros((Bsz, d_inner, d_state), x.dtype)
        _, ys = jax.lax.scan(step, state0, (dt_t, B_t, C_t, u_t))
        y = jnp.moveaxis(ys, 0, 2)
        y = y + D[None, :, None] * x
        y = y * silu(z)
        return jnp.swapaxes(y, 1, 2)

    def _L0_ffn_ref(hidden, attn_norm_w, q_w, k_w, v_w, o_w, q_norm_w, k_norm_w, ffn_norm_w, gate_w, wg, wu, wd):
        import jax, jax.numpy as jnp
        import numpy as np
        ROPE_THETA = 1000000.0
        TOP_K = 2

        def rmsnorm(x, w, eps=1e-06):
            xf = x.astype(jnp.float32)
            n = jax.lax.rsqrt(jnp.mean(xf * xf, axis=-1, keepdims=True) + eps)
            return (xf * n).astype(x.dtype) * w

        def rope_tables(seq_len, head_dim):
            freqs = 1.0 / ROPE_THETA ** (jnp.arange(0, head_dim, 2, dtype=jnp.float32) / head_dim)
            t = jnp.arange(seq_len, dtype=jnp.float32)
            f = jnp.outer(t, freqs)
            return (jnp.cos(f), jnp.sin(f))

        def apply_rope(x, cos, sin):
            half = x.shape[-1] // 2
            x1, x2 = (x[..., :half], x[..., half:])
            c = cos[None, None]
            s = sin[None, None]
            return jnp.concatenate([x1 * c - x2 * s, x2 * c + x1 * s], axis=-1)
        B, S, D = hidden.shape
        hd = q_norm_w.shape[0]
        Hq = q_w.shape[0] // hd
        Hkv = k_w.shape[0] // hd
        n_rep = Hq // Hkv
        h = rmsnorm(hidden, attn_norm_w)
        q = (h @ q_w.T).reshape(B, S, Hq, hd)
        k = (h @ k_w.T).reshape(B, S, Hkv, hd)
        v = (h @ v_w.T).reshape(B, S, Hkv, hd)
        q = rmsnorm(q, q_norm_w).transpose(0, 2, 1, 3)
        k = rmsnorm(k, k_norm_w).transpose(0, 2, 1, 3)
        v = v.transpose(0, 2, 1, 3)
        cos, sin = rope_tables(S, hd)
        q = apply_rope(q, cos, sin)
        k = apply_rope(k, cos, sin)
        k = jnp.repeat(k, n_rep, axis=1)
        v = jnp.repeat(v, n_rep, axis=1)
        scale = 1.0 / jnp.sqrt(jnp.float32(hd))
        scores = jnp.einsum('bhqd,bhkd->bhqk', q, k) * scale
        causal = jnp.tril(jnp.ones((S, S), bool))
        scores = jnp.where(causal[None, None], scores, jnp.finfo(scores.dtype).min)
        attn = jnp.einsum('bhqk,bhkd->bhqd', jax.nn.softmax(scores, axis=-1), v)
        attn = attn.transpose(0, 2, 1, 3).reshape(B, S, Hq * hd)
        hidden = hidden + attn @ o_w.T
        h2 = rmsnorm(hidden, ffn_norm_w)
        T = B * S
        E = gate_w.shape[0]
        tok = h2.reshape(T, D)
        probs = jax.nn.softmax(tok @ gate_w.T, axis=-1)
        topv, topi = jax.lax.top_k(probs, TOP_K)
        topw = topv / (jnp.sum(topv, axis=-1, keepdims=True) + 1e-09)
        combine = jnp.zeros((T, E), tok.dtype).at[jnp.arange(T)[:, None], topi].set(topw)
        eg = jnp.einsum('td,eid->eti', tok, wg)
        eu = jnp.einsum('td,eid->eti', tok, wu)
        eo = jnp.einsum('eti,edi->etd', jax.nn.silu(eg) * eu, wd)
        moe_out = jnp.einsum('te,etd->td', combine, eo).reshape(B, S, D)
        return hidden + moe_out
    x = _layernorm(x + _L0_attn_ref(x, L0_attn_Wq, L0_attn_bq, L0_attn_Wk, L0_attn_bk, L0_attn_Wv, L0_attn_bv, L0_attn_Wo, L0_attn_bo), axis=-1)
    x = _layernorm(x + _L0_xattn_ref(ctx_1024, x, L0_xattn_in_proj_w, L0_xattn_conv_w, L0_xattn_conv_b, L0_xattn_x_proj_w, L0_xattn_dt_proj_w, L0_xattn_dt_proj_b, L0_xattn_A_log, L0_xattn_D), axis=-1)
    x = _layernorm(x + _L0_ffn_ref(x, L0_ffn_attn_norm_w, L0_ffn_q_w, L0_ffn_k_w, L0_ffn_v_w, L0_ffn_o_w, L0_ffn_q_norm_w, L0_ffn_k_norm_w, L0_ffn_ffn_norm_w, L0_ffn_gate_w, L0_ffn_wg, L0_ffn_wu, L0_ffn_wd), axis=-1)
    return x

_drawn_inputs = setup_inputs


def setup_inputs(seed=0):
    import zlib

    import numpy as np

    out = dict(_drawn_inputs(seed))
    spreads = {'L0_xattn_D': (1.0, 0.6),
     'L0_ffn_attn_norm_w': (1.0, 0.6),
     'L0_ffn_q_norm_w': (1.0, 0.6),
     'L0_ffn_k_norm_w': (1.0, 0.6),
     'L0_ffn_ffn_norm_w': (1.0, 0.6)}
    factors = {'ctx_1024': 2.89,
     'L0_attn_Wq': 7.236,
     'L0_attn_bq': 8.0,
     'L0_attn_Wk': 7.227,
     'L0_attn_bk': 8.0,
     'L0_attn_Wv': 4.731,
     'L0_attn_bv': 8.0,
     'L0_attn_Wo': 4.273,
     'L0_attn_bo': 5.814,
     'L0_xattn_in_proj_w': 2.892,
     'L0_xattn_conv_w': 2.949,
     'L0_xattn_conv_b': 8.0,
     'L0_xattn_x_proj_w': 8.0,
     'L0_xattn_dt_proj_w': 8.0,
     'L0_xattn_dt_proj_b': 8.0,
     'L0_xattn_A_log': 8.0,
     'L0_ffn_gate_w': 4.07,
     'L0_ffn_wg': 3.65,
     'L0_ffn_wu': 3.579,
     'L0_ffn_wd': 3.579}
    for name, (base, spread) in spreads.items():
        noise = np.random.default_rng([zlib.crc32(name.encode()), seed]).standard_normal(out[name].shape)
        drawn = base * np.exp(spread * noise) if base else spread * noise
        out[name] = jnp.asarray(drawn.astype(out[name].dtype))
    for name, factor in factors.items():
        out[name] = (out[name] * factor).astype(out[name].dtype)
    return out
```

```python
from contextlib import ExitStack

import numpy as np

import concourse.bass as bass
from concourse import mybir
from concourse.alu_op_type import AluOpType as ALU

F32 = mybir.dt.float32
ACT = mybir.ActivationFunctionType
AX = mybir.AxisListType

P = 128


class Signal:

    def __init__(self, sem, per_turn=0, primed=False):
        self.sem, self.per, self.n, self.primed = sem, per_turn, 0, primed

    def prime(self, engine):
        engine.sem_inc(self.sem, 1)

    def inc(self, instruction, by=1):
        self.n += by
        return instruction.then_inc(self.sem, by)

    def wait(self, engine, turn, count):
        assert count > 0 or self.primed
        engine.wait_ge(self.sem, turn * self.per + (count + self.primed))

    def wait_last(self, engine, turn):
        self.wait(engine, turn, self.n)

    def wait_all(self, engine, count):
        engine.wait_ge(self.sem, count + self.primed)

    def close(self):
        assert self.n == self.per, (self.sem, self.n, self.per)


def attention_and_scan(nc, io, x2_dram, bc_dram):
    B, S, F = io["x"].shape
    DM = io["ctxT"].shape[1]
    NS = io["A_log"].shape[1]
    R = io["dt_wT"].shape[0]
    XD = R + 2 * NS
    KC = io["conv_w"].shape[1]
    HD = 64
    NH = F // HD
    FT, ST, MT = F // P, S // P, DM // P
    NPAIR = NH // 2
    QSCALE = float(1.0 / np.sqrt(float(NH)))
    SMALL = 2.0 ** -7
    assert NS == 2 * NH and ST == 4 and FT == 4

    uses = [("in", e, "act") for e in range(FT)] + [("xp", 0, "act")] + [("dt", e, "dve") for e in range(FT)]
    for p in range(NPAIR):
        uses += [("q", p, "act"), ("k", p, "act"), ("v", p, "dve")]
    uses += [("wo", i, "dve") for i in range(ST)] + [("gT", i, "dve") for i in range(ST)]
    PPU = {(what, k): n for n, (what, k, _) in enumerate(uses)}
    NPP = len(uses)
    emptied = {"act": [0], "dve": [0]}
    for _, _, who in uses:
        for w in emptied:
            emptied[w].append(emptied[w][-1] + (w == who))

    with ExitStack() as ctx:
        def sb(name, shape, dt=F32):
            return ctx.enter_context(nc.sbuf_tensor("p1_" + name, shape, dt))

        def sig(name, per=0, primed=False):
            return Signal(ctx.enter_context(nc.semaphore("p1_" + name)), per, primed)

        wq, wk, wv, wo = (sb(f"w{c}_sb", [P, FT, F]) for c in "qkvo")
        w_in = sb("w_in", [P, MT, F])
        w_xp = sb("w_xp", [P, FT, XD])
        w_dt = sb("w_dt", [R, F])
        conv_w = sb("conv_w_sb", [P, FT, KC])
        cols = sb("cols", [P, 7, FT])
        a_log = sb("a_log", [P, FT, NS])
        a_neg = sb("a_neg", [P, FT, NS])
        bv_row = sb("bv_row", [P, F])
        bo_row = sb("bo_row", [P, F])
        ident = sb("ident_sb", [P, P])
        mhalf = sb("mhalf", [P, 2 * ST])
        xT = sb("xT_sb", [P, FT, S])
        ctxT = sb("ctxT_sb", [P, MT, S])
        xtok = sb("xtok", [P, ST, F])
        xin = sb("xin", [P, FT, S + KC - 1])
        u = sb("u", [P, FT, S])
        dt = sb("dt", [P, FT, S])
        dtu = sb("dtu", [P, FT, S])
        yacc = sb("yacc", [P, FT, S])
        xdbl = sb("xdbl", [XD, S])
        decay = sb("decay", [P, 2, FT, S])
        hbuf = sb("hbuf", [P, 2, FT, S])
        bc = sb("bc", [P, 4, 2, S])
        qT = sb("qT", [P, 2, S])
        kT = sb("kT", [P, 2, S])
        v = sb("v", [P, 2, ST, P])
        prob = sb("prob", [P, 2, ST, S])
        probT = sb("probT", [P, 2, ST, S])
        feats = sb("feats", [P, NPAIR, S])
        nmax = sb("nmax", [P, 2, ST])
        rsum = sb("rsum", [P, 2, ST])
        rinv = sb("rinv", [P, 2, ST])
        stats = sb("stats", [P, ST, 6])
        mv = sb("mv", [P, ST, 2])
        veps = sb("veps", [P, ST])
        rstd = sb("rstd", [P, ST])

        pp = [ctx.enter_context(nc.psum_tensor(f"p1_pp{i}", [P, 512], F32)) for i in range(2)]
        ps_s = [ctx.enter_context(nc.psum_tensor(f"p1_ps_s{i}", [P, 512], F32)) for i in range(2)]
        ps_t = [ctx.enter_context(nc.psum_tensor(f"p1_ps_t{i}", [P, 512], F32)) for i in range(2)]
        ps_o = [ctx.enter_context(nc.psum_tensor(f"p1_ps_o{i}", [P, 512], F32)) for i in range(2)]

        weights_in = sig("weights_in")
        a_ready = sig("a_ready")
        pads_ready = sig("pads_ready")
        x_in = sig("x_in", 32)
        xtok_in = sig("xtok_in", 16)
        pp_ready = sig("pp_ready", NPP, primed=True)
        pp_free = {"act": sig("pp_free_act", emptied["act"][-1], primed=True), "dve": sig("pp_free_dve", emptied["dve"][-1], primed=True)}
        conv_step = sig("conv_step", FT * KC, primed=True)
        u_ready = sig("u_ready", 1)
        bc_stored = sig("bc_stored", 16, primed=True)
        bc_in = [sig(f"bc_in{i}", 16 * NS // 4) for i in range(4)]
        sp_act = sig("sp_act", 3)
        sp_dve = sig("sp_dve", 8)
        y_begun = sig("y_begun", FT)
        decay_ready = sig("decay_ready", NS * FT)
        dbu_ready = sig("dbu_ready", NS)
        scanned = sig("scanned", NS * FT)
        hc_ready = sig("hc_ready", NS, primed=True)
        y_added = sig("y_added", NS, primed=True)
        scores_ready = sig("scores_ready", NH * ST)
        max_ready = sig("max_ready", NH * ST)
        exp_ready = sig("exp_ready", NH * ST, primed=True)
        rinv_ready = sig("rinv_ready", NH)
        normed = sig("normed", NH * ST)
        turned = sig("turned", NH * ST)
        probT_ready = sig("probT_ready", NH * ST, primed=True)
        pv_ready = sig("pv_ready", NPAIR)
        feats_ready = sig("feats_ready", NPAIR, primed=True)
        resid = sig("resid", 1)
        ln_step = sig("ln_step", 2 * (2 * ST + 1) + ST)
        rstd_ready = sig("rstd_ready", 2)
        x1_ready = sig("x1_ready", ST)
        gate_ready = sig("gate_ready", 1)
        g_ready = sig("g_ready", 1)
        x2_stored = sig("x2_stored", 16, primed=True)

        stats_seen = ctx.enter_context(nc.semaphore("stats_seen"))
        block = ctx.enter_context(nc.Block())

        col_names = ("bq", "bk", "conv_b", "dt_b", "Dskip")

        def settled(engine):
            engine.wait_ge(pads_ready.sem, 2)

        @block.sync
        def _(sp):
            bc_stored.prime(sp)
            def const(dst, src):
                weights_in.inc(sp.dma_start(dst, src), 16)

            def rows(name):
                return io[name].rearrange("(t p) n -> p t n", p=P)

            const(w_in[:], rows("in_wT"))
            const(conv_w[:], rows("conv_w"))
            for c, name in enumerate(col_names):
                const(cols[:, c, :], io[name])
            const(w_xp[:], rows("x_wT"))
            const(w_dt[:], io["dt_wT"])
            const(a_log[:], rows("A_log"))
            const(wq[:], rows("Wq"))
            const(wk[:], rows("Wk"))
            const(wv[:], rows("Wv"))
            const(wo[:], rows("Wo"))
            const(bv_row[:], io["bv"].to_broadcast([P, F]))
            const(bo_row[:], io["bo"].to_broadcast([P, F]))
            const(ident[:], io["ident"])
            with sp.Fori(0, B) as b:
                pp_ready.wait(sp, b, 0)
                settled(sp)
                x_in.inc(sp.dma_start(ctxT[:], io["ctxT"][bass.ds(b, 1)].rearrange("o (t p) s -> p (o t) s", p=P)), 16)
                x_in.inc(sp.dma_start(xT[:], io["xT"][bass.ds(b, 1)].rearrange("o (t p) s -> p (o t) s", p=P)), 16)
                x2_stored.wait(sp, b, 0)
                settled(sp)
                xtok_in.inc(sp.dma_start(xtok[:], io["x"][bass.ds(b, 1)].rearrange("o (t p) f -> p (o t) f", p=P)), 16)
                pp_free["act"].wait(sp, b, emptied["act"][PPU["xp", 0] + 1])
                bc_stored.inc(sp.dma_start(bc_dram, xdbl[R:XD, :]), 16)
                bc_stored.wait(sp, b, 16)
                for n in range(NS):
                    hc_ready.wait(sp, b, max(n - 3, 0))
                    src = bc_dram.rearrange("(o c n) s -> n o c s", o=1, c=2)[n].to_broadcast([P, 2, S])
                    bc_in[n % 4].inc(sp.dma_start(bc[:, n % 4], src), 16)
            for s in (x_in, xtok_in, bc_stored, *bc_in):
                s.close()

        def pp_take(pe, b, key):
            k = PPU[key]
            if k < 2:
                for who in ("act", "dve"):
                    pp_free[who].wait(pe, b, 0)
            else:
                who = uses[k - 2][2]
                pp_free[who].wait(pe, b, emptied[who][k - 1])
            return pp[k % 2]

        @block.tensor
        def _(pe):
            pp_ready.prime(pe)
            pe.wait_ge(weights_in.sem, weights_in.n)
            with pe.Fori(0, B) as b:
                def gives(ins):
                    pp_ready.inc(ins)

                x_in.wait(pe, b, 32)
                for e in range(FT):
                    bank = pp_take(pe, b, ("in", e))
                    for k in range(MT):
                        mm = pe.matmul(bank[:, :], w_in[:, k, e * P:(e + 1) * P], ctxT[:, k, :],
                                       start=(k == 0), stop=(k == MT - 1))
                    gives(mm)
                bank = pp_take(pe, b, ("xp", 0))
                u_ready.wait(pe, b, 1)
                for k in range(FT):
                    mm = pe.matmul(bank[0:XD, :], w_xp[:, k, :], u[:, k, :], start=(k == 0), stop=(k == FT - 1))
                gives(mm)
                for e in range(FT):
                    bank = pp_take(pe, b, ("dt", e))
                    if e == 0:
                        pp_free["act"].wait(pe, b, emptied["act"][PPU["xp", 0] + 1])
                    gives(pe.matmul(bank[:, :], w_dt[:, e * P:(e + 1) * P], xdbl[0:R, :], start=True, stop=True))

                def project(p):
                    for what, w in (("q", wq), ("k", wk)):
                        bank = pp_take(pe, b, (what, p))
                        for k in range(FT):
                            mm = pe.matmul(bank[:, :], w[:, k, p * P:(p + 1) * P], xT[:, k, :],
                                           start=(k == 0), stop=(k == FT - 1))
                        gives(mm)
                    bank = pp_take(pe, b, ("v", p))
                    for t in range(ST):
                        for k in range(FT):
                            mm = pe.matmul(bank[:, t * P:(t + 1) * P], xT[:, k, t * P:(t + 1) * P],
                                           wv[:, k, p * P:(p + 1) * P], start=(k == 0), stop=(k == FT - 1))
                    gives(mm)

                def score(h, i):
                    p, r = h // 2, (h % 2) * HD
                    n = ST * h + i
                    exp_ready.wait(pe, b, max(n - 1, 0))
                    if i == 0:
                        pp_free["act"].wait(pe, b, emptied["act"][PPU["k", p] + 1])
                    scores_ready.inc(pe.matmul(ps_s[n % 2][:, :], qT[r:r + HD, p % 2, i * P:(i + 1) * P],
                                               kT[r:r + HD, p % 2, :], start=True, stop=True))

                def turn(h, j):
                    n = ST * h + j
                    probT_ready.wait(pe, b, max(n - 1, 0))
                    normed.wait(pe, b, ST * (h + 1))
                    for i in range(ST):
                        mm = pe.transpose(ps_t[n % 2][:, i * P:(i + 1) * P], prob[:, h % 2, i, j * P:(j + 1) * P], ident[:, :])
                    turned.inc(mm)

                def weigh(p):
                    feats_ready.wait(pe, b, max(p - 1, 0))
                    probT_ready.wait(pe, b, ST * (2 * p + 2))
                    pp_free["dve"].wait(pe, b, emptied["dve"][PPU["v", p] + 1])
                    for j in range(ST):
                        for hh in range(2):
                            mm = pe.matmul(ps_o[p % 2][hh * HD:(hh + 1) * HD, :], v[:, p % 2, j, hh * HD:(hh + 1) * HD],
                                           probT[:, hh, j, :], start=(j == 0), stop=(j == ST - 1))
                    pv_ready.inc(mm)

                project(0)
                for h in range(NH + 1):
                    for i in range(ST):
                        if h < NH:
                            score(h, i)
                        if h >= 1:
                            turn(h - 1, i)
                    if h % 2 == 0 and h >= 2:
                        weigh(h // 2 - 1)
                    if h % 2 == 1 and h // 2 + 1 < NPAIR:
                        project(h // 2 + 1)
                feats_ready.wait(pe, b, NPAIR)
                for i in range(ST):
                    bank = pp_take(pe, b, ("wo", i))
                    for p in range(NPAIR):
                        mm = pe.matmul(bank[:, :], feats[:, p, i * P:(i + 1) * P], wo[:, p, :],
                                       start=(p == 0), stop=(p == NPAIR - 1))
                    gives(mm)
                for i in range(ST):
                    bank = pp_take(pe, b, ("gT", i))
                    g_ready.wait(pe, b, 1)
                    for e in range(FT):
                        mm = pe.transpose(bank[:, e * P:(e + 1) * P], yacc[:, e, i * P:(i + 1) * P], ident[:, :])
                    gives(mm)
            for s in (pp_ready, scores_ready, turned, pv_ready):
                s.close()

        @block.scalar
        def _(act):
            x2_stored.prime(act)
            exp_ready.prime(act)
            probT_ready.prime(act)
            feats_ready.prime(act)
            pp_free["act"].prime(act)
            act.wait_ge(weights_in.sem, weights_in.n)
            a_ready.inc(act.activation(a_neg[:], a_log[:], ACT.Exp))
            a_ready.inc(act.mul(cols[:, 5, :], cols[:, 0, :], QSCALE))
            act.wait_ge(a_ready.sem, 1)
            a_ready.inc(act.mul(a_neg[:], a_neg[:], -1.0))
            act.wait_ge(a_ready.sem, 3)
            with act.Fori(0, B) as b:
                def empties(what, k, dst, src, **kw):
                    pp_ready.wait(act, b, PPU[what, k] + 1)
                    pp_free["act"].inc(act.activation(dst, src, **kw))

                conv_step.wait(act, b, 0)
                for e in range(FT):
                    n = PPU["in", e]
                    empties("in", e, xin[:, e, KC - 1:], pp[n % 2][:, :], func=ACT.Copy)
                conv_step.wait(act, b, FT * KC)
                u_ready.inc(act.activation(u[:], decay[:, 0], ACT.Silu))
                bc_stored.wait(act, b, 0)
                empties("xp", 0, xdbl[:, :], pp[PPU["xp", 0] % 2][0:XD, :], func=ACT.Copy)
                mag, low = decay[:, 0], decay[:, 1]
                pp_free["dve"].wait(act, b, emptied["dve"][PPU["dt", FT - 1] + 1])
                sp_act.inc(act.activation(mag, dt[:], ACT.Abs))
                sp_act.wait(act, b, 1)
                sp_act.inc(act.activation(mag, mag, ACT.Exp, scale=-1.0))
                sp_act.wait(act, b, 2)
                sp_act.inc(act.activation(low, mag, ACT.Ln, bias=1.0))

                def empty_qk(p):
                    if p >= 2:
                        scores_ready.wait(act, b, ST * 2 * (p - 1))
                    empties("q", p, qT[:, p % 2, :], pp[PPU["q", p] % 2][:, :], func=ACT.Identity,
                            bias=cols[:, 5, p:p + 1], scale=QSCALE)
                    empties("k", p, kT[:, p % 2, :], pp[PPU["k", p] % 2][:, :], func=ACT.Identity,
                            bias=cols[:, 1, p:p + 1])

                def exp_scores(h, i):
                    n = ST * h + i
                    max_ready.wait(act, b, n + 1)
                    if h >= 2:
                        turned.wait(act, b, ST * (h - 1))
                    exp_ready.inc(act.activation(prob[:, h % 2, i, :], ps_s[n % 2][:, :], ACT.Exp,
                                                 bias=nmax[:, h % 2, i:i + 1], accum_out=rsum[:, h % 2, i:i + 1]))

                def copy_turned(h, j):
                    n = ST * h + j
                    turned.wait(act, b, n + 1)
                    if h >= 2 and j == 0:
                        pv_ready.wait(act, b, h // 2)
                    probT_ready.inc(act.activation(probT[:, h % 2, j, :], ps_t[n % 2][:, :], ACT.Copy))

                def exp_decay(n, e):
                    if n >= 2 and e == 0:
                        scanned.wait(act, b, FT * (n - 1))
                    decay_ready.inc(act.activation(decay[:, n % 2, e, :], dt[:, e, :], ACT.Exp,
                                                   scale=a_neg[:, e, n:n + 1]))

                def copy_feats(p):
                    pv_ready.wait(act, b, p + 1)
                    feats_ready.inc(act.activation(feats[:, p, :], ps_o[p % 2][:, :], ACT.Copy))

                empty_qk(0)
                sp_dve.wait(act, b, 7)
                def decays(slot):
                    for e in (2 * (slot % 2), 2 * (slot % 2) + 1):
                        exp_decay(slot // 2, e)

                decays(0)
                for h in range(NH + 1):
                    for i in range(ST):
                        if h < NH:
                            exp_scores(h, i)
                        if ST * h + i + 1 < 2 * NS:
                            decays(ST * h + i + 1)
                        if h >= 1:
                            copy_turned(h - 1, i)
                    if h % 2 == 0 and h >= 2:
                        copy_feats(h // 2 - 1)
                    if h % 2 == 1 and h // 2 + 1 < NPAIR:
                        empty_qk(h // 2 + 1)
                x1_ready.wait(act, b, ST)
                scanned.wait(act, b, NS * FT)
                gate_ready.inc(act.activation(decay[:, 0], xtok[:], ACT.Silu))
                ln_step.wait(act, b, ln_step.per)
                settled(act)
                x2_stored.inc(act.dma_start(x2_dram[bass.ds(b, 1)].rearrange("o (t p) f -> p (o t) f", p=P), xtok[:]), 16)
            x2_stored.wait_all(act, 16 * B)
            for s in (pp_free["act"], u_ready, sp_act, exp_ready, probT_ready, decay_ready, feats_ready, gate_ready, x2_stored):
                s.close()

        @block.vector
        def _(dve):
            conv_step.prime(dve)
            y_added.prime(dve)
            pp_free["dve"].prime(dve)
            dve.wait_ge(weights_in.sem, weights_in.n)
            dve.wait_ge(pads_ready.sem, 2)
            with dve.Fori(0, B) as b:
                for e in range(FT):
                    pp_free["act"].wait(dve, b, emptied["act"][PPU["in", e] + 1])
                    out = decay[:, 0, e, :]
                    conv_step.inc(dve.tensor_scalar(out, xin[:, e, 0:S], conv_w[:, e, 0:1], cols[:, 2, e:e + 1], ALU.mult, ALU.add))
                for k in range(1, KC):
                    for e in range(FT):
                        out = decay[:, 0, e, :]
                        conv_step.wait(dve, b, FT * (k - 1) + e + 1)
                        conv_step.inc(dve.scalar_tensor_tensor(out, xin[:, e, k:k + S], conv_w[:, e, k:k + 1], out, ALU.mult, ALU.add))
                u_ready.wait(dve, b, 1)
                for e in range(FT):
                    y_begun.inc(dve.tensor_scalar(yacc[:, e, :], u[:, e, :], cols[:, 4, e:e + 1], None, ALU.mult))
                for e in range(FT):
                    n = PPU["dt", e]
                    pp_ready.wait(dve, b, n + 1)
                    pp_free["dve"].inc(dve.tensor_scalar(dt[:, e, :], pp[n % 2][:, :], cols[:, 3, e:e + 1], None, ALU.add))
                mag, low, poly, part = decay[:, 0], decay[:, 1], hbuf[:, 0], hbuf[:, 1]

                def step(instruction):
                    sp_dve.inc(instruction)
                    sp_dve.wait_last(dve, b)

                sp_act.wait(dve, b, 2)
                step(dve.tensor_scalar(poly, mag, 1.0 / 3.0, -0.5, ALU.mult, ALU.add))
                step(dve.tensor_tensor(poly, poly, mag, ALU.mult))
                step(dve.scalar_tensor_tensor(poly, poly, 1.0, mag, ALU.add, ALU.mult))
                step(dve.scalar_tensor_tensor(part, mag, SMALL, poly, ALU.is_lt, ALU.mult))
                sp_act.wait(dve, b, 3)
                step(dve.scalar_tensor_tensor(low, mag, SMALL, low, ALU.is_ge, ALU.mult))
                step(dve.tensor_tensor(low, low, part, ALU.add))
                step(dve.scalar_tensor_tensor(dt[:], dt[:], 0.0, low, ALU.max, ALU.add))
                sp_dve.inc(dve.tensor_tensor(dtu[:], dt[:], u[:], ALU.mult))

                def empty_v(p):
                    n = PPU["v", p]
                    pp_ready.wait(dve, b, n + 1)
                    if p >= 2:
                        pv_ready.wait(dve, b, p - 1)
                    pp_free["dve"].inc(dve.tensor_tensor(
                        v[:, p % 2], pp[n % 2][:, :].rearrange("p (t c) -> p t c", t=ST),
                        bv_row[:, p * P:(p + 1) * P].rearrange("p (o c) -> p o c", o=1).to_broadcast([P, ST, P]), ALU.add))

                def row_max(h, i):
                    n = ST * h + i
                    scores_ready.wait(dve, b, n + 1)
                    max_ready.inc(dve.tensor_reduce(nmax[:, h % 2, i:i + 1], ps_s[n % 2][:, :], AX.X, ALU.max, negate=True))

                def norm_inverse(h):
                    exp_ready.wait(dve, b, ST * (h + 1))
                    rinv_ready.inc(dve.reciprocal(rinv[:, h % 2, :], rsum[:, h % 2, :]))

                def normalise(h):
                    rinv_ready.wait(dve, b, h + 1)
                    for i in range(ST):
                        normed.inc(dve.tensor_scalar(prob[:, h % 2, i, :], prob[:, h % 2, i, :], rinv[:, h % 2, i:i + 1], None, ALU.mult))

                def make_dbu(n):
                    bc_in[n % 4].wait(dve, b, 16 * (n // 4 + 1))
                    y_added.wait(dve, b, max(n - 1, 0))
                    if n == 0:
                        sp_dve.wait(dve, b, 8)
                    dbu_ready.inc(dve.tensor_tensor(hbuf[:, n % 2], dtu[:], bc[:, n % 4, 0:1, :].to_broadcast([P, FT, S]), ALU.mult))

                def scan(n, e):
                    decay_ready.wait(dve, b, FT * n + e + 1)
                    if e == 0:
                        dbu_ready.wait(dve, b, n + 1)
                    scanned.inc(dve.tensor_tensor_scan(hbuf[:, n % 2, e, :], decay[:, n % 2, e, :], hbuf[:, n % 2, e, :],
                                                       0.0, ALU.mult, ALU.add))

                def add_y(n):
                    hc_ready.wait(dve, b, n + 1)
                    if n:
                        y_added.wait(dve, b, n)
                    else:
                        y_begun.wait(dve, b, FT)
                    y_added.inc(dve.tensor_tensor(yacc[:], yacc[:], hbuf[:, n % 2], ALU.add))

                empty_v(0)
                for h in range(NH + 1):
                    if h >= 1:
                        norm_inverse(h - 1)
                    for i in range(ST):
                        if h < NH:
                            row_max(h, i)
                        if h >= 1 and i == 0:
                            normalise(h - 1)
                        if h < NH:
                            n = 2 * h + i // 2
                            if i % 2 == 0:
                                make_dbu(n)
                                scan(n, 0)
                                scan(n, 1)
                            else:
                                scan(n, 2)
                                scan(n, 3)
                                if n >= 1:
                                    add_y(n - 1)
                    if h % 2 == 1 and h // 2 + 1 < NPAIR:
                        empty_v(h // 2 + 1)
                add_y(NS - 1)

                def layer_norm(turn):
                    base = turn * (2 * ST + 1)
                    for i in range(ST):
                        (resid if turn == 0 else pp_free["dve"]).wait_last(dve, b)
                        ln_step.inc(dve.bn_stats(stats[:, i, :], xtok[:, i, :]))
                    ln_step.wait(dve, b, base + ST)
                    dve.sem_inc(stats_seen, 1)
                    for i in range(ST):
                        ln_step.inc(dve.bn_aggr(mv[:, i, :], stats[:, i, :]))
                    ln_step.wait(dve, b, base + 2 * ST)
                    ln_step.inc(dve.tensor_scalar(veps[:, :], mv[:, :, 1], 1e-5, None, ALU.add))
                    rstd_ready.wait(dve, b, turn + 1)
                    for i in range(ST):
                        who = x1_ready if turn == 0 else ln_step
                        who.inc(dve.tensor_scalar(xtok[:, i, :], xtok[:, i, :], mv[:, i, 0:1], rstd[:, i:i + 1], ALU.subtract, ALU.mult))

                xtok_in.wait(dve, b, 16)
                resid.inc(dve.tensor_tensor(xtok[:], xtok[:], bo_row[:, :].rearrange("p (o f) -> p o f", o=1).to_broadcast([P, ST, F]), ALU.add))
                resid.wait_last(dve, b)
                for i in range(ST):
                    n = PPU["wo", i]
                    pp_ready.wait(dve, b, n + 1)
                    pp_free["dve"].inc(dve.tensor_tensor(xtok[:, i, :], xtok[:, i, :], pp[n % 2][:, :], ALU.add))
                pp_free["dve"].wait_last(dve, b)
                layer_norm(0)
                gate_ready.wait(dve, b, 1)
                y_added.wait(dve, b, NS)
                g_ready.inc(dve.tensor_tensor(yacc[:], yacc[:], decay[:, 0], ALU.mult))
                for i in range(ST):
                    n = PPU["gT", i]
                    pp_ready.wait(dve, b, n + 1)
                    pp_free["dve"].inc(dve.tensor_tensor(xtok[:, i, :], xtok[:, i, :], pp[n % 2][:, :], ALU.add))
                layer_norm(1)
            for s in (pp_free["dve"], conv_step, sp_dve, y_begun, max_ready, rinv_ready, normed, dbu_ready, scanned, y_added, resid, x1_ready, g_ready, ln_step):
                s.close()

        @block.gpsimd
        def _(pool):
            hc_ready.prime(pool)
            pads_ready.inc(pool.memset(mhalf[:], -0.5))
            pads_ready.inc(pool.memset(xin[:, :, 0:KC - 1], 0.0))
            pool.wait_ge(pads_ready.sem, 2)
            with pool.Fori(0, B) as b:
                for n in range(NS):
                    scanned.wait(pool, b, FT * (n + 1))
                    hc_ready.inc(pool.tensor_tensor(hbuf[:, n % 2], hbuf[:, n % 2], bc[:, n % 4, 1:2, :].to_broadcast([P, FT, S]), ALU.mult))
                for turn in range(2):
                    base = turn * (2 * ST + 1)
                    ln_step.wait(pool, b, base + 2 * ST + 1)
                    rstd_ready.inc(pool.tensor_tensor(rstd[:, :], veps[:, :], mhalf[:, 0:ST], ALU.pow))
            hc_ready.close(); rstd_ready.close()


def grouped_attention(nc, io, x2_dram, hidden_dram):
    B, S, F = io["x"].shape
    HD = P
    HQ = io["q_wT"].shape[1] // HD
    HK = io["k_wT"].shape[1] // HD
    QH = HQ // HK
    FT, ST = F // P, S // P
    EPS = 1e-6
    assert HK * HD == F and QH == ST == 4

    uses = [("hT", k, "act") for k in range(FT)]
    uses += [("k", i, "dve") for i in range(ST)] + [("v", i, "act") for i in range(ST)]
    uses += [("kT", k, "act") for k in range(HK)]
    uses += [("q", (0, i), "dve") for i in range(ST)] + [("qT", (0, h), "act") for h in range(QH)]

    slots = {}
    for kv in range(HK):
        for i in range(ST):
            if kv + 1 < HK:
                slots[QH * kv + 2 * (i // 2), 1 + 2 * (i % 2)] = ("q", (kv + 1, i), "dve")
                slots[QH * kv + 3, i] = ("qT", (kv + 1, i), "act")
            slots[QH * (kv + 1) + 1 if kv + 1 < HK else HQ, i] = ("o", (kv, i), "dve")
    uses += [slots[at] for at in sorted(slots)]
    PPU = {(what, k): n for n, (what, k, _) in enumerate(uses)}
    NPP = len(uses)
    emptied = {"act": [0], "dve": [0]}
    for _, _, who in uses:
        for w in emptied:
            emptied[w].append(emptied[w][-1] + (w == who))

    with ExitStack() as ctx:
        def sb(name, shape, dt=F32):
            return ctx.enter_context(nc.sbuf_tensor("p2_" + name, shape, dt))

        def sig(name, per=0, primed=False):
            return Signal(ctx.enter_context(nc.semaphore("p2_" + name)), per, primed)

        BF = mybir.dt.bfloat16
        q_w = sb("q_w", [P, FT, HQ * HD])
        k_w = sb("k_w", [P, FT, HK * HD])
        v_w = sb("v_w", [P, FT, HK * HD])
        o_w = sb("o_w", [P, HQ, F])
        norm_col = sb("norm_col", [P, FT])
        qn_row = sb("qn_row", [P, HD])
        kn_row = sb("kn_row", [P, HD])
        same = {c: sb(f"same_{c}", [P, ST, HD]) for c in "qk"}
        other = {c: sb(f"other_{c}", [P, ST, HD]) for c in "qk"}
        ident = sb("ident2", [P, P])
        ident_b = sb("ident_b", [P, P], BF)
        mask_b = sb("mask_b", [P, P], BF)
        mhalf = sb("mhalf2", [P, ST * QH])
        hid = sb("hid", [P, ST, F])
        hn = sb("hn", [P, ST, F])
        cosf = hn[:, :, 0:HD]
        sinf = hn[:, :, HD:2 * HD]
        mask = hn[:, 0, 2 * HD:3 * HD]
        hT = sb("hT", [P, FT, S])
        v = sb("v2", [P, ST, HK * HD])
        kT = sb("kT2", [P, HK, S])
        square = sb("square", [P, 2, QH, HD])
        part = sb("part", [P, 2, QH, HD])
        cross = sb("cross", [P, 2, QH, HD])
        roped = sb("roped", [P, ST, QH, HD])
        qT = sb("qT2", [P, 2, QH, S])
        prob = sb("prob2", [P, 2, ST, S])
        probT = sb("probT2", [P, ST, S])
        aT = sb("aT", [P, 8, S])
        ss = sb("ss", [P, ST])
        ssv = sb("ssv", [P, ST])
        hr = sb("hr", [P, ST])
        hsum = sb("hsum", [P, 2, ST, QH])
        heps = sb("heps", [P, 2, ST, QH])
        hinv = sb("hinv", [P, 2, ST, QH])
        nmax = sb("nmax2", [P, 2, ST])
        nbias = sb("nbias", [P, 2, ST])
        rsum = sb("rsum2", [P, 2, ST])
        rinv = sb("rinv2", [P, 2, ST])

        pp = [ctx.enter_context(nc.psum_tensor(f"p2_pp{i}", [P, 512], F32)) for i in range(2)]
        ps_s = [ctx.enter_context(nc.psum_tensor(f"p2_ps_s{i}", [P, 512], F32)) for i in range(3)]
        ps_t = [ctx.enter_context(nc.psum_tensor(f"p2_ps_t{i}", [P, 512], F32)) for i in range(2)]
        ps_o = [ctx.enter_context(nc.psum_tensor(f"p2_ps_o{i}", [P, 512], F32)) for i in range(1)]

        NG = HK + 1
        weights_in = sig("weights_in2")
        consts_ready = sig("consts_ready2")
        tables_ready = sig("tables_ready")
        x2_in = sig("x2_in", 16)
        squared = sig("squared", ST)
        eps_added = sig("eps_added", 1)
        hr_ready = sig("hr_ready", 1)
        hn_ready = sig("hn_ready", ST)
        pp_ready = sig("pp_ready2", NPP)
        pp_free = {"act": sig("pp_free_act2", emptied["act"][-1], primed=True), "dve": sig("pp_free_dve2", emptied["dve"][-1], primed=True)}
        sq_ready = sig("sq_ready", ST * NG)
        sum_ready = sig("sum_ready", ST * NG, primed=True)
        part_ready = sig("part_ready", 2 * ST * NG)
        hsum_ready = sig("hsum_ready", NG)
        hinv_ready = sig("hinv_ready", NG)
        roped_ready = sig("roped_ready", ST * NG, primed=True)
        k_normed = sig("k_normed", ST)
        scores_ready = sig("scores_ready2", HQ * ST)
        max_ready = sig("max_ready2", HQ * ST)
        nbias_ready = sig("nbias_ready", HQ * ST)
        exp_ready = sig("exp_ready2", HQ * ST, primed=True)
        rinv_ready = sig("rinv_ready2", HQ)
        normed = sig("normed2", HQ * ST)
        turned = sig("turned2", HQ * ST)
        probT_ready = sig("probT_ready2", HQ * ST, primed=True)
        pv_ready = sig("pv_ready2", HQ, primed=True)
        aT_ready = sig("aT_ready", HQ, primed=True)
        hidden_stored = sig("hidden_stored", 16, primed=True)

        def settled(engine):
            engine.wait_ge(consts_ready.sem, 1)

        block = ctx.enter_context(nc.Block())

        @block.sync
        def _(sp):
            hidden_stored.prime(sp)
            def const(dst, src):
                weights_in.inc(sp.dma_start(dst, src), 16)

            def rows(name):
                return io[name].rearrange("(t p) n -> p t n", p=P)

            const(norm_col[:], io["attn_norm"])
            const(k_w[:], rows("k_wT"))
            const(v_w[:], rows("v_wT"))
            const(q_w[:], rows("q_wT"))
            const(o_w[:], rows("o_wT"))
            const(cosf, rows("cos"))
            const(sinf, rows("sin"))
            const(qn_row[:], io["q_norm"].to_broadcast([P, HD]))
            const(kn_row[:], io["k_norm"].to_broadcast([P, HD]))
            const(ident[:], io["ident"])
            const(mask, io["mask"])
            with sp.Fori(0, B) as b:
                hidden_stored.wait(sp, b, 0)
                settled(sp)
                x2_in.inc(sp.dma_start(hid[:], x2_dram[bass.ds(b, 1)].rearrange("o (t p) f -> p (o t) f", p=P)), 16)
                pp_free["dve"].wait(sp, b, pp_free["dve"].per)
                settled(sp)
                hidden_stored.inc(sp.dma_start(hidden_dram[bass.ds(b, 1)].rearrange("o (t p) f -> p (o t) f", p=P), hid[:]), 16)
            hidden_stored.wait_all(sp, 16 * B)
            for s in (x2_in, hidden_stored):
                s.close()

        def pp_take(pe, b, key):
            k = PPU[key]
            if k < 2:
                for who in ("act", "dve"):
                    pp_free[who].wait(pe, b, 0)
            else:
                who = uses[k - 2][2]
                pp_free[who].wait(pe, b, emptied[who][k - 1])
            return pp[k % 2]

        @block.tensor
        def _(pe):
            pv_ready.prime(pe)
            pe.wait_ge(weights_in.sem, weights_in.n)
            with pe.Fori(0, B) as b:
                hn_ready.wait(pe, b, ST)
                for k in range(FT):
                    bank = pp_take(pe, b, ("hT", k))
                    for i in range(ST):
                        mm = pe.transpose(bank[:, i * P:(i + 1) * P], hn[:, i, k * P:(k + 1) * P], ident[:, :])
                    pp_ready.inc(mm)

                def project(key, i, w, c0):
                    bank = pp_take(pe, b, key)
                    pp_free["act"].wait(pe, b, emptied["act"][PPU["hT", FT - 1] + 1])
                    for k in range(FT):
                        mm = pe.matmul(bank[:, :], hT[:, k, i * P:(i + 1) * P], w[:, k, c0:c0 + 512],
                                       start=(k == 0), stop=(k == FT - 1))
                    pp_ready.inc(mm)

                def turn_roped(key, h):
                    bank = pp_take(pe, b, key)
                    for i in range(ST):
                        mm = pe.transpose(bank[:, i * P:(i + 1) * P], roped[:, i, h, :], ident[:, :])
                    pp_ready.inc(mm)

                for i in range(ST):
                    project(("k", i), i, k_w, 0)
                for i in range(ST):
                    project(("v", i), i, v_w, 0)
                k_normed.wait(pe, b, ST)
                for h in range(HK):
                    turn_roped(("kT", h), h)
                for i in range(ST):
                    project(("q", (0, i)), i, q_w, 0)
                roped_ready.wait(pe, b, 2 * ST)
                for h in range(QH):
                    turn_roped(("qT", (0, h)), h)

                def score(g, i):
                    kv, hh = divmod(g, QH)
                    n = ST * g + i
                    exp_ready.wait(pe, b, max(n - 2, 0))
                    if i == 0:
                        pp_free["act"].wait(pe, b, emptied["act"][PPU["qT", (kv, hh)] + 1])
                    bank = ps_s[n % 3]
                    pe.matmul(bank[:, 0:(i + 1) * P], qT[:, kv % 2, hh, i * P:(i + 1) * P], kT[:, kv, 0:(i + 1) * P],
                              start=True, stop=False)
                    scores_ready.inc(pe.matmul(bank[:, i * P:(i + 1) * P], ident_b[:, :], mask_b[:, :], start=False, stop=True))

                def turn(g, j):
                    n = ST * g + j
                    probT_ready.wait(pe, b, max(n - 1, 0))
                    normed.wait(pe, b, ST * (g + 1))
                    for i in range(j, ST):
                        mm = pe.transpose(ps_t[n % 2][:, i * P:(i + 1) * P], prob[:, g % 2, i, j * P:(j + 1) * P], ident[:, :])
                    turned.inc(mm)

                def weigh(g, j):
                    kv = g // QH
                    if j == 0:
                        aT_ready.wait(pe, b, g)
                    probT_ready.wait(pe, b, ST * g + j + 1)
                    mm = pe.matmul(ps_o[0][:, j * P:], v[:, j, kv * HD:(kv + 1) * HD], probT[:, j, j * P:],
                                   start=(j == 0), stop=(j == ST - 1))
                    if j == ST - 1:
                        pv_ready.inc(mm)

                def task(what, key):
                    kv, i = key
                    if what == "o":
                        aT_ready.wait(pe, b, QH * (kv + 1))
                        bank = pp_take(pe, b, (what, key))
                        for hh in range(QH):
                            h = QH * kv + hh
                            mm = pe.matmul(bank[:, :], aT[:, h % 8, i * P:(i + 1) * P], o_w[:, h, :],
                                           start=(hh == 0), stop=(hh == QH - 1))
                        pp_ready.inc(mm)
                    elif what == "q":
                        project((what, key), i, q_w, 512 * kv)
                    else:
                        roped_ready.wait(pe, b, ST * (kv + 2))
                        turn_roped((what, key), i)

                for g in range(HQ + 1):
                    for i in range(ST):
                        if g < HQ:
                            score(g, i)
                        if g >= 1:
                            turn(g - 1, i)
                            if i:
                                weigh(g - 1, i - 1)
                        if (g, i) in slots and g < HQ:
                            task(*slots[g, i][:2])
                    if g >= 1:
                        weigh(g - 1, ST - 1)
                for i in range(ST):
                    task(*slots[HQ, i][:2])
            for s in (pp_ready, scores_ready, turned, pv_ready):
                s.close()

        @block.scalar
        def _(act):
            exp_ready.prime(act)
            probT_ready.prime(act)
            aT_ready.prime(act)
            pp_free["act"].prime(act)
            act.wait_ge(weights_in.sem, weights_in.n)
            with act.Fori(0, B) as b:
                x2_in.wait(act, b, 16)
                for i in range(ST):
                    squared.inc(act.activation(square[:, i % 2].rearrange("p h d -> p (h d)"), hid[:, i, :], ACT.Square,
                                               accum_out=ss[:, i:i + 1]))
                    if i in (1, 2):
                        squared.wait(act, b, i)

                def empties(key, dst, **kw):
                    n = PPU[key]
                    pp_ready.wait(act, b, n + 1)
                    pp_free["act"].inc(act.activation(dst, pp[n % 2][:, :], **kw))

                for k in range(FT):
                    empties(("hT", k), hT[:, k, :], func=ACT.Copy, scale=norm_col[:, k:k + 1])

                def square_heads(key, group, i):
                    m = ST * group + i
                    n = PPU[key]
                    pp_ready.wait(act, b, n + 1)
                    sum_ready.wait(act, b, max(m - 1, 0))
                    sq_ready.inc(act.activation(square[:, m % 2].rearrange("p h d -> p (h d)"), pp[n % 2][:, :], ACT.Square))

                squared.wait(act, b, ST)
                for i in range(ST):
                    square_heads(("k", i), 0, i)
                for i in range(ST):
                    empties(("v", i), v[:, i, :], func=ACT.Copy)
                for h in range(HK):
                    empties(("kT", h), kT[:, h, :], func=ACT.Copy)
                for i in range(ST):
                    square_heads(("q", (0, i)), 1, i)
                for h in range(QH):
                    empties(("qT", (0, h)), qT[:, 0, h, :], func=ACT.Copy)

                def exp_scores(g, i):
                    n = ST * g + i
                    kv, hh = divmod(g, QH)
                    nbias_ready.wait(act, b, n + 1)
                    exp_ready.inc(act.activation(prob[:, g % 2, i, 0:(i + 1) * P], ps_s[n % 3][:, 0:(i + 1) * P], ACT.Exp,
                                                 bias=nbias[:, g % 2, i:i + 1], scale=hinv[:, (kv + 1) % 2, i, hh:hh + 1],
                                                 accum_out=rsum[:, g % 2, i:i + 1]))

                def copy_turned(g, j):
                    n = ST * g + j
                    turned.wait(act, b, n + 1)
                    if j == 0:
                        pv_ready.wait(act, b, g)
                    probT_ready.inc(act.activation(probT[:, j, j * P:], ps_t[n % 2][:, j * P:], ACT.Copy))

                for g in range(HQ + 1):
                    for i in range(ST):
                        if g < HQ:
                            exp_scores(g, i)
                        if g >= 1:
                            copy_turned(g - 1, i)
                        what, key, _ = slots.get((g, i), ("", None, ""))
                        if what == "q":
                            square_heads((what, key), key[0] + 1, key[1])
                        elif what == "qT":
                            empties((what, key), qT[:, key[0] % 2, key[1], :], func=ACT.Copy)
                    if g >= 1:
                        pv_ready.wait(act, b, g)
                        aT_ready.inc(act.activation(aT[:, (g - 1) % 8, :], ps_o[0][:, :], ACT.Copy))
            for s in (pp_free["act"], squared, sq_ready, exp_ready, probT_ready, aT_ready):
                s.close()

        @block.vector
        def _(dve):
            sum_ready.prime(dve)
            pp_free["dve"].prime(dve)
            consts_ready.inc(dve.memset(mhalf[:], -0.5))
            dve.wait_ge(weights_in.sem, weights_in.n)
            H2 = HD // 2
            for c, row in (("q", qn_row), ("k", kn_row)):
                def weight(a, z):
                    return row[:, a:z].rearrange("p (o d) -> p o d", o=1).to_broadcast([P, ST, z - a])
                tables_ready.inc(dve.tensor_tensor(same[c][:], cosf, weight(0, HD), ALU.mult))
                tables_ready.inc(dve.tensor_tensor(other[c][:, :, 0:H2], sinf[:, :, 0:H2], weight(H2, HD), ALU.mult))
                tables_ready.inc(dve.tensor_tensor(other[c][:, :, H2:], sinf[:, :, H2:], weight(0, H2), ALU.mult))
            tables_ready.inc(dve.tensor_copy(ident_b[:, :], ident[:, :]))
            tables_ready.inc(dve.tensor_copy(mask_b[:, :], mask))
            dve.wait_ge(tables_ready.sem, tables_ready.n)
            with dve.Fori(0, B) as b:
                squared.wait(dve, b, ST)
                eps_added.inc(dve.tensor_scalar(ssv[:, :], ss[:, :], 1.0 / F, EPS, ALU.mult, ALU.add))
                hr_ready.wait(dve, b, 1)
                for i in range(ST):
                    hn_ready.inc(dve.tensor_scalar(hn[:, i, :], hid[:, i, :], hr[:, i:i + 1], None, ALU.mult))

                def rope(key, c, group, i):
                    m = ST * group + i
                    n = PPU[key]
                    bank = pp[n % 2][:, :].rearrange("p (h d) -> p h d", h=QH)

                    def table(t, a, z):
                        return t[c][:, i:i + 1, a:z].to_broadcast([P, QH, z - a])

                    sq_ready.wait(dve, b, m + 1)
                    roped_ready.wait(dve, b, max(m - 1, 0))
                    part_ready.inc(dve.tensor_tensor(cross[:, m % 2, :, 0:H2], bank[:, :, H2:], table(other, 0, H2), ALU.mult))
                    part_ready.inc(dve.tensor_tensor(cross[:, m % 2, :, H2:], bank[:, :, 0:H2], table(other, H2, HD), ALU.mult))
                    pp_free["dve"].inc(dve.tensor_tensor(part[:, m % 2], bank, table(same, 0, HD), ALU.mult))
                    sum_ready.inc(dve.tensor_reduce(hsum[:, group % 2, i, :], square[:, m % 2], AX.X, ALU.add))
                    if i == ST - 1:
                        sum_ready.wait_last(dve, b)
                        mul, add = (1.0 / HD, EPS) if c == "k" else (1.0, HD * EPS)
                        hsum_ready.inc(dve.tensor_scalar(heps[:, group % 2], hsum[:, group % 2], mul, add, ALU.mult, ALU.add))

                for i in range(ST):
                    rope(("k", i), "k", 0, i)
                hinv_ready.wait(dve, b, 1)
                for i in range(ST):
                    roped_ready.wait(dve, b, i + 1)
                    k_normed.inc(dve.tensor_tensor(
                        roped[:, i], roped[:, i],
                        hinv[:, 0, i, :].rearrange("p (h o) -> p h o", o=1).to_broadcast([P, QH, HD]), ALU.mult))
                for i in range(ST):
                    rope(("q", (0, i)), "q", 1, i)

                def row_max(g, i):
                    n = ST * g + i
                    kv, hh = divmod(g, QH)
                    scores_ready.wait(dve, b, n + 1)
                    max_ready.inc(dve.tensor_reduce(nmax[:, g % 2, i:i + 1], ps_s[n % 3][:, 0:(i + 1) * P], AX.X, ALU.max, negate=True))
                    if i == 0 and hh == 0:
                        hinv_ready.wait(dve, b, kv + 2)
                    max_ready.wait_last(dve, b)
                    nbias_ready.inc(dve.tensor_tensor(nbias[:, g % 2, i:i + 1], nmax[:, g % 2, i:i + 1],
                                                      hinv[:, (kv + 1) % 2, i, hh:hh + 1], ALU.mult))

                def normalise(g):
                    exp_ready.wait(dve, b, ST * (g + 1))
                    rinv_ready.inc(dve.reciprocal(rinv[:, g % 2, :], rsum[:, g % 2, :]))
                    rinv_ready.wait_last(dve, b)
                    for i in range(ST):
                        block_ = prob[:, g % 2, i, 0:(i + 1) * P]
                        normed.inc(dve.tensor_scalar(block_, block_, rinv[:, g % 2, i:i + 1], None, ALU.mult))

                def task(what, key):
                    if what == "o":
                        i = key[1]
                        n = PPU[what, key]
                        pp_ready.wait(dve, b, n + 1)
                        if key[0]:
                            pp_free["dve"].wait(dve, b, emptied["dve"][PPU[what, (key[0] - 1, i)] + 1])
                        pp_free["dve"].inc(dve.tensor_tensor(hid[:, i, :], hid[:, i, :], pp[n % 2][:, :], ALU.add))
                    elif what == "q":
                        rope((what, key), "q", key[0] + 1, key[1])

                for g in range(HQ + 1):
                    for i in range(ST):
                        if g < HQ:
                            row_max(g, i)
                            if i == ST - 1:
                                normalise(g)
                        if (g, i) in slots:
                            task(*slots[g, i][:2])
            for s in (pp_free["dve"], eps_added, hn_ready, part_ready, sum_ready, hsum_ready, k_normed, max_ready,
                      nbias_ready, rinv_ready, normed):
                s.close()

        @block.gpsimd
        def _(pool):
            roped_ready.prime(pool)
            pool.wait_ge(consts_ready.sem, 1)
            with pool.Fori(0, B) as b:
                eps_added.wait(pool, b, 1)
                hr_ready.inc(pool.tensor_tensor(hr[:, :], ssv[:, :], mhalf[:, 0:ST], ALU.pow))
                for group in range(NG):
                    for i in range(ST):
                        m = ST * group + i
                        pp_free["dve"].wait(pool, b, emptied["dve"][PPU[("k", i) if group == 0 else ("q", (group - 1, i))] + 1])
                        if group == 1:
                            pp_ready.wait(pool, b, PPU["kT", HK - 1] + 1)
                        elif group > 1:
                            pp_ready.wait(pool, b, PPU["qT", (group - 2, QH - 1)] + 1)
                        roped_ready.inc(pool.tensor_tensor(roped[:, i], part[:, m % 2], cross[:, m % 2], ALU.add))
                    hsum_ready.wait(pool, b, group + 1)
                    hinv_ready.inc(pool.tensor_tensor(hinv[:, group % 2].rearrange("p t h -> p (t h)"),
                                                      heps[:, group % 2].rearrange("p t h -> p (t h)"), mhalf[:, :], ALU.pow))
            for s in (hr_ready, roped_ready, hinv_ready):
                s.close()


def mixture_of_experts(nc, io, x2_dram, hidden_dram, out):
    B, S, F = io["x"].shape
    E = io["gate_wT"].shape[1]
    I = io["wgT"].shape[2]
    FT, ST = F // P, S // P
    NT = B * ST
    J = 2 * NT
    NP = -(-(J * P + E * (P - 1)) // P)
    NP += NP % 2
    IT = -(-I // P)
    IL = I - (IT - 1) * P
    EPS = 1e-6
    RING = 8
    U32 = mybir.dt.uint32
    assert E == 8 and I <= 512 and NP <= P

    hn_dram = nc.dram_tensor("hn_rows", (B * S, F), F32, kind="Internal").ap()
    y_dram = nc.dram_tensor("expert_rows", (NP * P, F), F32, kind="Internal").ap()

    with ExitStack() as ctx:
        def sb(name, shape, dt=F32):
            return ctx.enter_context(nc.sbuf_tensor("p3_" + name, shape, dt))

        def sig(name, per=0, primed=False):
            return Signal(ctx.enter_context(nc.semaphore("p3_" + name)), per, primed)

        gate_w = sb("gate_w", [P, FT, E])
        norm_col = sb("norm_col3", [P, FT])
        ident = sb("ident3", [P, P])
        before = sb("before", [P, P])
        ones = sb("ones", [P, P])
        expert_no = sb("expert_no", [P, E])
        place_no = sb("place_no", [P, P])
        token_no = sb("token_no", [P, J])
        new_expert = sb("new_expert", [P, E * J])
        mhalf = sb("mhalf3", [P, NT])
        wg = sb("wg_sb", [P, E * FT * I])
        wu = sb("wu_sb", [P, E * FT * I])
        wd = sb("wd_sb", [P, E * IT * F])
        hbuf = sb("hbuf3", [P, 2, ST, F])
        acc = sb("acc", [P, NT, F])
        hT = sb("hT3", [P, FT, S])
        ss = sb("ss3", [P, NT])
        ssv = sb("ssv3", [P, NT])
        hr = sb("hr3", [P, NT])
        logits = sb("logits", [P, NT, E])
        shifted = sb("shifted", [P, NT, E])
        top = sb("top", [P, NT, 8])
        topi = sb("topi", [P, NT, 8], U32)
        topf = sb("topf", [P, 2, NT])
        small = sb("small", [P, 8, NT])
        chosen = sb("chosen", [P, E, J])
        upto = sb("upto", [P, E, J])
        per_expert = sb("per_expert", [P, 4, E])
        begun = sb("begun", [P, E, NT])
        pos = sb("pos", [P, J])
        pos_u = sb("pos_u", [P, J], U32)
        pos_hi = sb("pos_hi", [P, J], U32)
        pos_lo = sb("pos_lo", [P, J], U32)
        tile_of = sb("tile_of", [P, J])
        row_of = sb("row_of", [P, J])
        ended = sb("ended", [1, NP, E])
        expert_f = sb("expert_f", [1, NP])
        expert_of = sb("expert_of", [1, NP], U32)
        token_of = sb("token_of", [P, NP], U32)
        rows_of = [sb(f"rows_of{i}", [P, 1], U32) for i in range(2)]
        square = sb("square3", [P, F])
        stats = sb("stats3", [P, ST, 6])
        mv = sb("mv3", [P, NT, 2])
        veps = sb("veps3", [P, NT])
        rstd = sb("rstd3", [P, NT])
        spare = {"hbuf": hbuf[:].rearrange("p a t f -> p (a t f)"), "hT": hT[:].rearrange("p k s -> p (k s)")}

        def carved(name, n, width):
            got, spare[name] = spare[name][:, 0:n * width], spare[name][:, n * width:]
            return got.rearrange("p (n w) -> p n w", w=width)

        row_hot = spare["hbuf"][:, 0:J * P].rearrange("p (j r) -> p j r", r=P)
        tile_hot = spare["hT"][:, 0:J * NP].rearrange("p (j t) -> p j t", t=NP)
        xg = carved("hbuf", 2, F)
        xT = carved("hbuf", 2, F)
        y_row = carved("hbuf", 2, F)
        silu = carved("hbuf", 2, I)
        act_row = carved("hT", 2, I)
        actT = carved("hT", 2, IT * P)
        results = hbuf[:].rearrange("p a t f -> p (a t) f")
        assert 2 * ST == RING and J * P <= 2 * ST * F and J * NP <= FT * S

        ps_g = [ctx.enter_context(nc.psum_tensor(f"p3_ps_g{i}", [P, 512], F32)) for i in range(2)]
        ps_u = [ctx.enter_context(nc.psum_tensor(f"p3_ps_u{i}", [P, 512], F32)) for i in range(2)]
        ps_x = ctx.enter_context(nc.psum_tensor("p3_ps_x", [P, 512], F32))
        ps_a = ctx.enter_context(nc.psum_tensor("p3_ps_a", [P, 512], F32))
        ps_d = [ctx.enter_context(nc.psum_tensor(f"p3_ps_d{i}", [P, 512], F32)) for i in range(2)]

        small_in = sig("small_in")
        weights_in = sig("weights_in3")
        hidden_in = [sig(f"hidden_in{i}") for i in range(2)]
        acc_in = [sig(f"acc_in{c}") for c in range(B)]
        hn_stored = [sig(f"hn_stored{i}") for i in range(2)]
        consts_ready = sig("consts_ready3")
        squared = sig("squared3")
        eps_added = sig("eps_added3")
        hr_ready = sig("hr_ready3")
        acc_begun = sig("acc_begun")
        hn_ready = sig("hn_ready3")
        turned_in = sig("turned_in")
        hT_ready = sig("hT_ready")
        logits_made = sig("logits_made")
        logits_ready = sig("logits_ready")
        exp_ready = sig("exp_ready3")
        route = sig("route")
        chosen_ready = sig("chosen_ready")
        counted = sig("counted")
        hots_ready = sig("hots_ready")
        placed = sig("placed")
        table_ready = sig("table_ready")
        rows_copied = sig("rows_copied", 2)
        rows_seen = sig("rows_seen", 2)
        gathered = [sig(f"gathered{i}", 16) for i in range(2)]
        x_turned = sig("x_turned", 2)
        xT_ready = sig("xT_ready3", 2)
        gate_made = sig("gate_made", 2)
        up_made = sig("up_made", 2)
        silu_ready = sig("silu_ready", 2)
        row_ready = sig("row_ready", 2)
        act_turned = sig("act_turned", 2)
        actT_ready = sig("actT_ready", 4)
        down_made = sig("down_made", 2)
        y_ready = sig("y_ready", 2)
        y_stored = [sig(f"y_stored{i}", 16) for i in range(2)]
        result_in = [sig(f"result_in{i}") for i in range(RING)]
        added = sig("added3")
        ln_step = sig("ln_step3")
        rstd_ready = sig("rstd_ready3")
        out_ready = sig("out_ready")
        out_stored = sig("out_stored")

        def tile_done(engine, signal, turn, k):
            value = (k + 1) * signal.per // 2
            if isinstance(turn, int) and turn * signal.per + value <= 0:
                return
            engine.wait_ge(signal.sem, turn * signal.per + value)

        def ring_done(engine, signals, turn, k):
            value = (k // 2 + 1) * 16
            if isinstance(turn, int) and turn * 16 + value <= 0:
                return
            engine.wait_ge(signals[k % 2].sem, turn * 16 + value)

        def run_tiles(engine, turn):
            turn(0, True, False)
            with engine.Fori(1, NP // 2 - 1) as ee:
                turn(ee, False, False)
            turn(NP // 2 - 1, False, True)

        def at(turn, k, width=1):
            if isinstance(turn, int):
                return slice((2 * turn + k) * width, (2 * turn + k + 1) * width)
            return bass.ds(turn * (2 * width) + k * width, width)

        block = ctx.enter_context(nc.Block())

        @block.sync
        def _(sp):
            for dst, src in ((gate_w[:], io["gate_wT"].rearrange("(t p) e -> p t e", p=P)), (norm_col[:], io["ffn_norm"]),
                             (ident[:], io["ident"]), (before[:], io["before"]), (token_no[:], io["token_no"]),
                             (expert_no[:], io["place_no"][:, 0:E].to_broadcast([P, E])),
                             (place_no[:], io["place_no"].to_broadcast([P, P])),
                             (new_expert[:], io["new_expert"].to_broadcast([P, E * J]))):
                small_in.inc(sp.dma_start(dst, src), 16)

            def load_hidden(c):
                if c >= 2:
                    sp.wait_ge(turned_in.sem, FT * (c - 1))
                    sp.wait_ge(hn_stored[c % 2].sem, 16 * (c // 2))
                hidden_in[c % 2].inc(sp.dma_start(hbuf[:, c % 2], hidden_dram[c].rearrange("(t p) f -> p t f", p=P)), 16)

            def load_x2(c):
                acc_in[c].inc(sp.dma_start(acc[:, ST * c:ST * (c + 1), :], x2_dram[c].rearrange("(t p) f -> p t f", p=P)), 16)

            def load_in(w, name, e):
                weights_in.inc(sp.dma_start(w[:, e * FT * I:(e + 1) * FT * I].rearrange("p (t i) -> p t i", i=I),
                                            io[name][e].rearrange("(t p) i -> p t i", p=P)), 16)

            load_hidden(0)
            load_hidden(1)
            load_x2(0)
            load_x2(1)
            for c in range(2, B):
                load_hidden(c)
                load_x2(c)
                for e in range(E * (c - 2) // (B - 2), E * (c - 1) // (B - 2)):
                    load_in(wg, "wgT", e)
            for e in range(E):
                load_in(wu, "wuT", e)
            for e in range(E):
                wd_e = wd[:, e * IT * F:(e + 1) * IT * F].rearrange("p (t f) -> p t f", f=F)
                weights_in.inc(sp.dma_start(wd_e[:, 0:IT - 1], io["wdT"][e, 0:(IT - 1) * P].rearrange("(t p) f -> p t f", p=P)), 16)
                weights_in.inc(sp.dma_start(wd_e[0:IL, IT - 1], io["wdT"][e, (IT - 1) * P:]), 16)

            def turn(ee, first, last):
                for q in range(2):
                    tile_done(sp, y_ready, ee, q)
                    sp.dma_start(y_dram[at(ee, q, P)], y_row[:, q, :]).then_inc(y_stored[q].sem, 16)

            run_tiles(sp, turn)
            for c in range(B):
                sp.wait_ge(out_ready.sem, ST * (c + 1))
                out_stored.inc(sp.dma_start(out[c].rearrange("(t p) f -> p t f", p=P), acc[:, ST * c:ST * (c + 1), :]), 16)
            sp.wait_ge(out_stored.sem, out_stored.n)

        @block.tensor
        def _(pe):
            pe.wait_ge(small_in.sem, small_in.n)
            for c in range(B):
                pe.wait_ge(hn_ready.sem, ST * (c + 1))
                for k in range(FT):
                    n = FT * c + k
                    if n >= 2:
                        pe.wait_ge(hT_ready.sem, n - 1)
                    for i in range(ST):
                        mm = pe.transpose(ps_d[n % 2][:, i * P:(i + 1) * P], hbuf[:, c % 2, i, k * P:(k + 1) * P], ident[:, :])
                    turned_in.inc(mm)
                pe.wait_ge(hT_ready.sem, FT * (c + 1))
                for i in range(ST):
                    t = ST * c + i
                    for k in range(FT):
                        mm = pe.matmul(ps_g[0][:, t * E:(t + 1) * E], hT[:, k, i * P:(i + 1) * P], gate_w[:, k, :],
                                       start=(k == 0), stop=(k == FT - 1))
                logits_made.inc(mm)
            pe.wait_ge(chosen_ready.sem, 1)
            flat = chosen[:].rearrange("p e j -> p (e j)")
            pe.matmul(ps_u[0][:, 0:E * J], before[:, :], flat, start=True, stop=True)
            counted.inc(pe.matmul(ps_u[1][:, 0:E * J], ones[:, :], flat, start=True, stop=True))
            for j in range(J):
                if j % NT == 0:
                    pe.wait_ge(hots_ready.sem, 2 + j // NT)
                mm = pe.matmul(ps_d[0][:, 0:NP], row_hot[:, j, :], tile_hot[:, j, :], start=(j == 0), stop=(j == J - 1))
            placed.inc(mm)
            pe.wait_ge(weights_in.sem, weights_in.n)
            pe.wait_ge(table_ready.sem, 2)

            def expert(ee, k):
                return pe.value_load(expert_of[0:1, at(ee, k)], min_val=0, max_val=E - 1)

            def turn_x(ee, k):
                ring_done(pe, gathered, ee, k)
                tile_done(pe, xT_ready, ee, k - 1)
                for j in range(FT):
                    mm = pe.transpose(ps_x[:, j * P:(j + 1) * P], xg[:, k % 2, j * P:(j + 1) * P], ident[:, :])
                mm.then_inc(x_turned.sem, 1)

            def project(bank, w, e, q):
                for j in range(FT):
                    mm = pe.matmul(bank[:, 0:I], xT[:, q, j * P:(j + 1) * P], w[:, bass.ds(e * (FT * I) + j * I, I)],
                                   start=(j == 0), stop=(j == FT - 1))
                return mm

            def turn_act(ee, k):
                tile_done(pe, row_ready, ee, k)
                tile_done(pe, actT_ready, ee, k - 1)
                for j in range(IT):
                    w = P if j < IT - 1 else IL
                    mm = pe.transpose(ps_a[0:w, j * P:(j + 1) * P], act_row[:, k % 2, j * P:j * P + w], ident[:, :])
                mm.then_inc(act_turned.sem, 1)

            def down(ee, k, e):
                tile_done(pe, actT_ready, ee, k)
                tile_done(pe, y_ready, ee, k - 2)
                for j in range(IT):
                    w = P if j < IT - 1 else IL
                    mm = pe.matmul(ps_d[k % 2][:, :], actT[0:w, k % 2, j * P:(j + 1) * P], wd[0:w, bass.ds(e * (IT * F) + j * F, F)],
                                   start=(j == 0), stop=(j == IT - 1))
                mm.then_inc(down_made.sem, 1)

            def turn(ee, first, last):
                for q in range(2):
                    e = expert(ee, q)
                    e_last = None if first and q == 0 else expert(ee, q - 1)
                    tile_done(pe, xT_ready, ee, q)
                    tile_done(pe, silu_ready, ee, q - 2)
                    project(ps_g[q], wg, e, q).then_inc(gate_made.sem, 1)
                    if e_last is not None:
                        turn_act(ee, q - 1)
                    if not (last and q == 1):
                        turn_x(ee, q + 1)
                    tile_done(pe, row_ready, ee, q - 2)
                    project(ps_u[q], wu, e, q).then_inc(up_made.sem, 1)
                    if e_last is not None:
                        down(ee, q - 1, e_last)
                if last:
                    turn_act(ee, 1)
                    down(ee, 1, e)

            turn_x(0, 0)
            run_tiles(pe, turn)

        @block.scalar
        def _(act):
            act.wait_ge(small_in.sem, small_in.n)
            for c in range(B):
                act.wait_ge(hidden_in[c % 2].sem, 16 * (c // 2 + 1))
                for i in range(ST):
                    if i:
                        act.wait_ge(squared.sem, squared.n)
                    squared.inc(act.activation(square[:, :], hbuf[:, c % 2, i, :], ACT.Square, accum_out=ss[:, ST * c + i:ST * c + i + 1]))
                act.wait_ge(squared.sem, squared.n)
                act.wait_ge(hn_ready.sem, ST * (c + 1))
                hn_stored[c % 2].inc(act.dma_start(hn_dram[S * c:S * (c + 1)].rearrange("(t p) f -> p t f", p=P), hbuf[:, c % 2]), 16)
                if c:
                    act.wait_ge(logits_made.sem, c)
                for k in range(FT):
                    n = FT * c + k
                    act.wait_ge(turned_in.sem, n + 1)
                    hT_ready.inc(act.activation(hT[:, k, :], ps_d[n % 2][:, :], ACT.Copy, scale=norm_col[:, k:k + 1]))
            act.wait_ge(route.sem, 1)
            exp_ready.inc(act.activation(small[:, 1, :], small[:, 0, :], ACT.Exp))
            exp_ready.inc(act.activation(shifted[:], shifted[:], ACT.Exp))

            def keep_y(ee, k):
                tile_done(act, down_made, ee, k)
                ring_done(act, y_stored, ee, k - 2)
                act.activation(y_row[:, k % 2, :], ps_d[k % 2][:, :], ACT.Copy).then_inc(y_ready.sem, 1)

            def keep_actT(ee, k):
                q = k % 2
                tile_done(act, act_turned, ee, k)
                tile_done(act, down_made, ee, k - 2)
                act.activation(actT[:, q, 0:(IT - 1) * P], ps_a[:, 0:(IT - 1) * P], ACT.Copy).then_inc(actT_ready.sem, 1)
                act.activation(actT[0:IL, q, (IT - 1) * P:], ps_a[0:IL, (IT - 1) * P:IT * P], ACT.Copy).then_inc(actT_ready.sem, 1)

            def turn(ee, first, last):
                for q in range(2):
                    if not first:
                        keep_y(ee, q - 2)
                    tile_done(act, gate_made, ee, q)
                    tile_done(act, row_ready, ee, q - 2)
                    act.activation(silu[:, q, :], ps_g[q][:, 0:I], ACT.Silu).then_inc(silu_ready.sem, 1)
                    if not (first and q == 0):
                        keep_actT(ee, q - 1)
                if last:
                    keep_y(ee, 0)
                    keep_actT(ee, 1)
                    keep_y(ee, 1)

            run_tiles(act, turn)

        @block.vector
        def _(dve):
            consts_ready.inc(dve.memset(mhalf[:], -0.5))
            consts_ready.inc(dve.memset(ones[:], 1.0))
            dve.wait_ge(small_in.sem, small_in.n)

            def step(signal, instruction):
                signal.inc(instruction)
                dve.wait_ge(signal.sem, signal.n)

            for c in range(B):
                own = slice(ST * c, ST * (c + 1))
                dve.wait_ge(squared.sem, ST * (c + 1))
                eps_added.inc(dve.tensor_scalar(ssv[:, own], ss[:, own], 1.0 / F, EPS, ALU.mult, ALU.add))
                dve.wait_ge(acc_in[c].sem, 16)
                acc_begun.inc(dve.tensor_tensor(acc[:, own, :], acc[:, own, :], hbuf[:, c % 2], ALU.add))
                dve.wait_ge(acc_begun.sem, c + 1)
                dve.wait_ge(hr_ready.sem, c + 1)
                for i in range(ST):
                    hn_ready.inc(dve.tensor_scalar(hbuf[:, c % 2, i, :], hbuf[:, c % 2, i, :], hr[:, ST * c + i:ST * c + i + 1], None, ALU.mult))
            dve.wait_ge(logits_made.sem, B)
            step(logits_ready, dve.tensor_copy(logits[:].rearrange("p t e -> p (t e)"), ps_g[0][:, 0:NT * E]))
            for t in range(NT):
                logits_ready.inc(dve.max(top[:, t, :], logits[:, t, :]))
            dve.wait_ge(logits_ready.sem, 1 + NT)
            for t in range(NT):
                logits_ready.inc(dve.max_index(topi[:, t, :], top[:, t, :], logits[:, t, :]))
            dve.wait_ge(logits_ready.sem, 1 + 2 * NT)

            def wide(ap, n):
                return ap.rearrange("p (t o) -> p t o", o=1).to_broadcast([ap.shape[0], ap.shape[1], n])

            def tall(ap, n):
                return ap.rearrange("p (o t) -> p o t", o=1).to_broadcast([ap.shape[0], n, ap.shape[1]])

            step(logits_ready, dve.tensor_copy(topf[:], topi[:, :, 0:2].rearrange("p t k -> p k t")))
            chosen_ready.inc(dve.tensor_tensor(chosen[:], wide(expert_no[:, :], J), tall(topf[:].rearrange("p k t -> p (k t)"), E), ALU.is_equal))

            def row(k):
                return small[:, k, :]

            step(logits_ready, dve.tensor_tensor(shifted[:], logits[:], wide(top[:, :, 0], E), ALU.subtract))
            step(route, dve.tensor_tensor(row(0), top[:, :, 1], top[:, :, 0], ALU.subtract))
            dve.wait_ge(counted.sem, 1)
            ranks = ps_u[0][:, 0:E * J].rearrange("p (e j) -> p e j", j=J)
            counts = ps_u[1][:, 0:E * J].rearrange("p (e j) -> p e j", j=J)
            step(route, dve.tensor_tensor_scan(upto[:].rearrange("p e j -> p (e j)"), new_expert[:], ps_u[1][:, 0:E * J], 0.0, ALU.mult, ALU.add))
            step(route, dve.tensor_scalar(per_expert[:, 0, :], upto[:, :, J - 1], 1.0 / P, None, ALU.mult))
            step(route, dve.tensor_tensor(begun[:], wide(per_expert[:, 0, :], NT), tall(place_no[:, 0:NT], E), ALU.is_gt))
            step(route, dve.tensor_reduce(per_expert[:, 1, :], begun[:], AX.X, ALU.add))
            step(route, dve.tensor_tensor_scan(per_expert[:, 2, :], new_expert[:, 0:E], per_expert[:, 1, :], 0.0, ALU.mult, ALU.add))
            step(route, dve.tensor_tensor(per_expert[:, 3, :], per_expert[:, 2, :], per_expert[:, 1, :], ALU.subtract))
            step(route, dve.tensor_scalar(per_expert[:, 3, :], per_expert[:, 3, :], float(P), None, ALU.mult))
            step(route, dve.tensor_tensor(upto[:], upto[:], counts, ALU.subtract))
            step(route, dve.tensor_tensor(upto[:], upto[:], ranks, ALU.add))
            step(route, dve.tensor_tensor(upto[:], upto[:], wide(per_expert[:, 3, :], J), ALU.add))
            step(route, dve.tensor_tensor(upto[:], upto[:], chosen[:], ALU.mult))
            step(route, dve.tensor_reduce(pos[:], upto[:].rearrange("p e j -> p j e"), AX.X, ALU.add))
            step(route, dve.tensor_copy(pos_u[:], pos[:]))
            route.inc(dve.tensor_scalar(pos_hi[:], pos_u[:], P.bit_length() - 1, None, ALU.logical_shift_right))
            step(route, dve.tensor_scalar(pos_lo[:], pos_u[:], P - 1, None, ALU.bitwise_and))
            route.inc(dve.tensor_copy(tile_of[:], pos_hi[:]))
            step(route, dve.tensor_copy(row_of[:], pos_lo[:]))
            step(route, dve.tensor_tensor(tile_hot, tall(place_no[:, 0:NP], J), wide(tile_of[:], NP), ALU.is_equal))
            hots_ready.inc(dve.tensor_tensor(tile_hot, tile_hot, wide(token_no[:], NP), ALU.mult))
            for stored in hn_stored:
                dve.wait_ge(stored.sem, stored.n)
            for k in range(2):
                half = slice(k * NT, (k + 1) * NT)
                hots_ready.inc(dve.tensor_tensor(row_hot[:, half], tall(place_no[:], NT), wide(row_of[:, half], P), ALU.is_equal))
            step(route, dve.tensor_tensor(ended[:], wide(place_no[0:1, 0:NP], E), tall(per_expert[0:1, 2, :], NP), ALU.is_ge))
            step(route, dve.tensor_reduce(expert_f[:], ended[:], AX.X, ALU.add))
            step(route, dve.tensor_scalar(expert_f[:], expert_f[:], float(E - 1), None, ALU.min))
            table_ready.inc(dve.tensor_copy(expert_of[:], expert_f[:]))
            dve.wait_ge(placed.sem, 1)
            table_ready.inc(dve.tensor_copy(token_of[:], ps_d[0][:, 0:NP]))
            dve.wait_ge(exp_ready.sem, 2)
            step(route, dve.tensor_reduce(row(2), shifted[:], AX.X, ALU.add))
            step(route, dve.reciprocal(row(3), row(2)))
            step(route, dve.tensor_tensor(row(4), row(1), row(3), ALU.mult))
            step(route, dve.scalar_tensor_tensor(row(5), row(3), 1e-9, row(4), ALU.add, ALU.add))
            step(route, dve.reciprocal(row(6), row(5)))
            step(route, dve.tensor_tensor(row(3), row(3), row(6), ALU.mult))
            step(route, dve.tensor_tensor(row(4), row(4), row(6), ALU.mult))

            def keep_xT(ee, k):
                tile_done(dve, x_turned, ee, k)
                tile_done(dve, up_made, ee, k - 2)
                dve.tensor_tensor(xT[:, k % 2, :].rearrange("p (t o) -> p t o", o=P), ps_x[:, :].rearrange("p (t o) -> p t o", o=P),
                                  wide(norm_col[:], P), ALU.mult).then_inc(xT_ready.sem, 1)

            def turn(ee, first, last):
                for q in range(2):
                    if not (last and q == 1):
                        keep_xT(ee, q + 1)
                    tile_done(dve, up_made, ee, q)
                    tile_done(dve, silu_ready, ee, q)
                    tile_done(dve, act_turned, ee, q - 2)
                    dve.tensor_tensor(act_row[:, q, :], ps_u[q][:, 0:I], silu[:, q, :], ALU.mult).then_inc(row_ready.sem, 1)

            keep_xT(0, 0)
            run_tiles(dve, turn)

            def normed(c):
                dve.wait_ge(rstd_ready.sem, c + 1)
                for i in range(ST):
                    t = ST * c + i
                    out_ready.inc(dve.tensor_scalar(acc[:, t, :], acc[:, t, :], mv[:, t, 0:1], rstd[:, t:t + 1], ALU.subtract, ALU.mult))

            for c in range(B):
                for k in range(2):
                    for i in range(ST):
                        t = ST * c + i
                        n = 2 * ST * c + ST * k + i
                        dve.wait_ge(result_in[n % RING].sem, 16 * (n // RING + 1))
                        if k:
                            dve.wait_ge(added.sem, n - ST + 1)
                        added.inc(dve.scalar_tensor_tensor(acc[:, t, :], results[:, n % RING, :], small[:, 3 + k, t:t + 1],
                                                           acc[:, t, :], ALU.mult, ALU.add))
                for i in range(ST):
                    dve.wait_ge(added.sem, 2 * ST * (c + 1) - ST + i + 1)
                    ln_step.inc(dve.bn_stats(stats[:, i, :], acc[:, ST * c + i, :]))
                dve.wait_ge(ln_step.sem, ln_step.n)
                for i in range(ST):
                    ln_step.inc(dve.bn_aggr(mv[:, ST * c + i, :], stats[:, i, :]))
                dve.wait_ge(ln_step.sem, ln_step.n)
                step(ln_step, dve.tensor_scalar(veps[:, ST * c:ST * (c + 1)], mv[:, ST * c:ST * (c + 1), 1], 1e-5, None, ALU.add))
                assert ln_step.n == (2 * ST + 1) * (c + 1)
                if c:
                    normed(c - 1)
            normed(B - 1)

        @block.gpsimd
        def _(pool):
            pool.wait_ge(consts_ready.sem, 2)
            for c in range(B):
                own = slice(ST * c, ST * (c + 1))
                pool.wait_ge(eps_added.sem, c + 1)
                hr_ready.inc(pool.tensor_tensor(hr[:, own], ssv[:, own], mhalf[:, own], ALU.pow))
            pool.wait_ge(table_ready.sem, 2)
            for stored in hn_stored:
                pool.wait_ge(stored.sem, stored.n)

            def turn(ee, first, last):
                for q in range(2):
                    tile_done(pool, x_turned, ee, q - 2)
                    pool.tensor_copy(rows_of[q][:, :], token_of[:, at(ee, q)]).then_inc(rows_copied.sem, 1)
                    tile_done(pool, rows_copied, ee, q)
                    pool.sem_inc(rows_seen.sem, 1)
                    pool.indirect_dma_start(xg[:, q, :], None, hn_dram,
                                            bass.IndirectOffsetOnAxis(ap=rows_of[q][:, :], axis=0)).then_inc(gathered[q].sem, 16)

            def rsqrt(c):
                own = slice(ST * c, ST * (c + 1))
                pool.wait_ge(ln_step.sem, (2 * ST + 1) * (c + 1))
                rstd_ready.inc(pool.tensor_tensor(rstd[:, own], veps[:, own], mhalf[:, own], ALU.pow))

            run_tiles(pool, turn)
            for q in range(2):
                pool.wait_ge(y_stored[q].sem, 16 * (NP // 2))
            for c in range(B):
                for k in range(2):
                    for i in range(ST):
                        t = ST * c + i
                        n = 2 * ST * c + ST * k + i
                        if n >= RING:
                            pool.wait_ge(added.sem, n - RING + 1)
                        result_in[n % RING].inc(pool.indirect_dma_start(
                            results[:, n % RING, :], None, y_dram,
                            bass.IndirectOffsetOnAxis(ap=pos_u[:, k * NT + t:k * NT + t + 1], axis=0)), 16)
                if c:
                    rsqrt(c - 1)
            rsqrt(B - 1)


def build(nc, io, out):
    B, S, F = io["x"].shape
    x2 = nc.dram_tensor("x2", (B, S, F), F32, kind="Internal").ap()
    bc_dram = nc.dram_tensor("bc_rows", (2 * io["A_log"].shape[1], S), F32, kind="Internal").ap()
    hidden = nc.dram_tensor("hidden", (B, S, F), F32, kind="Internal").ap()
    attention_and_scan(nc, io, x2, bc_dram)
    grouped_attention(nc, io, x2, hidden)
    mixture_of_experts(nc, io, x2, hidden, out)


def shape_constants(length, width):
    freqs = (1.0 / np.float32(1000000.0) ** (np.arange(0, width, 2, dtype=np.float32) / np.float32(width))).astype(np.float32)
    angle = np.outer(np.arange(length, dtype=np.float32), freqs).astype(np.float32)
    cos, sin = np.cos(angle), np.sin(angle)
    return {"cos": np.concatenate([cos, cos], 1), "sin": np.concatenate([-sin, sin], 1),
            "mask": np.triu(np.ones((P, P), np.float32), 1) * np.float32(-1e30)}


def laid_out(inputs):
    i = {k: np.asarray(a) for k, a in inputs.items()}

    def T(a):
        return np.ascontiguousarray(np.swapaxes(a, -1, -2))

    def columns(a):
        return np.ascontiguousarray(a.reshape(-1, P).T)

    a, s = "L0_attn_", "L0_xattn_"
    got = {"x": i["x"], "xT": T(i["x"]), "ctxT": T(i["ctx_1024"])}
    for w in "qkvo":
        got["W" + w] = i[a + "W" + w]
    got |= {"bq": columns(i[a + "bq"]), "bk": columns(i[a + "bk"]), "bv": i[a + "bv"][None], "bo": i[a + "bo"][None]}
    got |= {"in_wT": T(i[s + "in_proj_w"]), "conv_w": i[s + "conv_w"][:, 0, :], "conv_b": columns(i[s + "conv_b"]),
            "x_wT": T(i[s + "x_proj_w"]), "dt_wT": T(i[s + "dt_proj_w"]), "dt_b": columns(i[s + "dt_proj_b"]),
            "A_log": i[s + "A_log"], "Dskip": columns(i[s + "D"])}
    f = "L0_ffn_"
    got |= {"q_wT": T(i[f + "q_w"]), "k_wT": T(i[f + "k_w"]), "v_wT": T(i[f + "v_w"]), "o_wT": T(i[f + "o_w"]),
            "attn_norm": columns(i[f + "attn_norm_w"]), "q_norm": i[f + "q_norm_w"][None], "k_norm": i[f + "k_norm_w"][None]}
    got |= shape_constants(i["x"].shape[1], i[f + "q_norm_w"].shape[0])
    got |= {"gate_wT": T(i[f + "gate_w"]), "ffn_norm": columns(i[f + "ffn_norm_w"]),
            "wgT": T(i[f + "wg"]), "wuT": T(i[f + "wu"]), "wdT": T(i[f + "wd"]),
            "before": np.triu(np.ones((P, P), np.float32), 1)}
    tokens, experts = i["x"].shape[0] * i["x"].shape[1], i[f + "gate_w"].shape[0]
    number = np.arange(tokens, dtype=np.float32).reshape(-1, P).T
    first = np.ones((experts, 2 * tokens // P), np.float32)
    first[:, 0] = 0
    got |= {"place_no": np.arange(P, dtype=np.float32)[None], "token_no": np.concatenate([number, number], 1), "new_expert": first.reshape(1, -1)}
    got["ident"] = np.eye(P, dtype=np.float32)
    return {k: np.ascontiguousarray(v) for k, v in got.items()}


def kernel(**inputs):
    import concourse.bacc as bacc
    from concourse.bass_utils import run_bass_kernel_spmd

    data = laid_out(inputs)
    nc = bacc.Bacc("TRN2", target_bir_lowering=False, num_devices=1)
    arrays, io = {}, {}
    for name, a in data.items():
        arrays["in_" + name] = a
        io[name] = nc.dram_tensor("in_" + name, a.shape, mybir.dt.from_np(a.dtype), kind="ExternalInput").ap()
    out = nc.dram_tensor("out", inputs["x"].shape, F32, kind="ExternalOutput").ap()
    build(nc, io, out)
    return run_bass_kernel_spmd(nc, [arrays], core_ids=[0]).results[0]["out"]
```

```python
from contextlib import ExitStack

import numpy as np

import concourse.bass as bass
from concourse import mybir
from concourse.alu_op_type import AluOpType as ALU

F32 = mybir.dt.float32
ACT = mybir.ActivationFunctionType
AX = mybir.AxisListType

P = 128


class Signal:

    def __init__(self, sem, per_turn=0, primed=False, base=0):
        self.sem, self.per, self.n, self.primed, self.base = sem, per_turn, 0, primed, base

    def prime(self, engine):
        engine.sem_inc(self.sem, 1)

    def inc(self, instruction, by=1):
        self.n += by
        return instruction.then_inc(self.sem, by)

    def wait(self, engine, turn, count):
        if turn is None:
            engine.wait_ge(self.sem, count + self.primed)
            return
        assert count + self.base > 0 or self.primed
        engine.wait_ge(self.sem, turn * self.per + (self.base + count + self.primed))

    def wait_last(self, engine, turn):
        self.wait(engine, turn, self.n)

    def wait_all(self, engine, count):
        engine.wait_ge(self.sem, count + self.primed)

    def close(self):
        assert self.n == self.per, (self.sem, self.n, self.per)


def attention_and_scan(nc, io, x2_dram, bc_dram):
    B, S, F = io["x"].shape
    DM = io["ctxT"].shape[1]
    NS = io["A_log"].shape[1]
    R = io["dt_wT"].shape[0]
    XD = R + 2 * NS
    KC = io["conv_w"].shape[1]
    HD = 64
    NH = F // HD
    FT, ST, MT = F // P, S // P, DM // P
    NPAIR = NH // 2
    QSCALE = float(1.0 / np.sqrt(float(NH)))
    SMALL = 2.0 ** -7
    assert NS == 2 * NH and ST == 4 and FT == 4

    uses = [("in", e, "act") for e in range(FT)] + [("xp", 0, "act")] + [("dt", e, "dve") for e in range(FT)]
    for p in range(NPAIR):
        uses += [("q", p, "act"), ("k", p, "act"), ("v", p, "dve")]
    uses += [("wo", i, "dve") for i in range(ST)] + [("gT", i, "dve") for i in range(ST)]
    PPU = {(what, k): n for n, (what, k, _) in enumerate(uses)}
    NPP = len(uses)
    emptied = {"act": [0], "dve": [0]}
    for _, _, who in uses:
        for w in emptied:
            emptied[w].append(emptied[w][-1] + (w == who))

    with ExitStack() as ctx:
        def sb(name, shape, dt=F32):
            return ctx.enter_context(nc.sbuf_tensor("p1_" + name, shape, dt))

        def sig(name, per=0, primed=False):
            return Signal(ctx.enter_context(nc.semaphore("p1_" + name)), per, primed)

        wq, wk, wv, wo = (sb(f"w{c}_sb", [P, FT, F]) for c in "qkvo")
        w_in = sb("w_in", [P, MT, F])
        w_xp = sb("w_xp", [P, FT, XD])
        w_dt = sb("w_dt", [R, F])
        conv_w = sb("conv_w_sb", [P, FT, KC])
        cols = sb("cols", [P, 7, FT])
        a_log = sb("a_log", [P, FT, NS])
        a_neg = sb("a_neg", [P, FT, NS])
        bv_row = sb("bv_row", [P, F])
        bo_row = sb("bo_row", [P, F])
        ident = sb("ident_sb", [P, P])
        mhalf = sb("mhalf", [P, 2 * ST])
        xT = sb("xT_sb", [P, FT, S])
        ctxT = sb("ctxT_sb", [P, MT, S])
        xtok = sb("xtok", [P, ST, F])
        xin = sb("xin", [P, FT, S + KC - 1])
        u = sb("u", [P, FT, S])
        dt = sb("dt", [P, FT, S])
        dtu = sb("dtu", [P, FT, S])
        yacc = sb("yacc", [P, FT, S])
        xdbl = sb("xdbl", [XD, S])
        decay = sb("decay", [P, 2, FT, S])
        hbuf = sb("hbuf", [P, 2, FT, S])
        bc = sb("bc", [P, 4, 2, S])
        qT = sb("qT", [P, 2, S])
        kT = sb("kT", [P, 2, S])
        v = sb("v", [P, 2, ST, P])
        prob = sb("prob", [P, 2, ST, S])
        probT = sb("probT", [P, 2, ST, S])
        feats = sb("feats", [P, NPAIR, S])
        nmax = sb("nmax", [P, 2, ST])
        rsum = sb("rsum", [P, 2, ST])
        rinv = sb("rinv", [P, 2, ST])
        stats = sb("stats", [P, ST, 6])
        mv = sb("mv", [P, ST, 2])
        veps = sb("veps", [P, ST])
        rstd = sb("rstd", [P, ST])

        pp = [ctx.enter_context(nc.psum_tensor(f"p1_pp{i}", [P, 512], F32)) for i in range(2)]
        ps_s = [ctx.enter_context(nc.psum_tensor(f"p1_ps_s{i}", [P, 512], F32)) for i in range(2)]
        ps_t = [ctx.enter_context(nc.psum_tensor(f"p1_ps_t{i}", [P, 512], F32)) for i in range(2)]
        ps_o = [ctx.enter_context(nc.psum_tensor(f"p1_ps_o{i}", [P, 512], F32)) for i in range(2)]

        weights_in = sig("weights_in")
        a_ready = sig("a_ready")
        pads_ready = sig("pads_ready")
        x_in = sig("x_in", 32)
        xtok_in = sig("xtok_in", 16)
        pp_ready = sig("pp_ready", NPP, primed=True)
        pp_free = {"act": sig("pp_free_act", emptied["act"][-1], primed=True), "dve": sig("pp_free_dve", emptied["dve"][-1], primed=True)}
        conv_step = sig("conv_step", FT * KC, primed=True)
        u_ready = sig("u_ready", 1)
        bc_stored = sig("bc_stored", 16, primed=True)
        bc_in = [sig(f"bc_in{i}", 16 * NS // 4) for i in range(4)]
        sp_act = sig("sp_act", 3)
        sp_dve = sig("sp_dve", 8)
        y_begun = sig("y_begun", FT)
        decay_ready = sig("decay_ready", NS * FT)
        dbu_ready = sig("dbu_ready", NS)
        scanned = sig("scanned", NS * FT)
        hc_ready = sig("hc_ready", NS, primed=True)
        y_added = sig("y_added", NS, primed=True)
        scores_ready = sig("scores_ready", NH * ST)
        max_ready = sig("max_ready", NH * ST)
        exp_ready = sig("exp_ready", NH * ST, primed=True)
        rinv_ready = sig("rinv_ready", NH)
        normed = sig("normed", NH * ST)
        turned = sig("turned", NH * ST)
        probT_ready = sig("probT_ready", NH * ST, primed=True)
        pv_ready = sig("pv_ready", NPAIR)
        feats_ready = sig("feats_ready", NPAIR, primed=True)
        resid = sig("resid", 1)
        ln_step = sig("ln_step", 2 * (2 * ST + 1) + ST)
        rstd_ready = sig("rstd_ready", 2)
        x1_ready = sig("x1_ready", ST)
        gate_ready = sig("gate_ready", 1)
        g_ready = sig("g_ready", 1)
        x2_stored = sig("x2_stored", 16, primed=True)

        stats_seen = ctx.enter_context(nc.semaphore("stats_seen"))
        block = ctx.enter_context(nc.Block())

        col_names = ("bq", "bk", "conv_b", "dt_b", "Dskip")

        def settled(engine):
            engine.wait_ge(pads_ready.sem, 2)

        @block.sync
        def _(sp):
            bc_stored.prime(sp)
            def const(dst, src):
                weights_in.inc(sp.dma_start(dst, src), 16)

            def rows(name):
                return io[name].rearrange("(t p) n -> p t n", p=P)

            const(w_in[:], rows("in_wT"))
            const(conv_w[:], rows("conv_w"))
            for c, name in enumerate(col_names):
                const(cols[:, c, :], io[name])
            const(w_xp[:], rows("x_wT"))
            const(w_dt[:], io["dt_wT"])
            const(a_log[:], rows("A_log"))
            const(wq[:], rows("Wq"))
            const(wk[:], rows("Wk"))
            const(wv[:], rows("Wv"))
            const(wo[:], rows("Wo"))
            const(bv_row[:], io["bv"].to_broadcast([P, F]))
            const(bo_row[:], io["bo"].to_broadcast([P, F]))
            const(ident[:], io["ident"])
            with sp.Fori(0, B) as b:
                pp_ready.wait(sp, b, 0)
                settled(sp)
                x_in.inc(sp.dma_start(ctxT[:], io["ctxT"][bass.ds(b, 1)].rearrange("o (t p) s -> p (o t) s", p=P)), 16)
                x_in.inc(sp.dma_start(xT[:], io["xT"][bass.ds(b, 1)].rearrange("o (t p) s -> p (o t) s", p=P)), 16)
                x2_stored.wait(sp, b, 0)
                settled(sp)
                xtok_in.inc(sp.dma_start(xtok[:], io["x"][bass.ds(b, 1)].rearrange("o (t p) f -> p (o t) f", p=P)), 16)
                pp_free["act"].wait(sp, b, emptied["act"][PPU["xp", 0] + 1])
                bc_stored.inc(sp.dma_start(bc_dram, xdbl[R:XD, :]), 16)
                bc_stored.wait(sp, b, 16)
                for n in range(NS):
                    hc_ready.wait(sp, b, max(n - 3, 0))
                    src = bc_dram.rearrange("(o c n) s -> n o c s", o=1, c=2)[n].to_broadcast([P, 2, S])
                    bc_in[n % 4].inc(sp.dma_start(bc[:, n % 4], src), 16)
            for s in (x_in, xtok_in, bc_stored, *bc_in):
                s.close()

        def pp_take(pe, b, key):
            k = PPU[key]
            if k < 2:
                for who in ("act", "dve"):
                    pp_free[who].wait(pe, b, 0)
            else:
                who = uses[k - 2][2]
                pp_free[who].wait(pe, b, emptied[who][k - 1])
            return pp[k % 2]

        @block.tensor
        def _(pe):
            pp_ready.prime(pe)
            pe.wait_ge(weights_in.sem, weights_in.n)
            with pe.Fori(0, B) as b:
                def gives(ins):
                    pp_ready.inc(ins)

                x_in.wait(pe, b, 32)
                for e in range(FT):
                    bank = pp_take(pe, b, ("in", e))
                    for k in range(MT):
                        mm = pe.matmul(bank[:, :], w_in[:, k, e * P:(e + 1) * P], ctxT[:, k, :],
                                       start=(k == 0), stop=(k == MT - 1))
                    gives(mm)
                bank = pp_take(pe, b, ("xp", 0))
                u_ready.wait(pe, b, 1)
                for k in range(FT):
                    mm = pe.matmul(bank[0:XD, :], w_xp[:, k, :], u[:, k, :], start=(k == 0), stop=(k == FT - 1))
                gives(mm)
                for e in range(FT):
                    bank = pp_take(pe, b, ("dt", e))
                    if e == 0:
                        pp_free["act"].wait(pe, b, emptied["act"][PPU["xp", 0] + 1])
                    gives(pe.matmul(bank[:, :], w_dt[:, e * P:(e + 1) * P], xdbl[0:R, :], start=True, stop=True))

                def project(p):
                    for what, w in (("q", wq), ("k", wk)):
                        bank = pp_take(pe, b, (what, p))
                        for k in range(FT):
                            mm = pe.matmul(bank[:, :], w[:, k, p * P:(p + 1) * P], xT[:, k, :],
                                           start=(k == 0), stop=(k == FT - 1))
                        gives(mm)
                    bank = pp_take(pe, b, ("v", p))
                    for t in range(ST):
                        for k in range(FT):
                            mm = pe.matmul(bank[:, t * P:(t + 1) * P], xT[:, k, t * P:(t + 1) * P],
                                           wv[:, k, p * P:(p + 1) * P], start=(k == 0), stop=(k == FT - 1))
                    gives(mm)

                def score(h, i):
                    p, r = h // 2, (h % 2) * HD
                    n = ST * h + i
                    exp_ready.wait(pe, b, max(n - 1, 0))
                    if i == 0:
                        pp_free["act"].wait(pe, b, emptied["act"][PPU["k", p] + 1])
                    scores_ready.inc(pe.matmul(ps_s[n % 2][:, :], qT[r:r + HD, p % 2, i * P:(i + 1) * P],
                                               kT[r:r + HD, p % 2, :], start=True, stop=True))

                def turn(h, j):
                    n = ST * h + j
                    probT_ready.wait(pe, b, max(n - 1, 0))
                    normed.wait(pe, b, ST * (h + 1))
                    for i in range(ST):
                        mm = pe.transpose(ps_t[n % 2][:, i * P:(i + 1) * P], prob[:, h % 2, i, j * P:(j + 1) * P], ident[:, :])
                    turned.inc(mm)

                def weigh(p):
                    feats_ready.wait(pe, b, max(p - 1, 0))
                    probT_ready.wait(pe, b, ST * (2 * p + 2))
                    pp_free["dve"].wait(pe, b, emptied["dve"][PPU["v", p] + 1])
                    for j in range(ST):
                        for hh in range(2):
                            mm = pe.matmul(ps_o[p % 2][hh * HD:(hh + 1) * HD, :], v[:, p % 2, j, hh * HD:(hh + 1) * HD],
                                           probT[:, hh, j, :], start=(j == 0), stop=(j == ST - 1))
                    pv_ready.inc(mm)

                project(0)
                for h in range(NH + 1):
                    for i in range(ST):
                        if h < NH:
                            score(h, i)
                        if h >= 1:
                            turn(h - 1, i)
                    if h % 2 == 0 and h >= 2:
                        weigh(h // 2 - 1)
                    if h % 2 == 1 and h // 2 + 1 < NPAIR:
                        project(h // 2 + 1)
                feats_ready.wait(pe, b, NPAIR)
                for i in range(ST):
                    bank = pp_take(pe, b, ("wo", i))
                    for p in range(NPAIR):
                        mm = pe.matmul(bank[:, :], feats[:, p, i * P:(i + 1) * P], wo[:, p, :],
                                       start=(p == 0), stop=(p == NPAIR - 1))
                    gives(mm)
                for i in range(ST):
                    bank = pp_take(pe, b, ("gT", i))
                    g_ready.wait(pe, b, 1)
                    for e in range(FT):
                        mm = pe.transpose(bank[:, e * P:(e + 1) * P], yacc[:, e, i * P:(i + 1) * P], ident[:, :])
                    gives(mm)
            for s in (pp_ready, scores_ready, turned, pv_ready):
                s.close()

        @block.scalar
        def _(act):
            x2_stored.prime(act)
            exp_ready.prime(act)
            probT_ready.prime(act)
            feats_ready.prime(act)
            pp_free["act"].prime(act)
            act.wait_ge(weights_in.sem, weights_in.n)
            a_ready.inc(act.activation(a_neg[:], a_log[:], ACT.Exp))
            a_ready.inc(act.mul(cols[:, 5, :], cols[:, 0, :], QSCALE))
            act.wait_ge(a_ready.sem, 1)
            a_ready.inc(act.mul(a_neg[:], a_neg[:], -1.0))
            act.wait_ge(a_ready.sem, 3)
            with act.Fori(0, B) as b:
                def empties(what, k, dst, src, **kw):
                    pp_ready.wait(act, b, PPU[what, k] + 1)
                    pp_free["act"].inc(act.activation(dst, src, **kw))

                conv_step.wait(act, b, 0)
                for e in range(FT):
                    n = PPU["in", e]
                    empties("in", e, xin[:, e, KC - 1:], pp[n % 2][:, :], func=ACT.Copy)
                conv_step.wait(act, b, FT * KC)
                u_ready.inc(act.activation(u[:], decay[:, 0], ACT.Silu))
                bc_stored.wait(act, b, 0)
                empties("xp", 0, xdbl[:, :], pp[PPU["xp", 0] % 2][0:XD, :], func=ACT.Copy)
                mag, low = decay[:, 0], decay[:, 1]
                pp_free["dve"].wait(act, b, emptied["dve"][PPU["dt", FT - 1] + 1])
                sp_act.inc(act.activation(mag, dt[:], ACT.Abs))
                sp_act.wait(act, b, 1)
                sp_act.inc(act.activation(mag, mag, ACT.Exp, scale=-1.0))
                sp_act.wait(act, b, 2)
                sp_act.inc(act.activation(low, mag, ACT.Ln, bias=1.0))

                def empty_qk(p):
                    if p >= 2:
                        scores_ready.wait(act, b, ST * 2 * (p - 1))
                    empties("q", p, qT[:, p % 2, :], pp[PPU["q", p] % 2][:, :], func=ACT.Identity,
                            bias=cols[:, 5, p:p + 1], scale=QSCALE)
                    empties("k", p, kT[:, p % 2, :], pp[PPU["k", p] % 2][:, :], func=ACT.Identity,
                            bias=cols[:, 1, p:p + 1])

                def exp_scores(h, i):
                    n = ST * h + i
                    max_ready.wait(act, b, n + 1)
                    if h >= 2:
                        turned.wait(act, b, ST * (h - 1))
                    exp_ready.inc(act.activation(prob[:, h % 2, i, :], ps_s[n % 2][:, :], ACT.Exp,
                                                 bias=nmax[:, h % 2, i:i + 1], accum_out=rsum[:, h % 2, i:i + 1]))

                def copy_turned(h, j):
                    n = ST * h + j
                    turned.wait(act, b, n + 1)
                    if h >= 2 and j == 0:
                        pv_ready.wait(act, b, h // 2)
                    probT_ready.inc(act.activation(probT[:, h % 2, j, :], ps_t[n % 2][:, :], ACT.Copy))

                def exp_decay(n, e):
                    if n >= 2 and e == 0:
                        scanned.wait(act, b, FT * (n - 1))
                    decay_ready.inc(act.activation(decay[:, n % 2, e, :], dt[:, e, :], ACT.Exp,
                                                   scale=a_neg[:, e, n:n + 1]))

                def copy_feats(p):
                    pv_ready.wait(act, b, p + 1)
                    feats_ready.inc(act.activation(feats[:, p, :], ps_o[p % 2][:, :], ACT.Copy))

                empty_qk(0)
                sp_dve.wait(act, b, 7)
                def decays(slot):
                    for e in (2 * (slot % 2), 2 * (slot % 2) + 1):
                        exp_decay(slot // 2, e)

                decays(0)
                for h in range(NH + 1):
                    for i in range(ST):
                        if h < NH:
                            exp_scores(h, i)
                        if ST * h + i + 1 < 2 * NS:
                            decays(ST * h + i + 1)
                        if h >= 1:
                            copy_turned(h - 1, i)
                    if h % 2 == 0 and h >= 2:
                        copy_feats(h // 2 - 1)
                    if h % 2 == 1 and h // 2 + 1 < NPAIR:
                        empty_qk(h // 2 + 1)
                x1_ready.wait(act, b, ST)
                scanned.wait(act, b, NS * FT)
                gate_ready.inc(act.activation(decay[:, 0], xtok[:], ACT.Silu))
                ln_step.wait(act, b, ln_step.per)
                settled(act)
                x2_stored.inc(act.dma_start(x2_dram[bass.ds(b, 1)].rearrange("o (t p) f -> p (o t) f", p=P), xtok[:]), 16)
            x2_stored.wait_all(act, 16 * B)
            for s in (pp_free["act"], u_ready, sp_act, exp_ready, probT_ready, decay_ready, feats_ready, gate_ready, x2_stored):
                s.close()

        @block.vector
        def _(dve):
            conv_step.prime(dve)
            y_added.prime(dve)
            pp_free["dve"].prime(dve)
            dve.wait_ge(weights_in.sem, weights_in.n)
            dve.wait_ge(pads_ready.sem, 2)
            with dve.Fori(0, B) as b:
                for e in range(FT):
                    pp_free["act"].wait(dve, b, emptied["act"][PPU["in", e] + 1])
                    out = decay[:, 0, e, :]
                    conv_step.inc(dve.tensor_scalar(out, xin[:, e, 0:S], conv_w[:, e, 0:1], cols[:, 2, e:e + 1], ALU.mult, ALU.add))
                for k in range(1, KC):
                    for e in range(FT):
                        out = decay[:, 0, e, :]
                        conv_step.wait(dve, b, FT * (k - 1) + e + 1)
                        conv_step.inc(dve.scalar_tensor_tensor(out, xin[:, e, k:k + S], conv_w[:, e, k:k + 1], out, ALU.mult, ALU.add))
                u_ready.wait(dve, b, 1)
                for e in range(FT):
                    y_begun.inc(dve.tensor_scalar(yacc[:, e, :], u[:, e, :], cols[:, 4, e:e + 1], None, ALU.mult))
                for e in range(FT):
                    n = PPU["dt", e]
                    pp_ready.wait(dve, b, n + 1)
                    pp_free["dve"].inc(dve.tensor_scalar(dt[:, e, :], pp[n % 2][:, :], cols[:, 3, e:e + 1], None, ALU.add))
                mag, low, poly, part = decay[:, 0], decay[:, 1], hbuf[:, 0], hbuf[:, 1]

                def step(instruction):
                    sp_dve.inc(instruction)
                    sp_dve.wait_last(dve, b)

                sp_act.wait(dve, b, 2)
                step(dve.tensor_scalar(poly, mag, 1.0 / 3.0, -0.5, ALU.mult, ALU.add))
                step(dve.tensor_tensor(poly, poly, mag, ALU.mult))
                step(dve.scalar_tensor_tensor(poly, poly, 1.0, mag, ALU.add, ALU.mult))
                step(dve.scalar_tensor_tensor(part, mag, SMALL, poly, ALU.is_lt, ALU.mult))
                sp_act.wait(dve, b, 3)
                step(dve.scalar_tensor_tensor(low, mag, SMALL, low, ALU.is_ge, ALU.mult))
                step(dve.tensor_tensor(low, low, part, ALU.add))
                step(dve.scalar_tensor_tensor(dt[:], dt[:], 0.0, low, ALU.max, ALU.add))
                sp_dve.inc(dve.tensor_tensor(dtu[:], dt[:], u[:], ALU.mult))

                def empty_v(p):
                    n = PPU["v", p]
                    pp_ready.wait(dve, b, n + 1)
                    if p >= 2:
                        pv_ready.wait(dve, b, p - 1)
                    pp_free["dve"].inc(dve.tensor_tensor(
                        v[:, p % 2], pp[n % 2][:, :].rearrange("p (t c) -> p t c", t=ST),
                        bv_row[:, p * P:(p + 1) * P].rearrange("p (o c) -> p o c", o=1).to_broadcast([P, ST, P]), ALU.add))

                def row_max(h, i):
                    n = ST * h + i
                    scores_ready.wait(dve, b, n + 1)
                    max_ready.inc(dve.tensor_reduce(nmax[:, h % 2, i:i + 1], ps_s[n % 2][:, :], AX.X, ALU.max, negate=True))

                def norm_inverse(h):
                    exp_ready.wait(dve, b, ST * (h + 1))
                    rinv_ready.inc(dve.reciprocal(rinv[:, h % 2, :], rsum[:, h % 2, :]))

                def normalise(h):
                    rinv_ready.wait(dve, b, h + 1)
                    for i in range(ST):
                        normed.inc(dve.tensor_scalar(prob[:, h % 2, i, :], prob[:, h % 2, i, :], rinv[:, h % 2, i:i + 1], None, ALU.mult))

                def make_dbu(n):
                    bc_in[n % 4].wait(dve, b, 16 * (n // 4 + 1))
                    y_added.wait(dve, b, max(n - 1, 0))
                    if n == 0:
                        sp_dve.wait(dve, b, 8)
                    dbu_ready.inc(dve.tensor_tensor(hbuf[:, n % 2], dtu[:], bc[:, n % 4, 0:1, :].to_broadcast([P, FT, S]), ALU.mult))

                def scan(n, e):
                    decay_ready.wait(dve, b, FT * n + e + 1)
                    if e == 0:
                        dbu_ready.wait(dve, b, n + 1)
                    scanned.inc(dve.tensor_tensor_scan(hbuf[:, n % 2, e, :], decay[:, n % 2, e, :], hbuf[:, n % 2, e, :],
                                                       0.0, ALU.mult, ALU.add))

                def add_y(n):
                    hc_ready.wait(dve, b, n + 1)
                    if n:
                        y_added.wait(dve, b, n)
                    else:
                        y_begun.wait(dve, b, FT)
                    y_added.inc(dve.tensor_tensor(yacc[:], yacc[:], hbuf[:, n % 2], ALU.add))

                empty_v(0)
                for h in range(NH + 1):
                    if h >= 1:
                        norm_inverse(h - 1)
                    for i in range(ST):
                        if h < NH:
                            row_max(h, i)
                        if h >= 1 and i == 0:
                            normalise(h - 1)
                        if h < NH:
                            n = 2 * h + i // 2
                            if i % 2 == 0:
                                make_dbu(n)
                                scan(n, 0)
                                scan(n, 1)
                            else:
                                scan(n, 2)
                                scan(n, 3)
                                if n >= 1:
                                    add_y(n - 1)
                    if h % 2 == 1 and h // 2 + 1 < NPAIR:
                        empty_v(h // 2 + 1)
                add_y(NS - 1)

                def layer_norm(turn):
                    base = turn * (2 * ST + 1)
                    for i in range(ST):
                        (resid if turn == 0 else pp_free["dve"]).wait_last(dve, b)
                        ln_step.inc(dve.bn_stats(stats[:, i, :], xtok[:, i, :]))
                    ln_step.wait(dve, b, base + ST)
                    dve.sem_inc(stats_seen, 1)
                    for i in range(ST):
                        ln_step.inc(dve.bn_aggr(mv[:, i, :], stats[:, i, :]))
                    ln_step.wait(dve, b, base + 2 * ST)
                    ln_step.inc(dve.tensor_scalar(veps[:, :], mv[:, :, 1], 1e-5, None, ALU.add))
                    rstd_ready.wait(dve, b, turn + 1)
                    for i in range(ST):
                        who = x1_ready if turn == 0 else ln_step
                        who.inc(dve.tensor_scalar(xtok[:, i, :], xtok[:, i, :], mv[:, i, 0:1], rstd[:, i:i + 1], ALU.subtract, ALU.mult))

                xtok_in.wait(dve, b, 16)
                resid.inc(dve.tensor_tensor(xtok[:], xtok[:], bo_row[:, :].rearrange("p (o f) -> p o f", o=1).to_broadcast([P, ST, F]), ALU.add))
                resid.wait_last(dve, b)
                for i in range(ST):
                    n = PPU["wo", i]
                    pp_ready.wait(dve, b, n + 1)
                    pp_free["dve"].inc(dve.tensor_tensor(xtok[:, i, :], xtok[:, i, :], pp[n % 2][:, :], ALU.add))
                pp_free["dve"].wait_last(dve, b)
                layer_norm(0)
                gate_ready.wait(dve, b, 1)
                y_added.wait(dve, b, NS)
                g_ready.inc(dve.tensor_tensor(yacc[:], yacc[:], decay[:, 0], ALU.mult))
                for i in range(ST):
                    n = PPU["gT", i]
                    pp_ready.wait(dve, b, n + 1)
                    pp_free["dve"].inc(dve.tensor_tensor(xtok[:, i, :], xtok[:, i, :], pp[n % 2][:, :], ALU.add))
                layer_norm(1)
            for s in (pp_free["dve"], conv_step, sp_dve, y_begun, max_ready, rinv_ready, normed, dbu_ready, scanned, y_added, resid, x1_ready, g_ready, ln_step):
                s.close()

        @block.gpsimd
        def _(pool):
            hc_ready.prime(pool)
            pads_ready.inc(pool.memset(mhalf[:], -0.5))
            pads_ready.inc(pool.memset(xin[:, :, 0:KC - 1], 0.0))
            pool.wait_ge(pads_ready.sem, 2)
            with pool.Fori(0, B) as b:
                for n in range(NS):
                    scanned.wait(pool, b, FT * (n + 1))
                    hc_ready.inc(pool.tensor_tensor(hbuf[:, n % 2], hbuf[:, n % 2], bc[:, n % 4, 1:2, :].to_broadcast([P, FT, S]), ALU.mult))
                for turn in range(2):
                    base = turn * (2 * ST + 1)
                    ln_step.wait(pool, b, base + 2 * ST + 1)
                    rstd_ready.inc(pool.tensor_tensor(rstd[:, :], veps[:, :], mhalf[:, 0:ST], ALU.pow))
            hc_ready.close(); rstd_ready.close()


def grouped_attention(nc, io, x2_dram, hidden_dram):
    B, S, F = io["x"].shape
    HD = P
    HQ = io["q_wT"].shape[1] // HD
    HK = io["k_wT"].shape[1] // HD
    QH = HQ // HK
    FT, ST = F // P, S // P
    EPS = 1e-6
    assert HK * HD == F and QH == ST == 4

    SN = HQ * ST
    EXP, TURN, WEIGH = 1, 6, 7
    tasks = {}
    for kv in range(HK):
        for i in range(ST):
            if kv + 1 < HK:
                tasks[16 * kv + 1 + 2 * i] = ("q", (kv + 1, i), "dve")
                tasks[16 * kv + 12 + i] = ("qT", (kv + 1, i), "act")
            tasks[16 * kv + 24 + i if kv + 1 < HK else SN + WEIGH + i] = ("o", (kv, i), "dve")
    ahead = {SN - ST + k: ("hT", k, "act") for k in range(FT)} | {SN + i: ("k", i, "dve") for i in range(ST)}
    SLOTS = SN + WEIGH + ST
    SQUARE = SN - 4 * ST
    assert FT == ST and not tasks.keys() & ahead.keys()

    class Plan:

        def __init__(self, uses, tasks):
            self.uses, self.tasks = uses, tasks
            self.number = {(what, key): n for n, (what, key, _) in enumerate(uses)}
            self.emptied = {who: [sum(w == who for _, _, w in uses[:n]) for n in range(len(uses) + 1)] for who in ("act", "dve")}

        def count(self, what, key):
            n = self.number[what, key]
            return self.emptied[self.uses[n][2]][n + 1]

    begin = [("kT", h, "act") for h in range(HK)] + [("q", (0, i), "dve") for i in range(ST)]
    begin += [("v", i, "act") for i in range(ST)] + [("qT", (0, h), "act") for h in range(QH)]

    def plan_of(tasks):
        return Plan(begin + [tasks[s] for s in sorted(tasks)], tasks)

    first = Plan([ahead[s] for s in sorted(ahead)], {})
    inner = plan_of(tasks | ahead)
    final = plan_of(tasks)
    NPP = len(inner.uses)
    assert len(first.uses) % 2 == NPP % 2 == 0

    with ExitStack() as ctx:
        def sb(name, shape, dt=F32):
            return ctx.enter_context(nc.sbuf_tensor("p2_" + name, shape, dt))

        def sig(name, per=0, primed=False, base=0):
            return Signal(ctx.enter_context(nc.semaphore("p2_" + name)), per, primed, base)

        BF = mybir.dt.bfloat16
        q_w = sb("q_w", [P, FT, HQ * HD])
        k_w = sb("k_w", [P, FT, HK * HD])
        v_w = sb("v_w", [P, FT, HK * HD])
        o_w = sb("o_w", [P, HQ, F])
        norm_col = sb("norm_col", [P, FT])
        qn_row = sb("qn_row", [P, HD])
        kn_row = sb("kn_row", [P, HD])
        same = {c: sb(f"same_{c}", [P, ST, HD]) for c in "qk"}
        other = {c: sb(f"other_{c}", [P, ST, HD]) for c in "qk"}
        ident = sb("ident2", [P, P])
        ident_b = sb("ident_b", [P, P], BF)
        mask_b = sb("mask_b", [P, P], BF)
        mhalf = sb("mhalf2", [P, ST * QH])
        hid = sb("hid", [P, ST, F])
        hn = sb("hn", [P, ST, F])
        hT = sb("hT", [P, FT, S])
        v = sb("v2", [P, ST, HK * HD])
        kT = sb("kT2", [P, HK, S])
        square = sb("square", [P, 2, QH, HD])
        part = sb("part", [P, 2, QH, HD])
        cross = sb("cross", [P, 2, QH, HD])
        roped = sb("roped", [P, ST, QH, HD])
        qT = sb("qT2", [P, 2, QH, S])
        prob = sb("prob2", [P, 2, ST, S])
        cosf = prob[:, 0, :, 0:HD]
        sinf = prob[:, 0, :, HD:2 * HD]
        mask = prob[:, 1, 0, 0:HD]
        probT = sb("probT2", [P, ST, S])
        aT = sb("aT", [P, 8, S])
        ss = sb("ss", [P, ST])
        ssv = sb("ssv", [P, ST])
        hr = sb("hr", [P, ST])
        hsum = sb("hsum", [P, 3, ST, QH])
        heps = sb("heps", [P, 3, ST, QH])
        hinv = sb("hinv", [P, 3, ST, QH])
        nmax = sb("nmax2", [P, 2, ST])
        nbias = sb("nbias", [P, 2, ST])
        rsum = sb("rsum2", [P, 2, ST])
        rinv = sb("rinv2", [P, 2, ST])

        pp = [ctx.enter_context(nc.psum_tensor(f"p2_pp{i}", [P, 512], F32)) for i in range(2)]
        ps_s = [ctx.enter_context(nc.psum_tensor(f"p2_ps_s{i}", [P, 512], F32)) for i in range(3)]
        ps_t = [ctx.enter_context(nc.psum_tensor(f"p2_ps_t{i}", [P, 512], F32)) for i in range(2)]
        ps_o = [ctx.enter_context(nc.psum_tensor(f"p2_ps_o{i}", [P, 512], F32)) for i in range(1)]

        NG = HK + 1
        weights_in = {w: sig(f"weights_in_{w}") for w in "tkvqo"}
        consts_ready = sig("consts_ready2")
        tables_ready = sig("tables_ready")
        x2_in = sig("x2_in", 16)
        hn_in = sig("hn_in", 16, base=16)
        squared = sig("squared", ST, base=ST)
        eps_added = sig("eps_added", 1, base=1)
        hr_ready = sig("hr_ready", 1, base=1)
        hn_ready = sig("hn_ready", ST, base=ST)
        pp_ready = sig("pp_ready2", NPP, base=len(first.uses))
        pp_free = {who: sig(f"pp_free_{who}2", inner.emptied[who][-1], base=first.emptied[who][-1]) for who in ("act", "dve")}
        sq_ready = sig("sq_ready", ST * NG, base=ST)
        sum_ready = sig("sum_ready", ST * NG, base=ST)
        part_ready = sig("part_ready", 3 * ST * NG, base=3 * ST)
        hsum_ready = sig("hsum_ready", NG, base=1)
        hinv_ready = sig("hinv_ready", NG, base=1)
        roped_ready = sig("roped_ready", ST * NG, base=ST)
        k_normed = sig("k_normed", ST, base=ST)
        scores_ready = sig("scores_ready2", SN)
        max_ready = sig("max_ready2", SN)
        nbias_ready = sig("nbias_ready", SN)
        exp_ready = sig("exp_ready2", SN, primed=True)
        rinv_ready = sig("rinv_ready2", HQ)
        normed = sig("normed2", SN)
        turned = sig("turned2", SN)
        probT_ready = sig("probT_ready2", SN, primed=True)
        weighed = sig("weighed2", SN, primed=True)
        aT_ready = sig("aT_ready", HQ, primed=True)
        hidden_stored = sig("hidden_stored", 16, primed=True)
        QM = ST * HK

        def run_batches(engine, batch):
            with engine.Fori(0, B - 1) as b:
                batch(b, inner)
            batch(B - 1, final)

        def settled(engine):
            engine.wait_ge(consts_ready.sem, 1)

        block = ctx.enter_context(nc.Block())

        @block.sync
        def _(sp):
            hidden_stored.prime(sp)
            def load(w, dst, src):
                weights_in[w].inc(sp.dma_start(dst, src), 16)

            def rows(name):
                return io[name].rearrange("(t p) n -> p t n", p=P)

            def load_hn(b):
                hn_in.inc(sp.dma_start(hn[:], x2_dram[b].rearrange("o (t p) f -> p (o t) f", p=P)), 16)

            load_hn(slice(0, 1))
            load("t", norm_col[:], io["attn_norm"])
            load("t", ident[:], io["ident"])
            load("t", cosf, rows("cos"))
            load("t", sinf, rows("sin"))
            load("t", qn_row[:], io["q_norm"].to_broadcast([P, HD]))
            load("t", kn_row[:], io["k_norm"].to_broadcast([P, HD]))
            load("t", mask, io["mask"])
            load("k", k_w[:], rows("k_wT"))
            for g in range(HK):
                load("q", q_w[:, :, 512 * g:512 * (g + 1)], rows("q_wT")[:, :, 512 * g:512 * (g + 1)])
                if g == 0:
                    load("v", v_w[:], rows("v_wT"))
            load("o", o_w[:], rows("o_wT"))

            def batch(b, plan):
                this = bass.ds(b, 1)
                hidden_stored.wait(sp, b, 0)
                settled(sp)
                x2_in.inc(sp.dma_start(hid[:], x2_dram[this].rearrange("o (t p) f -> p (o t) f", p=P)), 16)
                if plan is inner:
                    pp_ready.wait(sp, b, 0)
                    settled(sp)
                    load_hn(bass.ds(b + 1, 1))
                pp_free["dve"].wait(sp, b, plan.emptied["dve"][-1])
                settled(sp)
                hidden_stored.inc(sp.dma_start(hidden_dram[this].rearrange("o (t p) f -> p (o t) f", p=P), hid[:]), 16)

            run_batches(sp, batch)
            hidden_stored.wait_all(sp, 16 * B)

        @block.tensor
        def _(pe):
            weighed.prime(pe)

            def take(b, plan, what, key):
                n = plan.number[what, key]
                if n >= 2:
                    who = plan.uses[n - 2][2]
                    pp_free[who].wait(pe, b, plan.emptied[who][n - 1])
                elif b is not None:
                    for who in ("act", "dve"):
                        pp_free[who].wait(pe, b, 0)
                return pp[n % 2]

            def project(b, plan, what, key, i, w, c0):
                bank = take(b, plan, what, key)
                for k in range(FT):
                    mm = pe.matmul(bank[:, :], hT[:, k, i * P:(i + 1) * P], w[:, k, c0:c0 + 512],
                                   start=(k == 0), stop=(k == FT - 1))
                pp_ready.inc(mm)

            def turn_roped(b, plan, what, key, h):
                bank = take(b, plan, what, key)
                for i in range(ST):
                    mm = pe.transpose(bank[:, i * P:(i + 1) * P], roped[:, i, h, :], ident[:, :])
                pp_ready.inc(mm)

            def task(b, plan, what, key):
                if what == "hT":
                    if key == 0:
                        hn_ready.wait(pe, b, ST)
                    bank = take(b, plan, what, key)
                    for i in range(ST):
                        mm = pe.transpose(bank[:, i * P:(i + 1) * P], hn[:, i, key * P:(key + 1) * P], ident[:, :])
                    pp_ready.inc(mm)
                elif what == "k":
                    if key == 0:
                        pp_free["act"].wait(pe, b, plan.count("hT", FT - 1))
                    project(b, plan, what, key, key, k_w, 0)
                elif what == "q":
                    project(b, plan, what, key, key[1], q_w, 512 * key[0])
                elif what == "qT":
                    roped_ready.wait(pe, b, ST * (key[0] + 1))
                    turn_roped(b, plan, what, key, key[1])
                else:
                    kv, i = key
                    aT_ready.wait(pe, b, QH * (kv + 1))
                    bank = take(b, plan, what, key)
                    for hh in range(QH):
                        h = QH * kv + hh
                        mm = pe.matmul(bank[:, :], aT[:, h % 8, i * P:(i + 1) * P], o_w[:, h, :],
                                       start=(hh == 0), stop=(hh == QH - 1))
                    pp_ready.inc(mm)

            def batch(b, plan):
                k_normed.wait(pe, b, 0)
                for h in range(HK):
                    turn_roped(b, plan, "kT", h, h)
                for i in range(ST):
                    task(b, plan, "q", (0, i))
                for i in range(ST):
                    project(b, plan, "v", i, i, v_w, 0)
                for h in range(QH):
                    task(b, plan, "qT", (0, h))

                def score(g, i):
                    kv, hh = divmod(g, QH)
                    n = ST * g + i
                    exp_ready.wait(pe, b, max(n - 2, 0))
                    if i == 0:
                        pp_free["act"].wait(pe, b, plan.count("qT", (kv, hh)))
                    bank = ps_s[n % 3]
                    pe.matmul(bank[:, 0:(i + 1) * P], qT[:, kv % 2, hh, i * P:(i + 1) * P], kT[:, kv, 0:(i + 1) * P],
                              start=True, stop=False)
                    scores_ready.inc(pe.matmul(bank[:, i * P:(i + 1) * P], ident_b[:, :], mask_b[:, :], start=False, stop=True))

                def turn(g, j):
                    n = ST * g + j
                    probT_ready.wait(pe, b, max(n - 1, 0))
                    if j == 0:
                        normed.wait(pe, b, ST * (g + 1))
                    for i in range(j, ST):
                        mm = pe.transpose(ps_t[n % 2][:, i * P:(i + 1) * P], prob[:, g % 2, i, j * P:(j + 1) * P], ident[:, :])
                    turned.inc(mm)

                def weigh(g, j):
                    kv = g // QH
                    if j == 0:
                        aT_ready.wait(pe, b, g)
                    probT_ready.wait(pe, b, ST * g + j + 1)
                    weighed.inc(pe.matmul(ps_o[0][:, j * P:], v[:, j, kv * HD:(kv + 1) * HD], probT[:, j, j * P:],
                                          start=(j == 0), stop=(j == ST - 1)))

                for s in range(SLOTS):
                    if s < SN:
                        score(*divmod(s, ST))
                    if TURN <= s < SN + TURN:
                        turn(*divmod(s - TURN, ST))
                    if WEIGH <= s < SN + WEIGH:
                        weigh(*divmod(s - WEIGH, ST))
                    if s in plan.tasks:
                        task(b, plan, *plan.tasks[s][:2])

            pe.wait_ge(weights_in["t"].sem, weights_in["t"].n)
            for what, key, _ in first.uses:
                if what == "k" and key == 0:
                    pe.wait_ge(weights_in["k"].sem, weights_in["k"].n)
                task(None, first, what, key)
            for w in "qvo":
                pe.wait_ge(weights_in[w].sem, weights_in[w].n)
            run_batches(pe, batch)

        @block.scalar
        def _(act):
            exp_ready.prime(act)
            probT_ready.prime(act)
            aT_ready.prime(act)

            def square_rows(b, i):
                if i == 0:
                    hn_in.wait(act, b, 16)
                    if b is not None:
                        sum_ready.wait(act, b, QM)
                else:
                    squared.wait(act, b, i)
                squared.inc(act.activation(square[:, i % 2].rearrange("p h d -> p (h d)"), hn[:, i, :], ACT.Square,
                                           accum_out=ss[:, i:i + 1]))

            def empties(b, plan, what, key, dst, **kw):
                n = plan.number[what, key]
                pp_ready.wait(act, b, n + 1)
                pp_free["act"].inc(act.activation(dst, pp[n % 2][:, :], **kw))

            def square_heads(b, plan, what, key, m):
                n = plan.number[what, key]
                pp_ready.wait(act, b, n + 1)
                if what == "k" and key == 0:
                    squared.wait(act, b, ST)
                if b is not None or m >= 2:
                    sum_ready.wait(act, b, m - 1)
                sq_ready.inc(act.activation(square[:, m % 2].rearrange("p h d -> p (h d)"), pp[n % 2][:, :], ACT.Square))

            def task(b, plan, what, key):
                if what == "hT":
                    empties(b, plan, what, key, hT[:, key, :], func=ACT.Copy, scale=norm_col[:, key:key + 1])
                elif what == "k":
                    square_heads(b, plan, what, key, key if b is None else QM + key)
                elif what == "q":
                    square_heads(b, plan, what, key, ST * key[0] + key[1])
                elif what == "qT":
                    empties(b, plan, what, key, qT[:, key[0] % 2, key[1], :], func=ACT.Copy)

            def batch(b, plan):
                for h in range(HK):
                    empties(b, plan, "kT", h, kT[:, h, :], func=ACT.Copy)
                for i in range(ST):
                    task(b, plan, "q", (0, i))
                for i in range(ST):
                    empties(b, plan, "v", i, v[:, i, :], func=ACT.Copy)
                for h in range(QH):
                    task(b, plan, "qT", (0, h))

                def exp_scores(g, i):
                    n = ST * g + i
                    kv, hh = divmod(g, QH)
                    nbias_ready.wait(act, b, n + 1)
                    exp_ready.inc(act.activation(prob[:, g % 2, i, 0:(i + 1) * P], ps_s[n % 3][:, 0:(i + 1) * P], ACT.Exp,
                                                 bias=nbias[:, g % 2, i:i + 1], scale=hinv[:, kv % 2, i, hh:hh + 1],
                                                 accum_out=rsum[:, g % 2, i:i + 1]))

                def copy_turned(g, j):
                    n = ST * g + j
                    turned.wait(act, b, n + 1)
                    weighed.wait(act, b, max(n - ST + 1, 0))
                    probT_ready.inc(act.activation(probT[:, j, j * P:], ps_t[n % 2][:, j * P:], ACT.Copy))

                for s in range(SLOTS):
                    g, i = divmod(s - WEIGH - ST, ST)
                    if i == 0 and 0 <= g < HQ:
                        weighed.wait(act, b, ST * (g + 1))
                        aT_ready.inc(act.activation(aT[:, g % 8, :], ps_o[0][:, :], ACT.Copy))
                    if TURN <= s < SN + TURN:
                        copy_turned(*divmod(s - TURN, ST))
                    if EXP <= s < SN + EXP:
                        exp_scores(*divmod(s - EXP, ST))
                    if plan is inner and SQUARE <= s < SQUARE + ST:
                        square_rows(b, s - SQUARE)
                    if s in plan.tasks:
                        task(b, plan, *plan.tasks[s][:2])

            act.wait_ge(weights_in["t"].sem, weights_in["t"].n)
            for i in range(ST):
                square_rows(None, i)
            for what, key, _ in first.uses:
                task(None, first, what, key)
            run_batches(act, batch)

        @block.vector
        def _(dve):
            consts_ready.inc(dve.memset(mhalf[:], -0.5))
            dve.wait_ge(weights_in["t"].sem, weights_in["t"].n)
            H2 = HD // 2
            for c, row in (("q", qn_row), ("k", kn_row)):
                def weight(a, z):
                    return row[:, a:z].rearrange("p (o d) -> p o d", o=1).to_broadcast([P, ST, z - a])
                tables_ready.inc(dve.tensor_tensor(same[c][:], cosf, weight(0, HD), ALU.mult))
                tables_ready.inc(dve.tensor_tensor(other[c][:, :, 0:H2], sinf[:, :, 0:H2], weight(H2, HD), ALU.mult))
                tables_ready.inc(dve.tensor_tensor(other[c][:, :, H2:], sinf[:, :, H2:], weight(0, H2), ALU.mult))
            tables_ready.inc(dve.tensor_copy(ident_b[:, :], ident[:, :]))
            tables_ready.inc(dve.tensor_copy(mask_b[:, :], mask))
            dve.wait_ge(tables_ready.sem, tables_ready.n)

            def sum_up(b):
                squared.wait(dve, b, ST)
                eps_added.inc(dve.tensor_scalar(ssv[:, :], ss[:, :], 1.0 / F, EPS, ALU.mult, ALU.add))

            def norm_rows(b):
                hr_ready.wait(dve, b, 1)
                for i in range(ST):
                    hn_ready.inc(dve.tensor_scalar(hn[:, i, :], hn[:, i, :], hr[:, i:i + 1], None, ALU.mult))

            def rope(b, plan, c, key, i, m, group, place):
                n = plan.number[c, key]
                bank = pp[n % 2][:, :].rearrange("p (h d) -> p h d", h=QH)

                def table(t, a, z):
                    return t[c][:, i:i + 1, a:z].to_broadcast([P, QH, z - a])

                sq_ready.wait(dve, b, m + 1)
                if b is not None or m >= 2:
                    roped_ready.wait(dve, b, m - 1)
                part_ready.inc(dve.tensor_tensor(cross[:, m % 2, :, 0:H2], bank[:, :, H2:], table(other, 0, H2), ALU.mult))
                part_ready.inc(dve.tensor_tensor(cross[:, m % 2, :, H2:], bank[:, :, 0:H2], table(other, H2, HD), ALU.mult))
                pp_free["dve"].inc(dve.tensor_tensor(part[:, m % 2], bank, table(same, 0, HD), ALU.mult))
                sum_ready.inc(dve.tensor_reduce(hsum[:, place, i, :], square[:, m % 2], AX.X, ALU.add))
                if i == ST - 1:
                    sum_ready.wait(dve, b, m + 1)
                    mul, add = (1.0 / HD, EPS) if c == "k" else (1.0, HD * EPS)
                    hsum_ready.inc(dve.tensor_scalar(heps[:, place], hsum[:, place], mul, add, ALU.mult, ALU.add))

            def norm_keys(b, m0, group):
                hinv_ready.wait(dve, b, group + 1)
                for i in range(ST):
                    roped_ready.wait(dve, b, m0 + i + 1)
                    k_normed.inc(dve.tensor_tensor(
                        roped[:, i], roped[:, i],
                        hinv[:, 2, i, :].rearrange("p (h o) -> p h o", o=1).to_broadcast([P, QH, HD]), ALU.mult))

            def rope_queries(b, plan, key):
                rope(b, plan, "q", key, key[1], ST * key[0] + key[1], key[0], key[0] % 2)

            def batch(b, plan):
                for i in range(ST):
                    rope_queries(b, plan, (0, i))

                def row_max(g, i):
                    n = ST * g + i
                    kv, hh = divmod(g, QH)
                    scores_ready.wait(dve, b, n + 1)
                    max_ready.inc(dve.tensor_reduce(nmax[:, g % 2, i:i + 1], ps_s[n % 3][:, 0:(i + 1) * P], AX.X, ALU.max, negate=True))
                    if i == 0 and hh == 0:
                        hinv_ready.wait(dve, b, kv + 1)
                    max_ready.wait(dve, b, n + 1)
                    nbias_ready.inc(dve.tensor_tensor(nbias[:, g % 2, i:i + 1], nmax[:, g % 2, i:i + 1],
                                                      hinv[:, kv % 2, i, hh:hh + 1], ALU.mult))

                def normalise(g):
                    exp_ready.wait(dve, b, ST * (g + 1))
                    rinv_ready.inc(dve.reciprocal(rinv[:, g % 2, :], rsum[:, g % 2, :]))
                    rinv_ready.wait(dve, b, g + 1)
                    for i in range(ST):
                        block_ = prob[:, g % 2, i, 0:(i + 1) * P]
                        normed.inc(dve.tensor_scalar(block_, block_, rinv[:, g % 2, i:i + 1], None, ALU.mult))

                def task(what, key):
                    if what == "o":
                        kv, i = key
                        n = plan.number[what, key]
                        pp_ready.wait(dve, b, n + 1)
                        if kv:
                            pp_free["dve"].wait(dve, b, plan.count(what, (kv - 1, i)))
                        else:
                            x2_in.wait(dve, b, 16)
                        pp_free["dve"].inc(dve.tensor_tensor(hid[:, i, :], hid[:, i, :], pp[n % 2][:, :], ALU.add))
                    elif what == "q":
                        rope_queries(b, plan, key)
                    elif what == "k":
                        rope(b, plan, "k", key, key, QM + key, HK, 2)

                for s in range(SLOTS):
                    if s < SN:
                        row_max(*divmod(s, ST))
                    if s % ST == EXP and ST <= s <= SN + EXP:
                        normalise(s // ST - 1)
                    if plan is inner and s == SQUARE + ST:
                        sum_up(b)
                    if plan is inner and s == SQUARE + ST + 2:
                        norm_rows(b)
                    if s in plan.tasks:
                        task(*plan.tasks[s][:2])
                    if plan is inner and s == SN + ST + 1:
                        norm_keys(b, QM, HK)

            sum_up(None)
            norm_rows(None)
            for i in range(ST):
                rope(None, first, "k", i, i, i, 0, 2)
            norm_keys(None, 0, 0)
            run_batches(dve, batch)

        @block.gpsimd
        def _(pool):
            pool.wait_ge(consts_ready.sem, 1)

            def invert_rows(b):
                eps_added.wait(pool, b, 1)
                hr_ready.inc(pool.tensor_tensor(hr[:, :], ssv[:, :], mhalf[:, 0:ST], ALU.pow))

            def add_parts(b, plan, what, key, i, m):
                pp_free["dve"].wait(pool, b, plan.count(what, key))
                roped_ready.inc(pool.tensor_tensor(roped[:, i], part[:, m % 2], cross[:, m % 2], ALU.add))

            def invert_heads(b, group, place):
                hsum_ready.wait(pool, b, group + 1)
                hinv_ready.inc(pool.tensor_tensor(hinv[:, place].rearrange("p t h -> p (t h)"),
                                                  heps[:, place].rearrange("p t h -> p (t h)"), mhalf[:, :], ALU.pow))

            def batch(b, plan):
                for kv in range(HK):
                    pp_ready.wait(pool, b, plan.number[("qT", (kv - 1, QH - 1)) if kv else ("kT", HK - 1)] + 1)
                    for i in range(ST):
                        add_parts(b, plan, "q", (kv, i), i, ST * kv + i)
                    invert_heads(b, kv, kv % 2)
                if plan is inner:
                    invert_rows(b)
                    pp_ready.wait(pool, b, plan.number["qT", (HK - 1, QH - 1)] + 1)
                    for i in range(ST):
                        add_parts(b, plan, "k", i, i, QM + i)
                    invert_heads(b, HK, 2)

            invert_rows(None)
            for i in range(ST):
                add_parts(None, first, "k", i, i, i)
            invert_heads(None, 0, 2)
            run_batches(pool, batch)


def mixture_of_experts(nc, io, x2_dram, hidden_dram, out):
    B, S, F = io["x"].shape
    E = io["gate_wT"].shape[1]
    I = io["wgT"].shape[2]
    FT, ST = F // P, S // P
    NT = B * ST
    J = 2 * NT
    NP = -(-(J * P + E * (P - 1)) // P)
    NP += NP % 2
    IT = -(-I // P)
    IL = I - (IT - 1) * P
    EPS = 1e-6
    RING = 8
    U32 = mybir.dt.uint32
    assert E == 8 and I <= 512 and NP <= P

    hn_dram = nc.dram_tensor("hn_rows", (B * S, F), F32, kind="Internal").ap()
    y_dram = nc.dram_tensor("expert_rows", (NP * P, F), F32, kind="Internal").ap()

    with ExitStack() as ctx:
        def sb(name, shape, dt=F32):
            return ctx.enter_context(nc.sbuf_tensor("p3_" + name, shape, dt))

        def sig(name, per=0, primed=False):
            return Signal(ctx.enter_context(nc.semaphore("p3_" + name)), per, primed)

        gate_w = sb("gate_w", [P, FT, E])
        norm_col = sb("norm_col3", [P, FT])
        ident = sb("ident3", [P, P])
        before = sb("before", [P, P])
        ones = sb("ones", [P, P])
        expert_no = sb("expert_no", [P, E])
        place_no = sb("place_no", [P, P])
        token_no = sb("token_no", [P, J])
        new_expert = sb("new_expert", [P, E * J])
        mhalf = sb("mhalf3", [P, NT])
        wg = sb("wg_sb", [P, E * FT * I])
        wu = sb("wu_sb", [P, E * FT * I])
        wd = sb("wd_sb", [P, E * IT * F])
        hbuf = sb("hbuf3", [P, 2, ST, F])
        acc = sb("acc", [P, NT, F])
        hT = sb("hT3", [P, FT, S])
        ss = sb("ss3", [P, NT])
        ssv = sb("ssv3", [P, NT])
        hr = sb("hr3", [P, NT])
        logits = sb("logits", [P, NT, E])
        shifted = sb("shifted", [P, NT, E])
        top = sb("top", [P, NT, 8])
        topi = sb("topi", [P, NT, 8], U32)
        topf = sb("topf", [P, 2, NT])
        small = sb("small", [P, 8, NT])
        chosen = sb("chosen", [P, E, J])
        upto = sb("upto", [P, E, J])
        per_expert = sb("per_expert", [P, 4, E])
        begun = sb("begun", [P, E, NT])
        pos = sb("pos", [P, J])
        pos_u = sb("pos_u", [P, J], U32)
        pos_hi = sb("pos_hi", [P, J], U32)
        pos_lo = sb("pos_lo", [P, J], U32)
        tile_of = sb("tile_of", [P, J])
        row_of = sb("row_of", [P, J])
        ended = sb("ended", [1, NP, E])
        expert_f = sb("expert_f", [1, NP])
        expert_of = sb("expert_of", [1, NP], U32)
        token_of = sb("token_of", [P, NP], U32)
        rows_of = [sb(f"rows_of{i}", [P, 1], U32) for i in range(2)]
        square = sb("square3", [P, F])
        stats = sb("stats3", [P, ST, 6])
        mv = sb("mv3", [P, NT, 2])
        veps = sb("veps3", [P, NT])
        rstd = sb("rstd3", [P, NT])
        spare = {"hbuf": hbuf[:].rearrange("p a t f -> p (a t f)"), "hT": hT[:].rearrange("p k s -> p (k s)")}

        def carved(name, n, width):
            got, spare[name] = spare[name][:, 0:n * width], spare[name][:, n * width:]
            return got.rearrange("p (n w) -> p n w", w=width)

        row_hot = spare["hbuf"][:, 0:J * P].rearrange("p (j r) -> p j r", r=P)
        tile_hot = spare["hT"][:, 0:J * NP].rearrange("p (j t) -> p j t", t=NP)
        xg = carved("hbuf", 2, F)
        xT = carved("hbuf", 2, F)
        y_row = carved("hbuf", 2, F)
        silu = carved("hbuf", 2, I)
        act_row = carved("hT", 2, I)
        actT = carved("hT", 2, IT * P)
        results = hbuf[:].rearrange("p a t f -> p (a t) f")
        assert 2 * ST == RING and J * P <= 2 * ST * F and J * NP <= FT * S

        ps_g = [ctx.enter_context(nc.psum_tensor(f"p3_ps_g{i}", [P, 512], F32)) for i in range(2)]
        ps_u = [ctx.enter_context(nc.psum_tensor(f"p3_ps_u{i}", [P, 512], F32)) for i in range(2)]
        ps_x = ctx.enter_context(nc.psum_tensor("p3_ps_x", [P, 512], F32))
        ps_a = ctx.enter_context(nc.psum_tensor("p3_ps_a", [P, 512], F32))
        ps_d = [ctx.enter_context(nc.psum_tensor(f"p3_ps_d{i}", [P, 512], F32)) for i in range(2)]

        small_in = sig("small_in")
        weights_in = sig("weights_in3")
        hidden_in = [sig(f"hidden_in{i}") for i in range(2)]
        acc_in = [sig(f"acc_in{c}") for c in range(B)]
        hn_stored = [sig(f"hn_stored{i}") for i in range(2)]
        consts_ready = sig("consts_ready3")
        squared = sig("squared3")
        eps_added = sig("eps_added3")
        hr_ready = sig("hr_ready3")
        acc_begun = sig("acc_begun")
        hn_ready = sig("hn_ready3")
        turned_in = sig("turned_in")
        hT_ready = sig("hT_ready")
        logits_made = sig("logits_made")
        logits_ready = sig("logits_ready")
        exp_ready = sig("exp_ready3")
        route = sig("route")
        chosen_ready = sig("chosen_ready")
        counted = sig("counted")
        hots_ready = sig("hots_ready")
        placed = sig("placed")
        table_ready = sig("table_ready")
        rows_copied = sig("rows_copied", 2)
        rows_seen = sig("rows_seen", 2)
        gathered = [sig(f"gathered{i}", 16) for i in range(2)]
        x_turned = sig("x_turned", 2)
        xT_ready = sig("xT_ready3", 2)
        gate_made = sig("gate_made", 2)
        up_made = sig("up_made", 2)
        silu_ready = sig("silu_ready", 2)
        row_ready = sig("row_ready", 2)
        act_turned = sig("act_turned", 2)
        actT_ready = sig("actT_ready", 4)
        down_made = sig("down_made", 2)
        y_ready = sig("y_ready", 2)
        y_stored = [sig(f"y_stored{i}", 16) for i in range(2)]
        result_in = [sig(f"result_in{i}") for i in range(RING)]
        added = sig("added3")
        ln_step = sig("ln_step3")
        rstd_ready = sig("rstd_ready3")
        out_ready = sig("out_ready")
        out_stored = sig("out_stored")

        def tile_done(engine, signal, turn, k):
            value = (k + 1) * signal.per // 2
            if isinstance(turn, int) and turn * signal.per + value <= 0:
                return
            engine.wait_ge(signal.sem, turn * signal.per + value)

        def ring_done(engine, signals, turn, k):
            value = (k // 2 + 1) * 16
            if isinstance(turn, int) and turn * 16 + value <= 0:
                return
            engine.wait_ge(signals[k % 2].sem, turn * 16 + value)

        def run_tiles(engine, turn):
            turn(0, True, False)
            with engine.Fori(1, NP // 2 - 1) as ee:
                turn(ee, False, False)
            turn(NP // 2 - 1, False, True)

        def at(turn, k, width=1):
            if isinstance(turn, int):
                return slice((2 * turn + k) * width, (2 * turn + k + 1) * width)
            return bass.ds(turn * (2 * width) + k * width, width)

        block = ctx.enter_context(nc.Block())

        @block.sync
        def _(sp):
            for dst, src in ((gate_w[:], io["gate_wT"].rearrange("(t p) e -> p t e", p=P)), (norm_col[:], io["ffn_norm"]),
                             (ident[:], io["ident"]), (before[:], io["before"]), (token_no[:], io["token_no"]),
                             (expert_no[:], io["place_no"][:, 0:E].to_broadcast([P, E])),
                             (place_no[:], io["place_no"].to_broadcast([P, P])),
                             (new_expert[:], io["new_expert"].to_broadcast([P, E * J]))):
                small_in.inc(sp.dma_start(dst, src), 16)

            def load_hidden(c):
                if c >= 2:
                    sp.wait_ge(turned_in.sem, FT * (c - 1))
                    sp.wait_ge(hn_stored[c % 2].sem, 16 * (c // 2))
                hidden_in[c % 2].inc(sp.dma_start(hbuf[:, c % 2], hidden_dram[c].rearrange("(t p) f -> p t f", p=P)), 16)

            def load_x2(c):
                acc_in[c].inc(sp.dma_start(acc[:, ST * c:ST * (c + 1), :], x2_dram[c].rearrange("(t p) f -> p t f", p=P)), 16)

            def load_in(w, name, e):
                weights_in.inc(sp.dma_start(w[:, e * FT * I:(e + 1) * FT * I].rearrange("p (t i) -> p t i", i=I),
                                            io[name][e].rearrange("(t p) i -> p t i", p=P)), 16)

            load_hidden(0)
            load_hidden(1)
            load_x2(0)
            load_x2(1)
            for c in range(2, B):
                load_hidden(c)
                load_x2(c)
                for e in range(E * (c - 2) // (B - 2), E * (c - 1) // (B - 2)):
                    load_in(wg, "wgT", e)
            for e in range(E):
                load_in(wu, "wuT", e)
            for e in range(E):
                wd_e = wd[:, e * IT * F:(e + 1) * IT * F].rearrange("p (t f) -> p t f", f=F)
                weights_in.inc(sp.dma_start(wd_e[:, 0:IT - 1], io["wdT"][e, 0:(IT - 1) * P].rearrange("(t p) f -> p t f", p=P)), 16)
                weights_in.inc(sp.dma_start(wd_e[0:IL, IT - 1], io["wdT"][e, (IT - 1) * P:]), 16)

            def turn(ee, first, last):
                for q in range(2):
                    tile_done(sp, y_ready, ee, q)
                    sp.dma_start(y_dram[at(ee, q, P)], y_row[:, q, :]).then_inc(y_stored[q].sem, 16)

            run_tiles(sp, turn)
            for c in range(B):
                sp.wait_ge(out_ready.sem, ST * (c + 1))
                out_stored.inc(sp.dma_start(out[c].rearrange("(t p) f -> p t f", p=P), acc[:, ST * c:ST * (c + 1), :]), 16)
            sp.wait_ge(out_stored.sem, out_stored.n)

        @block.tensor
        def _(pe):
            pe.wait_ge(small_in.sem, small_in.n)
            for c in range(B):
                pe.wait_ge(hn_ready.sem, ST * (c + 1))
                for k in range(FT):
                    n = FT * c + k
                    if n >= 2:
                        pe.wait_ge(hT_ready.sem, n - 1)
                    for i in range(ST):
                        mm = pe.transpose(ps_d[n % 2][:, i * P:(i + 1) * P], hbuf[:, c % 2, i, k * P:(k + 1) * P], ident[:, :])
                    turned_in.inc(mm)
                pe.wait_ge(hT_ready.sem, FT * (c + 1))
                for i in range(ST):
                    t = ST * c + i
                    for k in range(FT):
                        mm = pe.matmul(ps_g[0][:, t * E:(t + 1) * E], hT[:, k, i * P:(i + 1) * P], gate_w[:, k, :],
                                       start=(k == 0), stop=(k == FT - 1))
                logits_made.inc(mm)
            pe.wait_ge(chosen_ready.sem, 1)
            flat = chosen[:].rearrange("p e j -> p (e j)")
            pe.matmul(ps_u[0][:, 0:E * J], before[:, :], flat, start=True, stop=True)
            counted.inc(pe.matmul(ps_u[1][:, 0:E * J], ones[:, :], flat, start=True, stop=True))
            for j in range(J):
                if j % NT == 0:
                    pe.wait_ge(hots_ready.sem, 2 + j // NT)
                mm = pe.matmul(ps_d[0][:, 0:NP], row_hot[:, j, :], tile_hot[:, j, :], start=(j == 0), stop=(j == J - 1))
            placed.inc(mm)
            pe.wait_ge(weights_in.sem, weights_in.n)
            pe.wait_ge(table_ready.sem, 2)

            def expert(ee, k):
                return pe.value_load(expert_of[0:1, at(ee, k)], min_val=0, max_val=E - 1)

            def turn_x(ee, k):
                ring_done(pe, gathered, ee, k)
                tile_done(pe, xT_ready, ee, k - 1)
                for j in range(FT):
                    mm = pe.transpose(ps_x[:, j * P:(j + 1) * P], xg[:, k % 2, j * P:(j + 1) * P], ident[:, :])
                mm.then_inc(x_turned.sem, 1)

            def project(bank, w, e, q):
                for j in range(FT):
                    mm = pe.matmul(bank[:, 0:I], xT[:, q, j * P:(j + 1) * P], w[:, bass.ds(e * (FT * I) + j * I, I)],
                                   start=(j == 0), stop=(j == FT - 1))
                return mm

            def turn_act(ee, k):
                tile_done(pe, row_ready, ee, k)
                tile_done(pe, actT_ready, ee, k - 1)
                for j in range(IT):
                    w = P if j < IT - 1 else IL
                    mm = pe.transpose(ps_a[0:w, j * P:(j + 1) * P], act_row[:, k % 2, j * P:j * P + w], ident[:, :])
                mm.then_inc(act_turned.sem, 1)

            def down(ee, k, e):
                tile_done(pe, actT_ready, ee, k)
                tile_done(pe, y_ready, ee, k - 2)
                for j in range(IT):
                    w = P if j < IT - 1 else IL
                    mm = pe.matmul(ps_d[k % 2][:, :], actT[0:w, k % 2, j * P:(j + 1) * P], wd[0:w, bass.ds(e * (IT * F) + j * F, F)],
                                   start=(j == 0), stop=(j == IT - 1))
                mm.then_inc(down_made.sem, 1)

            def turn(ee, first, last):
                for q in range(2):
                    e = expert(ee, q)
                    e_last = None if first and q == 0 else expert(ee, q - 1)
                    tile_done(pe, xT_ready, ee, q)
                    tile_done(pe, silu_ready, ee, q - 2)
                    project(ps_g[q], wg, e, q).then_inc(gate_made.sem, 1)
                    if e_last is not None:
                        turn_act(ee, q - 1)
                    if not (last and q == 1):
                        turn_x(ee, q + 1)
                    tile_done(pe, row_ready, ee, q - 2)
                    project(ps_u[q], wu, e, q).then_inc(up_made.sem, 1)
                    if e_last is not None:
                        down(ee, q - 1, e_last)
                if last:
                    turn_act(ee, 1)
                    down(ee, 1, e)

            turn_x(0, 0)
            run_tiles(pe, turn)

        @block.scalar
        def _(act):
            act.wait_ge(small_in.sem, small_in.n)
            for c in range(B):
                act.wait_ge(hidden_in[c % 2].sem, 16 * (c // 2 + 1))
                for i in range(ST):
                    if i:
                        act.wait_ge(squared.sem, squared.n)
                    squared.inc(act.activation(square[:, :], hbuf[:, c % 2, i, :], ACT.Square, accum_out=ss[:, ST * c + i:ST * c + i + 1]))
                act.wait_ge(squared.sem, squared.n)
                act.wait_ge(hn_ready.sem, ST * (c + 1))
                hn_stored[c % 2].inc(act.dma_start(hn_dram[S * c:S * (c + 1)].rearrange("(t p) f -> p t f", p=P), hbuf[:, c % 2]), 16)
                if c:
                    act.wait_ge(logits_made.sem, c)
                for k in range(FT):
                    n = FT * c + k
                    act.wait_ge(turned_in.sem, n + 1)
                    hT_ready.inc(act.activation(hT[:, k, :], ps_d[n % 2][:, :], ACT.Copy, scale=norm_col[:, k:k + 1]))
            act.wait_ge(route.sem, 1)
            exp_ready.inc(act.activation(small[:, 1, :], small[:, 0, :], ACT.Exp))
            exp_ready.inc(act.activation(shifted[:], shifted[:], ACT.Exp))

            def keep_y(ee, k):
                tile_done(act, down_made, ee, k)
                ring_done(act, y_stored, ee, k - 2)
                act.activation(y_row[:, k % 2, :], ps_d[k % 2][:, :], ACT.Copy).then_inc(y_ready.sem, 1)

            def keep_actT(ee, k):
                q = k % 2
                tile_done(act, act_turned, ee, k)
                tile_done(act, down_made, ee, k - 2)
                act.activation(actT[:, q, 0:(IT - 1) * P], ps_a[:, 0:(IT - 1) * P], ACT.Copy).then_inc(actT_ready.sem, 1)
                act.activation(actT[0:IL, q, (IT - 1) * P:], ps_a[0:IL, (IT - 1) * P:IT * P], ACT.Copy).then_inc(actT_ready.sem, 1)

            def turn(ee, first, last):
                for q in range(2):
                    if not first:
                        keep_y(ee, q - 2)
                    tile_done(act, gate_made, ee, q)
                    tile_done(act, row_ready, ee, q - 2)
                    act.activation(silu[:, q, :], ps_g[q][:, 0:I], ACT.Silu).then_inc(silu_ready.sem, 1)
                    if not (first and q == 0):
                        keep_actT(ee, q - 1)
                if last:
                    keep_y(ee, 0)
                    keep_actT(ee, 1)
                    keep_y(ee, 1)

            run_tiles(act, turn)

        @block.vector
        def _(dve):
            consts_ready.inc(dve.memset(mhalf[:], -0.5))
            consts_ready.inc(dve.memset(ones[:], 1.0))
            dve.wait_ge(small_in.sem, small_in.n)

            def step(signal, instruction):
                signal.inc(instruction)
                dve.wait_ge(signal.sem, signal.n)

            for c in range(B):
                own = slice(ST * c, ST * (c + 1))
                dve.wait_ge(squared.sem, ST * (c + 1))
                eps_added.inc(dve.tensor_scalar(ssv[:, own], ss[:, own], 1.0 / F, EPS, ALU.mult, ALU.add))
                dve.wait_ge(acc_in[c].sem, 16)
                acc_begun.inc(dve.tensor_tensor(acc[:, own, :], acc[:, own, :], hbuf[:, c % 2], ALU.add))
                dve.wait_ge(acc_begun.sem, c + 1)
                dve.wait_ge(hr_ready.sem, c + 1)
                for i in range(ST):
                    hn_ready.inc(dve.tensor_scalar(hbuf[:, c % 2, i, :], hbuf[:, c % 2, i, :], hr[:, ST * c + i:ST * c + i + 1], None, ALU.mult))
            dve.wait_ge(logits_made.sem, B)
            step(logits_ready, dve.tensor_copy(logits[:].rearrange("p t e -> p (t e)"), ps_g[0][:, 0:NT * E]))
            for t in range(NT):
                logits_ready.inc(dve.max(top[:, t, :], logits[:, t, :]))
            dve.wait_ge(logits_ready.sem, 1 + NT)
            for t in range(NT):
                logits_ready.inc(dve.max_index(topi[:, t, :], top[:, t, :], logits[:, t, :]))
            dve.wait_ge(logits_ready.sem, 1 + 2 * NT)

            def wide(ap, n):
                return ap.rearrange("p (t o) -> p t o", o=1).to_broadcast([ap.shape[0], ap.shape[1], n])

            def tall(ap, n):
                return ap.rearrange("p (o t) -> p o t", o=1).to_broadcast([ap.shape[0], n, ap.shape[1]])

            step(logits_ready, dve.tensor_copy(topf[:], topi[:, :, 0:2].rearrange("p t k -> p k t")))
            chosen_ready.inc(dve.tensor_tensor(chosen[:], wide(expert_no[:, :], J), tall(topf[:].rearrange("p k t -> p (k t)"), E), ALU.is_equal))

            def row(k):
                return small[:, k, :]

            step(logits_ready, dve.tensor_tensor(shifted[:], logits[:], wide(top[:, :, 0], E), ALU.subtract))
            step(route, dve.tensor_tensor(row(0), top[:, :, 1], top[:, :, 0], ALU.subtract))
            dve.wait_ge(counted.sem, 1)
            ranks = ps_u[0][:, 0:E * J].rearrange("p (e j) -> p e j", j=J)
            counts = ps_u[1][:, 0:E * J].rearrange("p (e j) -> p e j", j=J)
            step(route, dve.tensor_tensor_scan(upto[:].rearrange("p e j -> p (e j)"), new_expert[:], ps_u[1][:, 0:E * J], 0.0, ALU.mult, ALU.add))
            step(route, dve.tensor_scalar(per_expert[:, 0, :], upto[:, :, J - 1], 1.0 / P, None, ALU.mult))
            step(route, dve.tensor_tensor(begun[:], wide(per_expert[:, 0, :], NT), tall(place_no[:, 0:NT], E), ALU.is_gt))
            step(route, dve.tensor_reduce(per_expert[:, 1, :], begun[:], AX.X, ALU.add))
            step(route, dve.tensor_tensor_scan(per_expert[:, 2, :], new_expert[:, 0:E], per_expert[:, 1, :], 0.0, ALU.mult, ALU.add))
            step(route, dve.tensor_tensor(per_expert[:, 3, :], per_expert[:, 2, :], per_expert[:, 1, :], ALU.subtract))
            step(route, dve.tensor_scalar(per_expert[:, 3, :], per_expert[:, 3, :], float(P), None, ALU.mult))
            step(route, dve.tensor_tensor(upto[:], upto[:], counts, ALU.subtract))
            step(route, dve.tensor_tensor(upto[:], upto[:], ranks, ALU.add))
            step(route, dve.tensor_tensor(upto[:], upto[:], wide(per_expert[:, 3, :], J), ALU.add))
            step(route, dve.tensor_tensor(upto[:], upto[:], chosen[:], ALU.mult))
            step(route, dve.tensor_reduce(pos[:], upto[:].rearrange("p e j -> p j e"), AX.X, ALU.add))
            step(route, dve.tensor_copy(pos_u[:], pos[:]))
            route.inc(dve.tensor_scalar(pos_hi[:], pos_u[:], P.bit_length() - 1, None, ALU.logical_shift_right))
            step(route, dve.tensor_scalar(pos_lo[:], pos_u[:], P - 1, None, ALU.bitwise_and))
            route.inc(dve.tensor_copy(tile_of[:], pos_hi[:]))
            step(route, dve.tensor_copy(row_of[:], pos_lo[:]))
            step(route, dve.tensor_tensor(tile_hot, tall(place_no[:, 0:NP], J), wide(tile_of[:], NP), ALU.is_equal))
            hots_ready.inc(dve.tensor_tensor(tile_hot, tile_hot, wide(token_no[:], NP), ALU.mult))
            for stored in hn_stored:
                dve.wait_ge(stored.sem, stored.n)
            for k in range(2):
                half = slice(k * NT, (k + 1) * NT)
                hots_ready.inc(dve.tensor_tensor(row_hot[:, half], tall(place_no[:], NT), wide(row_of[:, half], P), ALU.is_equal))
            step(route, dve.tensor_tensor(ended[:], wide(place_no[0:1, 0:NP], E), tall(per_expert[0:1, 2, :], NP), ALU.is_ge))
            step(route, dve.tensor_reduce(expert_f[:], ended[:], AX.X, ALU.add))
            step(route, dve.tensor_scalar(expert_f[:], expert_f[:], float(E - 1), None, ALU.min))
            table_ready.inc(dve.tensor_copy(expert_of[:], expert_f[:]))
            dve.wait_ge(placed.sem, 1)
            table_ready.inc(dve.tensor_copy(token_of[:], ps_d[0][:, 0:NP]))
            dve.wait_ge(exp_ready.sem, 2)
            step(route, dve.tensor_reduce(row(2), shifted[:], AX.X, ALU.add))
            step(route, dve.reciprocal(row(3), row(2)))
            step(route, dve.tensor_tensor(row(4), row(1), row(3), ALU.mult))
            step(route, dve.scalar_tensor_tensor(row(5), row(3), 1e-9, row(4), ALU.add, ALU.add))
            step(route, dve.reciprocal(row(6), row(5)))
            step(route, dve.tensor_tensor(row(3), row(3), row(6), ALU.mult))
            step(route, dve.tensor_tensor(row(4), row(4), row(6), ALU.mult))

            def keep_xT(ee, k):
                tile_done(dve, x_turned, ee, k)
                tile_done(dve, up_made, ee, k - 2)
                dve.tensor_tensor(xT[:, k % 2, :].rearrange("p (t o) -> p t o", o=P), ps_x[:, :].rearrange("p (t o) -> p t o", o=P),
                                  wide(norm_col[:], P), ALU.mult).then_inc(xT_ready.sem, 1)

            def turn(ee, first, last):
                for q in range(2):
                    if not (last and q == 1):
                        keep_xT(ee, q + 1)
                    tile_done(dve, up_made, ee, q)
                    tile_done(dve, silu_ready, ee, q)
                    tile_done(dve, act_turned, ee, q - 2)
                    dve.tensor_tensor(act_row[:, q, :], ps_u[q][:, 0:I], silu[:, q, :], ALU.mult).then_inc(row_ready.sem, 1)

            keep_xT(0, 0)
            run_tiles(dve, turn)

            def normed(c):
                dve.wait_ge(rstd_ready.sem, c + 1)
                for i in range(ST):
                    t = ST * c + i
                    out_ready.inc(dve.tensor_scalar(acc[:, t, :], acc[:, t, :], mv[:, t, 0:1], rstd[:, t:t + 1], ALU.subtract, ALU.mult))

            for c in range(B):
                for k in range(2):
                    for i in range(ST):
                        t = ST * c + i
                        n = 2 * ST * c + ST * k + i
                        dve.wait_ge(result_in[n % RING].sem, 16 * (n // RING + 1))
                        if k:
                            dve.wait_ge(added.sem, n - ST + 1)
                        added.inc(dve.scalar_tensor_tensor(acc[:, t, :], results[:, n % RING, :], small[:, 3 + k, t:t + 1],
                                                           acc[:, t, :], ALU.mult, ALU.add))
                for i in range(ST):
                    dve.wait_ge(added.sem, 2 * ST * (c + 1) - ST + i + 1)
                    ln_step.inc(dve.bn_stats(stats[:, i, :], acc[:, ST * c + i, :]))
                dve.wait_ge(ln_step.sem, ln_step.n)
                for i in range(ST):
                    ln_step.inc(dve.bn_aggr(mv[:, ST * c + i, :], stats[:, i, :]))
                dve.wait_ge(ln_step.sem, ln_step.n)
                step(ln_step, dve.tensor_scalar(veps[:, ST * c:ST * (c + 1)], mv[:, ST * c:ST * (c + 1), 1], 1e-5, None, ALU.add))
                assert ln_step.n == (2 * ST + 1) * (c + 1)
                if c:
                    normed(c - 1)
            normed(B - 1)

        @block.gpsimd
        def _(pool):
            pool.wait_ge(consts_ready.sem, 2)
            for c in range(B):
                own = slice(ST * c, ST * (c + 1))
                pool.wait_ge(eps_added.sem, c + 1)
                hr_ready.inc(pool.tensor_tensor(hr[:, own], ssv[:, own], mhalf[:, own], ALU.pow))
            pool.wait_ge(table_ready.sem, 2)
            for stored in hn_stored:
                pool.wait_ge(stored.sem, stored.n)

            def turn(ee, first, last):
                for q in range(2):
                    tile_done(pool, x_turned, ee, q - 2)
                    pool.tensor_copy(rows_of[q][:, :], token_of[:, at(ee, q)]).then_inc(rows_copied.sem, 1)
                    tile_done(pool, rows_copied, ee, q)
                    pool.sem_inc(rows_seen.sem, 1)
                    pool.indirect_dma_start(xg[:, q, :], None, hn_dram,
                                            bass.IndirectOffsetOnAxis(ap=rows_of[q][:, :], axis=0)).then_inc(gathered[q].sem, 16)

            def rsqrt(c):
                own = slice(ST * c, ST * (c + 1))
                pool.wait_ge(ln_step.sem, (2 * ST + 1) * (c + 1))
                rstd_ready.inc(pool.tensor_tensor(rstd[:, own], veps[:, own], mhalf[:, own], ALU.pow))

            run_tiles(pool, turn)
            for q in range(2):
                pool.wait_ge(y_stored[q].sem, 16 * (NP // 2))
            for c in range(B):
                for k in range(2):
                    for i in range(ST):
                        t = ST * c + i
                        n = 2 * ST * c + ST * k + i
                        if n >= RING:
                            pool.wait_ge(added.sem, n - RING + 1)
                        result_in[n % RING].inc(pool.indirect_dma_start(
                            results[:, n % RING, :], None, y_dram,
                            bass.IndirectOffsetOnAxis(ap=pos_u[:, k * NT + t:k * NT + t + 1], axis=0)), 16)
                if c:
                    rsqrt(c - 1)
            rsqrt(B - 1)


def build(nc, io, out):
    B, S, F = io["x"].shape
    x2 = nc.dram_tensor("x2", (B, S, F), F32, kind="Internal").ap()
    bc_dram = nc.dram_tensor("bc_rows", (2 * io["A_log"].shape[1], S), F32, kind="Internal").ap()
    hidden = nc.dram_tensor("hidden", (B, S, F), F32, kind="Internal").ap()
    attention_and_scan(nc, io, x2, bc_dram)
    grouped_attention(nc, io, x2, hidden)
    mixture_of_experts(nc, io, x2, hidden, out)


def shape_constants(length, width):
    freqs = (1.0 / np.float32(1000000.0) ** (np.arange(0, width, 2, dtype=np.float32) / np.float32(width))).astype(np.float32)
    angle = np.outer(np.arange(length, dtype=np.float32), freqs).astype(np.float32)
    cos, sin = np.cos(angle), np.sin(angle)
    return {"cos": np.concatenate([cos, cos], 1), "sin": np.concatenate([-sin, sin], 1),
            "mask": np.triu(np.ones((P, P), np.float32), 1) * np.float32(-1e30)}


def laid_out(inputs):
    i = {k: np.asarray(a) for k, a in inputs.items()}

    def T(a):
        return np.ascontiguousarray(np.swapaxes(a, -1, -2))

    def columns(a):
        return np.ascontiguousarray(a.reshape(-1, P).T)

    a, s = "L0_attn_", "L0_xattn_"
    got = {"x": i["x"], "xT": T(i["x"]), "ctxT": T(i["ctx_1024"])}
    for w in "qkvo":
        got["W" + w] = i[a + "W" + w]
    got |= {"bq": columns(i[a + "bq"]), "bk": columns(i[a + "bk"]), "bv": i[a + "bv"][None], "bo": i[a + "bo"][None]}
    got |= {"in_wT": T(i[s + "in_proj_w"]), "conv_w": i[s + "conv_w"][:, 0, :], "conv_b": columns(i[s + "conv_b"]),
            "x_wT": T(i[s + "x_proj_w"]), "dt_wT": T(i[s + "dt_proj_w"]), "dt_b": columns(i[s + "dt_proj_b"]),
            "A_log": i[s + "A_log"], "Dskip": columns(i[s + "D"])}
    f = "L0_ffn_"
    got |= {"q_wT": T(i[f + "q_w"]), "k_wT": T(i[f + "k_w"]), "v_wT": T(i[f + "v_w"]), "o_wT": T(i[f + "o_w"]),
            "attn_norm": columns(i[f + "attn_norm_w"]), "q_norm": i[f + "q_norm_w"][None], "k_norm": i[f + "k_norm_w"][None]}
    got |= shape_constants(i["x"].shape[1], i[f + "q_norm_w"].shape[0])
    got |= {"gate_wT": T(i[f + "gate_w"]), "ffn_norm": columns(i[f + "ffn_norm_w"]),
            "wgT": T(i[f + "wg"]), "wuT": T(i[f + "wu"]), "wdT": T(i[f + "wd"]),
            "before": np.triu(np.ones((P, P), np.float32), 1)}
    tokens, experts = i["x"].shape[0] * i["x"].shape[1], i[f + "gate_w"].shape[0]
    number = np.arange(tokens, dtype=np.float32).reshape(-1, P).T
    first = np.ones((experts, 2 * tokens // P), np.float32)
    first[:, 0] = 0
    got |= {"place_no": np.arange(P, dtype=np.float32)[None], "token_no": np.concatenate([number, number], 1), "new_expert": first.reshape(1, -1)}
    got["ident"] = np.eye(P, dtype=np.float32)
    return {k: np.ascontiguousarray(v) for k, v in got.items()}


def kernel(**inputs):
    import concourse.bacc as bacc
    from concourse.bass_utils import run_bass_kernel_spmd

    data = laid_out(inputs)
    nc = bacc.Bacc("TRN2", target_bir_lowering=False, num_devices=1)
    arrays, io = {}, {}
    for name, a in data.items():
        arrays["in_" + name] = a
        io[name] = nc.dram_tensor("in_" + name, a.shape, mybir.dt.from_np(a.dtype), kind="ExternalInput").ap()
    out = nc.dram_tensor("out", inputs["x"].shape, F32, kind="ExternalOutput").ap()
    build(nc, io, out)
    return run_bass_kernel_spmd(nc, [arrays], core_ids=[0]).results[0]["out"]
```

```python
from contextlib import ExitStack

import numpy as np

import concourse.bass as bass
from concourse import mybir
from concourse.alu_op_type import AluOpType as ALU

F32 = mybir.dt.float32
ACT = mybir.ActivationFunctionType
AX = mybir.AxisListType

P = 128


class Signal:

    def __init__(self, sem, per_turn=0, primed=False, base=0):
        self.sem, self.per, self.n, self.primed, self.base = sem, per_turn, 0, primed, base

    def prime(self, engine):
        engine.sem_inc(self.sem, 1)

    def inc(self, instruction, by=1):
        self.n += by
        return instruction.then_inc(self.sem, by)

    def wait(self, engine, turn, count):
        if turn is None:
            engine.wait_ge(self.sem, count + self.primed)
            return
        assert count + self.base > 0 or self.primed
        engine.wait_ge(self.sem, turn * self.per + (self.base + count + self.primed))

    def wait_last(self, engine, turn):
        self.wait(engine, turn, self.n)

    def wait_all(self, engine, count):
        engine.wait_ge(self.sem, count + self.primed)

    def close(self):
        assert self.n == self.per, (self.sem, self.n, self.per)


class Plan:

    def __init__(self, uses, tasks, before=0):
        self.uses, self.tasks, self.before = uses, tasks, before
        self.number = {(what, key): n for n, (what, key, _) in enumerate(uses)}
        self.emptied = {who: [sum(w == who for _, _, w in uses[:n]) for n in range(len(uses) + 1)] for who in ("act", "dve")}

    def count(self, what, key):
        n = self.number[what, key]
        return self.emptied[self.uses[n][2]][n + 1]

    def bank(self, what, key):
        return (self.before + self.number[what, key]) % 2


def attention_and_scan(nc, io, x2_dram, bc_dram):
    B, S, F = io["x"].shape
    DM = io["ctxT"].shape[1]
    NS = io["A_log"].shape[1]
    R = io["dt_wT"].shape[0]
    XD = R + 2 * NS
    KC = io["conv_w"].shape[1]
    HD = 64
    NH = F // HD
    FT, ST, MT = F // P, S // P, DM // P
    NPAIR = NH // 2
    QSCALE = float(1.0 / np.sqrt(float(NH)))
    SMALL = 2.0 ** -7
    assert NS == 2 * NH and ST == 4 and FT == 4

    SN = NH * ST
    EXP, TURN, WEIGH = 1, 6, 2 * ST + 3
    SLOTS = SN + 7
    tasks = {}
    for p in range(1, NPAIR):
        tasks |= {8 * p - 6: ("q", p, "act"), 8 * p - 4: ("k", p, "act"), 8 * p - 2: ("v", p, "dve")}
    ahead = {5 + 2 * e: ("in", e, "act") for e in range(FT)} | {19 + 2 * e: ("dt", e, "act") for e in range(FT)}
    ahead |= {SN - 4: ("q", 0, "act"), SN - 2: ("k", 0, "act"), SN: ("v", 0, "dve")}
    POOL = 2
    CONV, SILU, XP = 6, 14, 16
    RESID = NS - 2
    assert NH == 8 and not tasks.keys() & ahead.keys()
    finish = [("gT", i, "dve") for i in range(ST)]
    PARTIAL = {SN + 1 + i: i for i in range(ST - 1)}

    def plan_of(tasks, before):
        named = {s: ("next " + what if (what, k) in (("q", 0), ("k", 0), ("v", 0)) else what, k, who) for s, (what, k, who) in tasks.items()}
        return Plan([named[s] for s in sorted(named)] + finish, named, before)

    first = Plan([(what if what in ("in", "dt") else "next " + what, k, who) for what, k, who in (ahead[s] for s in sorted(ahead))], {})
    inner = plan_of(tasks | ahead, len(first.uses))
    final = plan_of(tasks, len(first.uses))
    NPP = len(inner.uses)
    assert NPP % 2 == 0

    with ExitStack() as ctx:
        def sb(name, shape, dt=F32):
            return ctx.enter_context(nc.sbuf_tensor("p1_" + name, shape, dt))

        def sig(name, per=0, primed=False, base=0):
            return Signal(ctx.enter_context(nc.semaphore("p1_" + name)), per, primed, base)

        wq, wk, wv, wo = (sb(f"w{c}_sb", [P, FT, F]) for c in "qkvo")
        w_in = sb("w_in", [P, MT, F])
        w_xp = sb("w_xp", [P, FT, XD])
        w_dt = sb("w_dt", [R, F])
        conv_w = sb("conv_w_sb", [P, FT, KC])
        cols = sb("cols", [P, 6, FT])
        a_log = sb("a_log", [P, FT, NS])
        a_neg = sb("a_neg", [P, FT, NS])
        bv_row = sb("bv_row", [P, F])
        bo_row = sb("bo_row", [P, F])
        ident = sb("ident_sb", [P, P])
        mhalf = sb("mhalf", [P, 2 * ST])
        xT = sb("xT_sb", [P, FT, S])
        ctxT = sb("ctxT_sb", [P, MT, S])
        xtok = sb("xtok", [P, ST, F])
        xin = sb("xin", [P, FT, S + KC - 1])
        z = xin[:, :, KC - 1:]
        u = sb("u", [P, FT, S])
        dt = sb("dt", [P, FT, S])
        dtu = sb("dtu", [P, FT, S])
        yacc = sb("yacc", [P, FT, S])
        xdbl = sb("xdbl", [XD, S])
        decay = sb("decay", [P, 2, FT, S])
        hbuf = sb("hbuf", [P, 2, FT, S])
        bc = sb("bc", [P, 4, 2, S])
        qT = sb("qT", [P, 2, S])
        kT = sb("kT", [P, 2, S])
        v = sb("v", [P, 2, ST, P])
        prob = sb("prob", [P, 2, ST, S])
        probT = sb("probT", [P, 2, ST, S])
        feats = sb("feats", [P, NPAIR, S])
        nmax = sb("nmax", [P, 2, ST])
        rsum = sb("rsum", [P, 2, ST])
        rinv = sb("rinv", [P, 2, ST])
        stats = sb("stats", [P, ST, 6])
        mv = sb("mv", [P, ST, 2])
        veps = sb("veps", [P, ST])
        rstd = sb("rstd", [P, ST])

        pp = [ctx.enter_context(nc.psum_tensor(f"p1_pp{i}", [P, 512], F32)) for i in range(2)]
        ps_s = [ctx.enter_context(nc.psum_tensor(f"p1_ps_s{i}", [P, 512], F32)) for i in range(3)]
        ps_t = [ctx.enter_context(nc.psum_tensor(f"p1_ps_t{i}", [P, 512], F32)) for i in range(2)]
        ps_o = ctx.enter_context(nc.psum_tensor("p1_ps_o", [P, 512], F32))

        wo_bank = [*ps_s, ps_o]
        weights_in = {w: sig(f"weights_in1_{w}") for w in ("scan", "qkv", "wo")}
        a_ready = sig("a_ready")
        pads_ready = sig("pads_ready")
        ctx_in = sig("ctx_in", 16, base=16)
        xT_in = sig("xT_in", 16, base=16)
        xtok_in = sig("xtok_in", 16)
        pp_ready = sig("pp_ready", NPP, base=len(first.uses))
        pp_free = {who: sig(f"pp_free_{who}", inner.emptied[who][-1], base=first.emptied[who][-1]) for who in ("act", "dve")}
        conv_step = sig("conv_step", FT * KC, base=FT * KC)
        u_ready = sig("u_ready", 1, base=1)
        xp_made = sig("xp_made", 1, base=1)
        xdbl_ready = sig("xdbl_ready", 1, base=1)
        bc_stored = sig("bc_stored", 16, base=16)
        bc_in = [sig(f"bc_in{i}", 16 * NS // 4) for i in range(4)]
        sp_act = sig("sp_act", 3, base=3)
        sp_dve = sig("sp_dve", 6, base=6)
        dtu_ready = sig("dtu_ready", 1, base=1)
        y_begun = sig("y_begun", FT, base=FT)
        decay_ready = sig("decay_ready", NS * FT)
        dbu_ready = sig("dbu_ready", NS)
        pool_dbu = sig("pool_dbu", NS)
        scanned = sig("scanned", NS * FT)
        hc_ready = sig("hc_ready", NS, primed=True)
        y_added = sig("y_added", NS, primed=True)
        scores_ready = sig("scores_ready", SN)
        max_ready = sig("max_ready", SN)
        exp_ready = sig("exp_ready", SN, primed=True)
        rinv_ready = sig("rinv_ready", NH)
        normed = sig("normed", NH * 3)
        normed_dve = sig("normed_dve", NH * 1)
        turned = sig("turned", SN)
        probT_ready = sig("probT_ready", SN, primed=True)
        weighed = sig("weighed", NPAIR * ST)
        feats_ready = sig("feats_ready", NPAIR, primed=True)
        wo_made = sig("wo_made", ST)
        wo_added = sig("wo_added", ST)
        resid = sig("resid", 1)
        ln_step = sig("ln_step", 2 * (2 * ST + 1) + ST)
        rstd_ready = sig("rstd_ready", 2)
        x1_ready = sig("x1_ready", ST)
        gate_ready = sig("gate_ready", ST)
        g_ready = sig("g_ready", FT)
        x2_stored = sig("x2_stored", 16, primed=True)

        waits_seen = ctx.enter_context(nc.semaphore("waits_seen"))
        stats_seen = ctx.enter_context(nc.semaphore("stats_seen"))
        block = ctx.enter_context(nc.Block())

        col_names = ("bq", "bk", "conv_b", "dt_b", "Dskip")

        def settled(engine):
            engine.wait_ge(pads_ready.sem, 2)

        def run_batches(engine, batch):
            with engine.Fori(0, B - 1) as b:
                batch(b, inner)
            batch(B - 1, final)

        @block.sync
        def _(sp):
            def load(w, dst, src):
                weights_in[w].inc(sp.dma_start(dst, src), 16)

            def rows(name):
                return io[name].rearrange("(t p) n -> p t n", p=P)

            def load_ctx(this):
                ctx_in.inc(sp.dma_start(ctxT[:], io["ctxT"][this].rearrange("o (t p) s -> p (o t) s", p=P)), 16)

            def load_xT(this):
                xT_in.inc(sp.dma_start(xT[:], io["xT"][this].rearrange("o (t p) s -> p (o t) s", p=P)), 16)

            def store_bc(b):
                xdbl_ready.wait(sp, b, 1)
                bc_stored.inc(sp.dma_start(bc_dram, xdbl[R:XD, :]), 16)
                bc_stored.wait(sp, b, 16)
                sp.sem_inc(waits_seen, 1)

            load("scan", w_in[:], rows("in_wT"))
            load_ctx(slice(0, 1))
            load("scan", conv_w[:], rows("conv_w"))
            for c, name in enumerate(col_names):
                load("scan", cols[:, c, :], io[name])
            load("scan", w_xp[:], rows("x_wT"))
            load("scan", w_dt[:], io["dt_wT"])
            load("scan", a_log[:], rows("A_log"))
            load("scan", ident[:], io["ident"])
            load("scan", bv_row[:], io["bv"].to_broadcast([P, F]))
            load("scan", bo_row[:], io["bo"].to_broadcast([P, F]))
            load_xT(slice(0, 1))
            load("qkv", wq[:], rows("Wq"))
            load("qkv", wk[:], rows("Wk"))
            load("qkv", wv[:], rows("Wv"))
            load("wo", wo[:], rows("Wo"))
            store_bc(None)

            def batch(b, plan):
                if plan is inner:
                    pp_ready.wait(sp, b, 0)
                    settled(sp)
                    load_ctx(bass.ds(b + 1, 1))
                for n in range(NS):
                    if n == 4:
                        x2_stored.wait(sp, b, 0)
                        settled(sp)
                        xtok_in.inc(sp.dma_start(xtok[:], io["x"][bass.ds(b, 1)].rearrange("o (t p) f -> p (o t) f", p=P)), 16)
                    if n == NS - 2 and plan is inner:
                        pp_ready.wait(sp, b, plan.number["v", NPAIR - 1] + 1)
                        settled(sp)
                        load_xT(bass.ds(b + 1, 1))
                    hc_ready.wait(sp, b, max(n - 3, 0))
                    src = bc_dram.rearrange("(o c n) s -> n o c s", o=1, c=2)[n].to_broadcast([P, 2, S])
                    bc_in[n % 4].inc(sp.dma_start(bc[:, n % 4], src), 16)
                if plan is inner:
                    for i in range(4):
                        bc_in[i].wait(sp, b, bc_in[i].per)
                        sp.sem_inc(waits_seen, 1)
                    store_bc(b)

            run_batches(sp, batch)

        @block.tensor
        def _(pe):
            def take(b, plan, what, key):
                n = plan.number[what, key]
                if n >= 2:
                    who = plan.uses[n - 2][2]
                    pp_free[who].wait(pe, b, plan.emptied[who][n - 1])
                elif b is not None:
                    for who in ("act", "dve"):
                        pp_free[who].wait(pe, b, 0)
                return pp[plan.bank(what, key)]

            def x_proj(b):
                u_ready.wait(pe, b, 1)
                if b is not None:
                    feats_ready.wait(pe, b, 1)
                for k in range(FT):
                    mm = pe.matmul(ps_o[0:XD, :], w_xp[:, k, :], u[:, k, :], start=(k == 0), stop=(k == FT - 1))
                xp_made.inc(mm)

            def task(b, plan, what, key):
                bank = take(b, plan, what, key)
                what = what.removeprefix("next ")
                if what == "in":
                    if key == 0:
                        ctx_in.wait(pe, b, 16)
                    for k in range(MT):
                        mm = pe.matmul(bank[:, :], w_in[:, k, key * P:(key + 1) * P], ctxT[:, k, :],
                                       start=(k == 0), stop=(k == MT - 1))
                elif what == "dt":
                    if key == 0:
                        xdbl_ready.wait(pe, b, 1)
                    mm = pe.matmul(bank[:, :], w_dt[:, key * P:(key + 1) * P], xdbl[0:R, :], start=True, stop=True)
                elif what in ("q", "k"):
                    if what == "q" and key == 0:
                        xT_in.wait(pe, b, 16)
                    w = wq if what == "q" else wk
                    for k in range(FT):
                        mm = pe.matmul(bank[:, :], w[:, k, key * P:(key + 1) * P], xT[:, k, :],
                                       start=(k == 0), stop=(k == FT - 1))
                else:
                    for t in range(ST):
                        for k in range(FT):
                            mm = pe.matmul(bank[:, t * P:(t + 1) * P], xT[:, k, t * P:(t + 1) * P],
                                           wv[:, k, key * P:(key + 1) * P], start=(k == 0), stop=(k == FT - 1))
                pp_ready.inc(mm)

            def batch(b, plan):
                def score(h, i):
                    p, r = h // 2, (h % 2) * HD
                    n = ST * h + i
                    exp_ready.wait(pe, b, max(n - 2, 0))
                    if i == 0:
                        pp_free["act"].wait(pe, b, plan.count("k", p) if p else 0)
                    scores_ready.inc(pe.matmul(ps_s[n % 3][:, :], qT[r:r + HD, p % 2, i * P:(i + 1) * P],
                                               kT[r:r + HD, p % 2, :], start=True, stop=True))

                def turn(h, j):
                    n = ST * h + j
                    probT_ready.wait(pe, b, max(n - 1, 0))
                    if j == 0:
                        normed.wait(pe, b, 3 * (h + 1))
                        normed_dve.wait(pe, b, 1 * (h + 1))
                    for i in range(ST):
                        mm = pe.transpose(ps_t[n % 2][:, i * P:(i + 1) * P], prob[:, h % 2, i, j * P:(j + 1) * P], ident[:, :])
                    turned.inc(mm)

                def weigh(p, j):
                    if j == 0:
                        feats_ready.wait(pe, b, p)
                        pp_free["dve"].wait(pe, b, plan.count("v", p) if p else 0)
                        if p == 1:
                            xdbl_ready.wait(pe, b, 1 if plan is inner else 0)
                    probT_ready.wait(pe, b, ST * (2 * p + 1) + j + 1)
                    for hh in range(2):
                        mm = pe.matmul(ps_o[hh * HD:(hh + 1) * HD, :], v[:, p % 2, j, hh * HD:(hh + 1) * HD],
                                       probT[:, hh, j, :], start=(j == 0), stop=(j == ST - 1))
                    weighed.inc(mm)

                def weigh_out(i, pairs):
                    for p in pairs:
                        mm = pe.matmul(wo_bank[i][:, :], feats[:, p, i * P:(i + 1) * P], wo[:, p, :],
                                       start=(p == 0), stop=(p == NPAIR - 1))
                    return mm

                score(0, 0)
                for s in range(SLOTS):
                    if s + 1 < SN:
                        score(*divmod(s + 1, ST))
                    if TURN <= s < SN + TURN:
                        turn(*divmod(s - TURN, ST))
                    p, j = divmod(s - WEIGH, 2 * ST)
                    if 0 <= p and j < ST:
                        weigh(p, j)
                    if plan is inner and s == XP:
                        x_proj(b)
                    if s in plan.tasks:
                        task(b, plan, *plan.tasks[s][:2])
                    if s in PARTIAL:
                        exp_ready.wait(pe, b, SN)
                        feats_ready.wait(pe, b, NPAIR - 1)
                        weigh_out(PARTIAL[s], range(NPAIR - 1))
                feats_ready.wait(pe, b, NPAIR)
                for i in range(ST):
                    wo_made.inc(weigh_out(i, range(NPAIR - 1 if i in PARTIAL.values() else 0, NPAIR)))
                for i in range(ST):
                    bank = take(b, plan, "gT", i)
                    for e in range(FT):
                        if i == 0:
                            g_ready.wait(pe, b, e + 1)
                        mm = pe.transpose(bank[:, e * P:(e + 1) * P], yacc[:, e, i * P:(i + 1) * P], ident[:, :])
                    pp_ready.inc(mm)

            pe.wait_ge(weights_in["scan"].sem, weights_in["scan"].n)
            for what, key, _ in first.uses:
                if (what, key) == ("dt", 0):
                    x_proj(None)
                if what == "next q":
                    pe.wait_ge(weights_in["qkv"].sem, weights_in["qkv"].n)
                task(None, first, what, key)
            pe.wait_ge(weights_in["wo"].sem, weights_in["wo"].n)
            run_batches(pe, batch)

        @block.scalar
        def _(act):
            x2_stored.prime(act)
            exp_ready.prime(act)
            probT_ready.prime(act)
            feats_ready.prime(act)
            act.wait_ge(weights_in["scan"].sem, weights_in["scan"].n)
            a_ready.inc(act.activation(a_neg[:], a_log[:], ACT.Exp))
            a_ready.inc(act.mul(cols[:, 5, :], cols[:, 0, :], QSCALE))
            act.wait_ge(a_ready.sem, 1)
            a_ready.inc(act.mul(a_neg[:], a_neg[:], -1.0))
            act.wait_ge(a_ready.sem, 3)

            def task(b, plan, what, key):
                bank = pp[plan.bank(what, key)]
                if what == "in" and key == 0 and b is not None:
                    sp_dve.wait(act, b, 0)
                if what == "q" and key >= 2:
                    scores_ready.wait(act, b, 2 * ST * (key - 1))
                if what == "next q" and b is not None:
                    scores_ready.wait(act, b, 2 * ST * (NPAIR - 1))
                pp_ready.wait(act, b, plan.number[what, key] + 1)
                what = what.removeprefix("next ")
                if what == "in":
                    got = act.activation(xin[:, key, KC - 1:], bank[:, :], ACT.Copy)
                elif what == "dt":
                    got = act.activation(z[:, key, :], bank[:, :], ACT.Identity, bias=cols[:, 3, key:key + 1])
                elif what == "q":
                    got = act.activation(qT[:, key % 2, :], bank[:, :], ACT.Identity, bias=cols[:, 5, key:key + 1], scale=QSCALE)
                else:
                    got = act.activation(kT[:, key % 2, :], bank[:, :], ACT.Identity, bias=cols[:, 1, key:key + 1])
                pp_free["act"].inc(got)

            def silu_of_conv(b):
                conv_step.wait(act, b, FT * KC)
                u_ready.inc(act.activation(u[:], u[:], ACT.Silu))

            def keep_xdbl(b):
                xp_made.wait(act, b, 1)
                if b is not None:
                    bc_stored.wait(act, b, 0)
                xdbl_ready.inc(act.activation(xdbl[:, :], ps_o[0:XD, :], ACT.Copy))

            mag, low = decay[:, 0], decay[:, 1]

            def softplus(b, plan, k):
                if k == 0:
                    pp_free["act"].wait(act, b, plan.count("dt", FT - 1))
                    if b is not None:
                        scanned.wait(act, b, NS * FT)
                    sp_act.inc(act.activation(mag, z, ACT.Abs))
                elif k == 1:
                    sp_act.wait(act, b, 1)
                    sp_act.inc(act.activation(mag, mag, ACT.Exp, scale=-1.0))
                else:
                    sp_act.wait(act, b, 2)
                    sp_act.inc(act.activation(low, mag, ACT.Ln, bias=1.0))

            def begin_y(b, plan):
                if b is not None:
                    pp_ready.wait(act, b, plan.number["gT", ST - 1] + 1)
                for e in range(FT):
                    y_begun.inc(act.activation(yacc[:, e, :], u[:, e, :], ACT.Copy, scale=cols[:, 4, e:e + 1]))

            def batch(b, plan):
                def exp_scores(h, i):
                    n = ST * h + i
                    max_ready.wait(act, b, n + 1)
                    if h >= 2 and i == 0:
                        turned.wait(act, b, ST * (h - 1))
                    exp_ready.inc(act.activation(prob[:, h % 2, i, :], ps_s[n % 3][:, :], ACT.Exp,
                                                 bias=nmax[:, h % 2, i:i + 1], accum_out=rsum[:, h % 2, i:i + 1]))

                def normalise(h, i):
                    rinv_ready.wait(act, b, h + 1)
                    normed.inc(act.activation(prob[:, h % 2, i, :], prob[:, h % 2, i, :], ACT.Copy, scale=rinv[:, h % 2, i:i + 1]))

                def copy_turned(h, j):
                    n = ST * h + j
                    turned.wait(act, b, n + 1)
                    if h >= 2:
                        weighed.wait(act, b, ST * (h // 2 - 1) + j + 1)
                    probT_ready.inc(act.activation(probT[:, h % 2, j, :], ps_t[n % 2][:, :], ACT.Copy))

                def decays(slot):
                    n = slot // 2
                    if n >= 2 and slot % 2 == 0:
                        scanned.wait(act, b, FT * (n - 1))
                    for e in ((2, 3) if slot % 2 == 0 else (0, 1)):
                        decay_ready.inc(act.activation(decay[:, n % 2, e, :], dt[:, e, :], ACT.Exp, scale=a_neg[:, e, n:n + 1]))

                def copy_feats(p):
                    weighed.wait(act, b, ST * (p + 1))
                    feats_ready.inc(act.activation(feats[:, p, :], ps_o[:, :], ACT.Copy))

                sp_dve.wait(act, b, 0)
                decays(0)
                for s in range(SLOTS + 1):
                    p, j = divmod(s - WEIGH - ST, 2 * ST)
                    if 0 <= p and j == 0:
                        copy_feats(p)
                    if EXP <= s < SN + EXP:
                        exp_scores(*divmod(s - EXP, ST))
                    if TURN <= s < SN + TURN:
                        copy_turned(*divmod(s - TURN, ST))
                    if s % ST == EXP and ST < s <= SN + EXP:
                        for i in range(1, ST):
                            normalise(s // ST - 1, i)
                    if s + 1 < SN:
                        decays(s + 1)
                    if plan is inner:
                        if s == SILU:
                            silu_of_conv(b)
                        if s == XP:
                            keep_xdbl(b)
                        if SN + 1 <= s < SN + 4:
                            softplus(b, plan, s - SN - 1)
                    if s in plan.tasks and plan.tasks[s][2] == "act":
                        task(b, plan, *plan.tasks[s][:2])
                for e in range(ST):
                    x1_ready.wait(act, b, e + 1)
                    gate_ready.inc(act.activation(prob[:, 0, e, :], xtok[:, e, :], ACT.Silu))
                if plan is inner:
                    begin_y(b, plan)
                ln_step.wait(act, b, ln_step.per)
                settled(act)
                x2_stored.inc(act.dma_start(x2_dram[bass.ds(b, 1)].rearrange("o (t p) f -> p (o t) f", p=P), xtok[:]), 16)

            for what, key, _ in first.uses:
                if (what, key) == ("dt", 0):
                    silu_of_conv(None)
                    keep_xdbl(None)
                elif what == "next q":
                    for k in range(3):
                        softplus(None, first, k)
                if first.uses[first.number[what, key]][2] == "act":
                    task(None, first, what, key)
            begin_y(None, first)
            run_batches(act, batch)
            x2_stored.wait_all(act, 16 * B)

        @block.vector
        def _(dve):
            y_added.prime(dve)
            dve.wait_ge(weights_in["scan"].sem, weights_in["scan"].n)
            dve.wait_ge(pads_ready.sem, 2)

            def convolve(b, plan, e):
                pp_free["act"].wait(dve, b, plan.count("in", e))
                out = u[:, e, :]
                conv_step.inc(dve.tensor_scalar(out, xin[:, e, 0:S], conv_w[:, e, 0:1], cols[:, 2, e:e + 1], ALU.mult, ALU.add))
                for k in range(1, KC):
                    conv_step.wait(dve, b, KC * e + k)
                    conv_step.inc(dve.scalar_tensor_tensor(out, xin[:, e, k:k + S], conv_w[:, e, k:k + 1], out, ALU.mult, ALU.add))

            def task(b, plan, what, key):
                bank = pp[plan.bank(what, key)]
                if what == "v" and key >= 2:
                    weighed.wait(dve, b, ST * (key - 1))
                if what == "next v" and b is not None:
                    weighed.wait(dve, b, ST * (NPAIR - 1))
                pp_ready.wait(dve, b, plan.number[what, key] + 1)
                if what in ("v", "next v"):
                    pp_free["dve"].inc(dve.tensor_tensor(
                        v[:, key % 2], bank[:, :].rearrange("p (t c) -> p t c", t=ST),
                        bv_row[:, key * P:(key + 1) * P].rearrange("p (o c) -> p o c", o=1).to_broadcast([P, ST, P]), ALU.add))
                else:
                    pp_free["dve"].inc(dve.tensor_tensor(xtok[:, key, :], xtok[:, key, :], bank[:, :], ALU.add))

            mag, low, poly, part = decay[:, 0], decay[:, 1], hbuf[:, 0], hbuf[:, 1]

            def softplus(b, k):
                if k == 0:
                    sp_act.wait(dve, b, 2)
                elif k == 3:
                    sp_act.wait(dve, b, 3)
                if k:
                    sp_dve.wait(dve, b, k)
                if k == 0:
                    step = dve.scalar_tensor_tensor(poly, mag, -1.5, mag, ALU.add, ALU.mult)
                elif k == 1:
                    step = dve.scalar_tensor_tensor(poly, poly, 3.0, mag, ALU.add, ALU.mult)
                elif k == 2:
                    step = dve.scalar_tensor_tensor(part, mag, SMALL, poly, ALU.is_lt, ALU.mult)
                elif k == 3:
                    step = dve.scalar_tensor_tensor(low, mag, SMALL, low, ALU.is_ge, ALU.mult)
                elif k == 4:
                    step = dve.scalar_tensor_tensor(low, part, 1.0 / 3.0, low, ALU.mult, ALU.add)
                else:
                    step = dve.scalar_tensor_tensor(dt[:], z, 0.0, low, ALU.max, ALU.add)
                sp_dve.inc(step)

            def batch(b, plan):
                def row_max(h, i):
                    n = ST * h + i
                    scores_ready.wait(dve, b, n + 1)
                    max_ready.inc(dve.tensor_reduce(nmax[:, h % 2, i:i + 1], ps_s[n % 3][:, :], AX.X, ALU.max, negate=True))

                def invert_sums(h):
                    exp_ready.wait(dve, b, ST * (h + 1))
                    rinv_ready.inc(dve.reciprocal(rinv[:, h % 2, :], rsum[:, h % 2, :]))
                    rinv_ready.wait(dve, b, h + 1)
                    for i in range(1):
                        normed_dve.inc(dve.tensor_scalar(prob[:, h % 2, i, :], prob[:, h % 2, i, :], rinv[:, h % 2, i:i + 1], None, ALU.mult))

                def make_dbu(n):
                    bc_in[n % 4].wait(dve, b, 16 * (n // 4 + 1))
                    y_added.wait(dve, b, max(n - 1, 0))
                    if n == 0:
                        dtu_ready.wait(dve, b, 0)
                    dbu_ready.inc(dve.tensor_tensor(hbuf[:, n % 2, POOL:], dtu[:, POOL:], bc[:, n % 4, 0:1, :].to_broadcast([P, FT - POOL, S]), ALU.mult))

                def scan(n, e):
                    decay_ready.wait(dve, b, FT * n + (e + 2) % FT + 1)
                    if e == POOL:
                        dbu_ready.wait(dve, b, n + 1)
                    elif e == 0:
                        pool_dbu.wait(dve, b, n + 1)
                    scanned.inc(dve.tensor_tensor_scan(hbuf[:, n % 2, e, :], decay[:, n % 2, e, :], hbuf[:, n % 2, e, :],
                                                       0.0, ALU.mult, ALU.add))

                def add_y(n):
                    hc_ready.wait(dve, b, n + 1)
                    if n:
                        y_added.wait(dve, b, n)
                    else:
                        y_begun.wait(dve, b, 0)
                    y_added.inc(dve.tensor_tensor(yacc[:], yacc[:], hbuf[:, n % 2], ALU.add))

                for s in range(SN + 2):
                    if s < SN:
                        row_max(*divmod(s, ST))
                        n = s // 2
                        if s % 2 == 0:
                            make_dbu(n)
                            scan(n, 2)
                            scan(n, 3)
                        else:
                            scan(n, 0)
                            scan(n, 1)
                            if n >= 1:
                                add_y(n - 1)
                    if s % ST == 0 and 0 < s <= SN:
                        invert_sums(s // ST - 1)
                    if s - 1 in plan.tasks and plan.tasks[s - 1][2] == "dve":
                        task(b, plan, *plan.tasks[s - 1][:2])
                    if plan is inner and CONV <= s < CONV + 2 * FT and s % 2 == 0:
                        convolve(b, plan, (s - CONV) // 2)
                add_y(NS - 1)
                if plan is inner:
                    for k in range(4):
                        softplus(b, k)
                resid.wait(dve, b, 1)
                for i in range(ST):
                    wo_made.wait(dve, b, i + 1)
                    wo_added.inc(dve.tensor_tensor(xtok[:, i, :], xtok[:, i, :], wo_bank[i][:, :], ALU.add))
                    if plan is inner and i < 2:
                        softplus(b, 4 + i)

                def layer_norm(turn):
                    base = turn * (2 * ST + 1)
                    for i in range(ST):
                        if turn == 0:
                            wo_added.wait(dve, b, i + 1)
                        else:
                            pp_free["dve"].wait(dve, b, plan.count("gT", i))
                        ln_step.inc(dve.bn_stats(stats[:, i, :], xtok[:, i, :]))
                    ln_step.wait(dve, b, base + ST)
                    dve.sem_inc(stats_seen, 1)
                    for i in range(ST):
                        ln_step.inc(dve.bn_aggr(mv[:, i, :], stats[:, i, :]))
                    ln_step.wait(dve, b, base + 2 * ST)
                    ln_step.inc(dve.tensor_scalar(veps[:, :], mv[:, :, 1], 1e-5, None, ALU.add))
                    rstd_ready.wait(dve, b, turn + 1)
                    for i in range(ST):
                        who = x1_ready if turn == 0 else ln_step
                        who.inc(dve.tensor_scalar(xtok[:, i, :], xtok[:, i, :], mv[:, i, 0:1], rstd[:, i:i + 1], ALU.subtract, ALU.mult))

                layer_norm(0)
                y_added.wait(dve, b, NS)
                for e in range(FT):
                    gate_ready.wait(dve, b, e + 1)
                    g_ready.inc(dve.tensor_tensor(yacc[:, e, :], yacc[:, e, :], prob[:, 0, e, :], ALU.mult))
                for i in range(ST):
                    task(b, plan, "gT", i)
                layer_norm(1)

            for e in range(FT):
                convolve(None, first, e)
            for k in range(6):
                softplus(None, k)
            task(None, first, "next v", 0)
            run_batches(dve, batch)

        @block.gpsimd
        def _(pool):
            hc_ready.prime(pool)
            pads_ready.inc(pool.memset(mhalf[:], -0.5))
            pads_ready.inc(pool.memset(xin[:, :, 0:KC - 1], 0.0))
            pool.wait_ge(pads_ready.sem, 2)

            def make_dtu(b):
                sp_dve.wait(pool, b, 6)
                dtu_ready.inc(pool.tensor_tensor(dtu[:], dt[:], u[:], ALU.mult))

            def batch(b, plan):
                def make_dbu(n):
                    bc_in[n % 4].wait(pool, b, 16 * (n // 4 + 1))
                    y_added.wait(pool, b, max(n - 1, 0))
                    if n == 0:
                        dtu_ready.wait(pool, b, 0)
                    pool_dbu.inc(pool.tensor_tensor(hbuf[:, n % 2, 0:POOL], dtu[:, 0:POOL], bc[:, n % 4, 0:1, :].to_broadcast([P, POOL, S]), ALU.mult))

                make_dbu(0)
                for n in range(NS):
                    if n == RESID:
                        xtok_in.wait(pool, b, 16)
                        resid.inc(pool.tensor_tensor(xtok[:], xtok[:], bo_row[:, :].rearrange("p (o f) -> p o f", o=1).to_broadcast([P, ST, F]), ALU.add))
                    scanned.wait(pool, b, FT * (n + 1))
                    hc_ready.inc(pool.tensor_tensor(hbuf[:, n % 2], hbuf[:, n % 2], bc[:, n % 4, 1:2, :].to_broadcast([P, FT, S]), ALU.mult))
                    if n + 1 < NS:
                        make_dbu(n + 1)
                if plan is inner:
                    make_dtu(b)
                for turn in range(2):
                    base = turn * (2 * ST + 1)
                    ln_step.wait(pool, b, base + 2 * ST + 1)
                    rstd_ready.inc(pool.tensor_tensor(rstd[:, :], veps[:, :], mhalf[:, 0:ST], ALU.pow))

            make_dtu(None)
            run_batches(pool, batch)


def grouped_attention(nc, io, x2_dram, hidden_dram):
    B, S, F = io["x"].shape
    HD = P
    HQ = io["q_wT"].shape[1] // HD
    HK = io["k_wT"].shape[1] // HD
    QH = HQ // HK
    FT, ST = F // P, S // P
    EPS = 1e-6
    assert HK * HD == F and QH == ST == 4

    SN = HQ * ST
    EXP, TURN, WEIGH = 1, 6, 7
    tasks = {}
    for kv in range(HK):
        for i in range(ST):
            if kv + 1 < HK:
                tasks[16 * kv + 1 + 2 * i] = ("q", (kv + 1, i), "dve")
                tasks[16 * kv + 12 + i] = ("qT", (kv + 1, i), "act")
            tasks[16 * kv + 24 + i if kv + 1 < HK else SN + WEIGH + i] = ("o", (kv, i), "dve")
    ahead = {SN - ST + k: ("hT", k, "act") for k in range(FT)} | {SN + i: ("k", i, "dve") for i in range(ST)}
    SLOTS = SN + WEIGH + ST
    SQUARE = SN - 4 * ST
    assert FT == ST and not tasks.keys() & ahead.keys()

    begin = [("kT", h, "act") for h in range(HK)] + [("q", (0, i), "dve") for i in range(ST)]
    begin += [("v", i, "act") for i in range(ST)] + [("qT", (0, h), "act") for h in range(QH)]

    def plan_of(tasks):
        return Plan(begin + [tasks[s] for s in sorted(tasks)], tasks)

    first = Plan([ahead[s] for s in sorted(ahead)], {})
    inner = plan_of(tasks | ahead)
    final = plan_of(tasks)
    NPP = len(inner.uses)
    assert len(first.uses) % 2 == NPP % 2 == 0

    with ExitStack() as ctx:
        def sb(name, shape, dt=F32):
            return ctx.enter_context(nc.sbuf_tensor("p2_" + name, shape, dt))

        def sig(name, per=0, primed=False, base=0):
            return Signal(ctx.enter_context(nc.semaphore("p2_" + name)), per, primed, base)

        BF = mybir.dt.bfloat16
        q_w = sb("q_w", [P, FT, HQ * HD])
        k_w = sb("k_w", [P, FT, HK * HD])
        v_w = sb("v_w", [P, FT, HK * HD])
        o_w = sb("o_w", [P, HQ, F])
        norm_col = sb("norm_col", [P, FT])
        qn_row = sb("qn_row", [P, HD])
        kn_row = sb("kn_row", [P, HD])
        same = {c: sb(f"same_{c}", [P, ST, HD]) for c in "qk"}
        other = {c: sb(f"other_{c}", [P, ST, HD]) for c in "qk"}
        ident = sb("ident2", [P, P])
        ident_b = sb("ident_b", [P, P], BF)
        mask_b = sb("mask_b", [P, P], BF)
        mhalf = sb("mhalf2", [P, ST * QH])
        hid = sb("hid", [P, ST, F])
        hn = sb("hn", [P, ST, F])
        hT = sb("hT", [P, FT, S])
        v = sb("v2", [P, ST, HK * HD])
        kT = sb("kT2", [P, HK, S])
        square = sb("square", [P, 2, QH, HD])
        part = sb("part", [P, 2, QH, HD])
        cross = sb("cross", [P, 2, QH, HD])
        roped = sb("roped", [P, ST, QH, HD])
        qT = sb("qT2", [P, 2, QH, S])
        prob = sb("prob2", [P, 2, ST, S])
        cosf = prob[:, 0, :, 0:HD]
        sinf = prob[:, 0, :, HD:2 * HD]
        mask = prob[:, 1, 0, 0:HD]
        probT = sb("probT2", [P, ST, S])
        aT = sb("aT", [P, 8, S])
        ss = sb("ss", [P, ST])
        ssv = sb("ssv", [P, ST])
        hr = sb("hr", [P, ST])
        hsum = sb("hsum", [P, 3, ST, QH])
        heps = sb("heps", [P, 3, ST, QH])
        hinv = sb("hinv", [P, 3, ST, QH])
        nmax = sb("nmax2", [P, 2, ST])
        nbias = sb("nbias", [P, 2, ST])
        rsum = sb("rsum2", [P, 2, ST])
        rinv = sb("rinv2", [P, 2, ST])

        pp = [ctx.enter_context(nc.psum_tensor(f"p2_pp{i}", [P, 512], F32)) for i in range(2)]
        ps_s = [ctx.enter_context(nc.psum_tensor(f"p2_ps_s{i}", [P, 512], F32)) for i in range(3)]
        ps_t = [ctx.enter_context(nc.psum_tensor(f"p2_ps_t{i}", [P, 512], F32)) for i in range(2)]
        ps_o = [ctx.enter_context(nc.psum_tensor(f"p2_ps_o{i}", [P, 512], F32)) for i in range(1)]

        NG = HK + 1
        weights_in = {w: sig(f"weights_in_{w}") for w in "itkvqro"}
        consts_ready = sig("consts_ready2")
        tables_ready = sig("tables_ready")
        x2_in = sig("x2_in", 16)
        hn_in = sig("hn_in", 16, base=16)
        squared = sig("squared", ST, base=ST)
        eps_added = sig("eps_added", 1, base=1)
        hr_ready = sig("hr_ready", 1, base=1)
        hn_ready = sig("hn_ready", ST, base=ST)
        pp_ready = sig("pp_ready2", NPP, base=len(first.uses))
        pp_free = {who: sig(f"pp_free_{who}2", inner.emptied[who][-1], base=first.emptied[who][-1]) for who in ("act", "dve")}
        sq_ready = sig("sq_ready", ST * NG, base=ST)
        sum_ready = sig("sum_ready", ST * NG, base=ST)
        part_ready = sig("part_ready", 3 * ST * NG, base=3 * ST)
        hsum_ready = sig("hsum_ready", NG, base=1)
        hinv_ready = sig("hinv_ready", NG, base=1)
        roped_ready = sig("roped_ready", ST * NG, base=ST)
        k_normed = sig("k_normed", ST, base=ST)
        scores_ready = sig("scores_ready2", SN)
        max_ready = sig("max_ready2", SN)
        nbias_ready = sig("nbias_ready", SN)
        exp_ready = sig("exp_ready2", SN, primed=True)
        rinv_ready = sig("rinv_ready2", HQ)
        normed = sig("normed2", SN)
        turned = sig("turned2", SN)
        probT_ready = sig("probT_ready2", SN, primed=True)
        weighed = sig("weighed2", SN, primed=True)
        aT_ready = sig("aT_ready", HQ, primed=True)
        hidden_stored = sig("hidden_stored", 16, primed=True)
        QM = ST * HK

        def weights_here(engine, w):
            engine.wait_ge(weights_in[w].sem, weights_in[w].n)

        def run_batches(engine, batch):
            with engine.Fori(0, B - 1) as b:
                batch(b, inner)
            batch(B - 1, final)

        def settled(engine):
            engine.wait_ge(consts_ready.sem, 1)

        block = ctx.enter_context(nc.Block())

        @block.sync
        def _(sp):
            hidden_stored.prime(sp)
            def load(w, dst, src):
                weights_in[w].inc(sp.dma_start(dst, src), 16)

            def rows(name):
                return io[name].rearrange("(t p) n -> p t n", p=P)

            def load_hn(b):
                hn_in.inc(sp.dma_start(hn[:], x2_dram[b].rearrange("o (t p) f -> p (o t) f", p=P)), 16)

            load_hn(slice(0, 1))
            load("i", norm_col[:], io["attn_norm"])
            load("i", ident[:], io["ident"])
            load("k", k_w[:], rows("k_wT"))
            load("t", cosf, rows("cos"))
            load("t", sinf, rows("sin"))
            load("t", qn_row[:], io["q_norm"].to_broadcast([P, HD]))
            load("t", kn_row[:], io["k_norm"].to_broadcast([P, HD]))
            load("t", mask, io["mask"])
            for g in range(HK):
                load("r" if g else "q", q_w[:, :, 512 * g:512 * (g + 1)], rows("q_wT")[:, :, 512 * g:512 * (g + 1)])
                if g == 0:
                    load("v", v_w[:], rows("v_wT"))
            load("o", o_w[:], rows("o_wT"))

            def batch(b, plan):
                this = bass.ds(b, 1)
                hidden_stored.wait(sp, b, 0)
                settled(sp)
                x2_in.inc(sp.dma_start(hid[:], x2_dram[this].rearrange("o (t p) f -> p (o t) f", p=P)), 16)
                if plan is inner:
                    pp_ready.wait(sp, b, 0)
                    settled(sp)
                    load_hn(bass.ds(b + 1, 1))
                pp_free["dve"].wait(sp, b, plan.emptied["dve"][-1])
                settled(sp)
                hidden_stored.inc(sp.dma_start(hidden_dram[this].rearrange("o (t p) f -> p (o t) f", p=P), hid[:]), 16)

            run_batches(sp, batch)
            hidden_stored.wait_all(sp, 16 * B)

        @block.tensor
        def _(pe):
            weighed.prime(pe)

            def take(b, plan, what, key):
                n = plan.number[what, key]
                if n >= 2:
                    who = plan.uses[n - 2][2]
                    pp_free[who].wait(pe, b, plan.emptied[who][n - 1])
                elif b is not None:
                    for who in ("act", "dve"):
                        pp_free[who].wait(pe, b, 0)
                return pp[n % 2]

            def project(b, plan, what, key, i, w, c0):
                bank = take(b, plan, what, key)
                for k in range(FT):
                    mm = pe.matmul(bank[:, :], hT[:, k, i * P:(i + 1) * P], w[:, k, c0:c0 + 512],
                                   start=(k == 0), stop=(k == FT - 1))
                pp_ready.inc(mm)

            def turn_roped(b, plan, what, key, h):
                bank = take(b, plan, what, key)
                for i in range(ST):
                    mm = pe.transpose(bank[:, i * P:(i + 1) * P], roped[:, i, h, :], ident[:, :])
                pp_ready.inc(mm)

            def task(b, plan, what, key):
                if what == "hT":
                    if key == 0:
                        hn_ready.wait(pe, b, ST)
                    bank = take(b, plan, what, key)
                    for i in range(ST):
                        mm = pe.transpose(bank[:, i * P:(i + 1) * P], hn[:, i, key * P:(key + 1) * P], ident[:, :])
                    pp_ready.inc(mm)
                elif what == "k":
                    if key == 0:
                        pp_free["act"].wait(pe, b, plan.count("hT", FT - 1))
                    project(b, plan, what, key, key, k_w, 0)
                elif what == "q":
                    if key == (1, 0):
                        weights_here(pe, "r")
                    project(b, plan, what, key, key[1], q_w, 512 * key[0])
                elif what == "qT":
                    roped_ready.wait(pe, b, ST * (key[0] + 1))
                    turn_roped(b, plan, what, key, key[1])
                else:
                    kv, i = key
                    if key == (0, 0):
                        weights_here(pe, "o")
                    aT_ready.wait(pe, b, QH * (kv + 1))
                    bank = take(b, plan, what, key)
                    for hh in range(QH):
                        h = QH * kv + hh
                        mm = pe.matmul(bank[:, :], aT[:, h % 8, i * P:(i + 1) * P], o_w[:, h, :],
                                       start=(hh == 0), stop=(hh == QH - 1))
                    pp_ready.inc(mm)

            def batch(b, plan):
                k_normed.wait(pe, b, 0)
                for h in range(HK):
                    turn_roped(b, plan, "kT", h, h)
                weights_here(pe, "q")
                for i in range(ST):
                    task(b, plan, "q", (0, i))
                weights_here(pe, "v")
                for i in range(ST):
                    project(b, plan, "v", i, i, v_w, 0)
                for h in range(QH):
                    task(b, plan, "qT", (0, h))

                def score(g, i):
                    kv, hh = divmod(g, QH)
                    n = ST * g + i
                    exp_ready.wait(pe, b, max(n - 2, 0))
                    if i == 0:
                        pp_free["act"].wait(pe, b, plan.count("qT", (kv, hh)))
                    bank = ps_s[n % 3]
                    pe.matmul(bank[:, 0:(i + 1) * P], qT[:, kv % 2, hh, i * P:(i + 1) * P], kT[:, kv, 0:(i + 1) * P],
                              start=True, stop=False)
                    scores_ready.inc(pe.matmul(bank[:, i * P:(i + 1) * P], ident_b[:, :], mask_b[:, :], start=False, stop=True))

                def turn(g, j):
                    n = ST * g + j
                    probT_ready.wait(pe, b, max(n - 1, 0))
                    if j == 0:
                        normed.wait(pe, b, ST * (g + 1))
                    for i in range(j, ST):
                        mm = pe.transpose(ps_t[n % 2][:, i * P:(i + 1) * P], prob[:, g % 2, i, j * P:(j + 1) * P], ident[:, :])
                    turned.inc(mm)

                def weigh(g, j):
                    kv = g // QH
                    if j == 0:
                        aT_ready.wait(pe, b, g)
                    probT_ready.wait(pe, b, ST * g + j + 1)
                    weighed.inc(pe.matmul(ps_o[0][:, j * P:], v[:, j, kv * HD:(kv + 1) * HD], probT[:, j, j * P:],
                                          start=(j == 0), stop=(j == ST - 1)))

                for s in range(SLOTS):
                    if s < SN:
                        score(*divmod(s, ST))
                    if s in plan.tasks:
                        task(b, plan, *plan.tasks[s][:2])
                    if TURN <= s < SN + TURN:
                        turn(*divmod(s - TURN, ST))
                    if WEIGH <= s < SN + WEIGH:
                        weigh(*divmod(s - WEIGH, ST))

            weights_here(pe, "i")
            for what, key, _ in first.uses:
                if (what, key) == ("k", 0):
                    weights_here(pe, "k")
                task(None, first, what, key)
            run_batches(pe, batch)

        @block.scalar
        def _(act):
            exp_ready.prime(act)
            probT_ready.prime(act)
            aT_ready.prime(act)

            def square_rows(b, i):
                if i == 0:
                    hn_in.wait(act, b, 16)
                    if b is not None:
                        sum_ready.wait(act, b, QM)
                else:
                    squared.wait(act, b, i)
                squared.inc(act.activation(square[:, i % 2].rearrange("p h d -> p (h d)"), hn[:, i, :], ACT.Square,
                                           accum_out=ss[:, i:i + 1]))

            def empties(b, plan, what, key, dst, **kw):
                n = plan.number[what, key]
                pp_ready.wait(act, b, n + 1)
                pp_free["act"].inc(act.activation(dst, pp[n % 2][:, :], **kw))

            def square_heads(b, plan, what, key, m):
                n = plan.number[what, key]
                pp_ready.wait(act, b, n + 1)
                if what == "k" and key == 0:
                    squared.wait(act, b, ST)
                if b is not None or m >= 2:
                    sum_ready.wait(act, b, m - 1)
                sq_ready.inc(act.activation(square[:, m % 2].rearrange("p h d -> p (h d)"), pp[n % 2][:, :], ACT.Square))

            def task(b, plan, what, key):
                if what == "hT":
                    empties(b, plan, what, key, hT[:, key, :], func=ACT.Copy, scale=norm_col[:, key:key + 1])
                elif what == "k":
                    square_heads(b, plan, what, key, key if b is None else QM + key)
                elif what == "q":
                    square_heads(b, plan, what, key, ST * key[0] + key[1])
                elif what == "qT":
                    empties(b, plan, what, key, qT[:, key[0] % 2, key[1], :], func=ACT.Copy)

            def batch(b, plan):
                for h in range(HK):
                    empties(b, plan, "kT", h, kT[:, h, :], func=ACT.Copy)
                for i in range(ST):
                    task(b, plan, "q", (0, i))
                for i in range(ST):
                    empties(b, plan, "v", i, v[:, i, :], func=ACT.Copy)
                for h in range(QH):
                    task(b, plan, "qT", (0, h))

                def exp_scores(g, i):
                    n = ST * g + i
                    kv, hh = divmod(g, QH)
                    nbias_ready.wait(act, b, n + 1)
                    exp_ready.inc(act.activation(prob[:, g % 2, i, 0:(i + 1) * P], ps_s[n % 3][:, 0:(i + 1) * P], ACT.Exp,
                                                 bias=nbias[:, g % 2, i:i + 1], scale=hinv[:, kv % 2, i, hh:hh + 1],
                                                 accum_out=rsum[:, g % 2, i:i + 1]))

                def copy_turned(g, j):
                    n = ST * g + j
                    turned.wait(act, b, n + 1)
                    weighed.wait(act, b, max(n - ST + 1, 0))
                    probT_ready.inc(act.activation(probT[:, j, j * P:], ps_t[n % 2][:, j * P:], ACT.Copy))

                for s in range(SLOTS):
                    g, i = divmod(s - WEIGH - ST, ST)
                    if i == 0 and 0 <= g < HQ:
                        weighed.wait(act, b, ST * (g + 1))
                        aT_ready.inc(act.activation(aT[:, g % 8, :], ps_o[0][:, :], ACT.Copy))
                    if EXP <= s < SN + EXP:
                        exp_scores(*divmod(s - EXP, ST))
                    if TURN <= s < SN + TURN:
                        copy_turned(*divmod(s - TURN, ST))
                    if plan is inner and SQUARE <= s < SQUARE + ST:
                        square_rows(b, s - SQUARE)
                    if s in plan.tasks:
                        task(b, plan, *plan.tasks[s][:2])

            weights_here(act, "i")
            for i in range(ST):
                square_rows(None, i)
            for what, key, _ in first.uses:
                task(None, first, what, key)
            run_batches(act, batch)

        @block.vector
        def _(dve):
            consts_ready.inc(dve.memset(mhalf[:], -0.5))

            def sum_up(b):
                squared.wait(dve, b, ST)
                eps_added.inc(dve.tensor_scalar(ssv[:, :], ss[:, :], 1.0 / F, EPS, ALU.mult, ALU.add))

            def norm_rows(b):
                hr_ready.wait(dve, b, 1)
                for i in range(ST):
                    hn_ready.inc(dve.tensor_scalar(hn[:, i, :], hn[:, i, :], hr[:, i:i + 1], None, ALU.mult))

            weights_here(dve, "i")
            sum_up(None)
            norm_rows(None)
            weights_here(dve, "t")
            H2 = HD // 2
            for c, row in (("q", qn_row), ("k", kn_row)):
                def weight(a, z):
                    return row[:, a:z].rearrange("p (o d) -> p o d", o=1).to_broadcast([P, ST, z - a])
                tables_ready.inc(dve.tensor_tensor(same[c][:], cosf, weight(0, HD), ALU.mult))
                tables_ready.inc(dve.tensor_tensor(other[c][:, :, 0:H2], sinf[:, :, 0:H2], weight(H2, HD), ALU.mult))
                tables_ready.inc(dve.tensor_tensor(other[c][:, :, H2:], sinf[:, :, H2:], weight(0, H2), ALU.mult))
            tables_ready.inc(dve.tensor_copy(ident_b[:, :], ident[:, :]))
            tables_ready.inc(dve.tensor_copy(mask_b[:, :], mask))
            dve.wait_ge(tables_ready.sem, tables_ready.n)

            def rope(b, plan, c, key, i, m, group, place):
                n = plan.number[c, key]
                bank = pp[n % 2][:, :].rearrange("p (h d) -> p h d", h=QH)

                def table(t, a, z):
                    return t[c][:, i:i + 1, a:z].to_broadcast([P, QH, z - a])

                sq_ready.wait(dve, b, m + 1)
                if b is not None or m >= 2:
                    roped_ready.wait(dve, b, m - 1)
                part_ready.inc(dve.tensor_tensor(cross[:, m % 2, :, 0:H2], bank[:, :, H2:], table(other, 0, H2), ALU.mult))
                part_ready.inc(dve.tensor_tensor(cross[:, m % 2, :, H2:], bank[:, :, 0:H2], table(other, H2, HD), ALU.mult))
                pp_free["dve"].inc(dve.tensor_tensor(part[:, m % 2], bank, table(same, 0, HD), ALU.mult))
                sum_ready.inc(dve.tensor_reduce(hsum[:, place, i, :], square[:, m % 2], AX.X, ALU.add))
                if i == ST - 1:
                    sum_ready.wait(dve, b, m + 1)
                    mul, add = (1.0 / HD, EPS) if c == "k" else (1.0, HD * EPS)
                    hsum_ready.inc(dve.tensor_scalar(heps[:, place], hsum[:, place], mul, add, ALU.mult, ALU.add))

            def norm_keys(b, m0, group):
                hinv_ready.wait(dve, b, group + 1)
                for i in range(ST):
                    roped_ready.wait(dve, b, m0 + i + 1)
                    k_normed.inc(dve.tensor_tensor(
                        roped[:, i], roped[:, i],
                        hinv[:, 2, i, :].rearrange("p (h o) -> p h o", o=1).to_broadcast([P, QH, HD]), ALU.mult))

            def rope_queries(b, plan, key):
                rope(b, plan, "q", key, key[1], ST * key[0] + key[1], key[0], key[0] % 2)

            def batch(b, plan):
                for i in range(ST):
                    rope_queries(b, plan, (0, i))

                def row_max(g, i):
                    n = ST * g + i
                    kv, hh = divmod(g, QH)
                    scores_ready.wait(dve, b, n + 1)
                    max_ready.inc(dve.tensor_reduce(nmax[:, g % 2, i:i + 1], ps_s[n % 3][:, 0:(i + 1) * P], AX.X, ALU.max, negate=True))
                    if i == 0 and hh == 0:
                        hinv_ready.wait(dve, b, kv + 1)
                    max_ready.wait(dve, b, n + 1)
                    nbias_ready.inc(dve.tensor_tensor(nbias[:, g % 2, i:i + 1], nmax[:, g % 2, i:i + 1],
                                                      hinv[:, kv % 2, i, hh:hh + 1], ALU.mult))

                def normalise(g):
                    exp_ready.wait(dve, b, ST * (g + 1))
                    rinv_ready.inc(dve.reciprocal(rinv[:, g % 2, :], rsum[:, g % 2, :]))
                    rinv_ready.wait(dve, b, g + 1)
                    for i in range(ST):
                        block_ = prob[:, g % 2, i, 0:(i + 1) * P]
                        normed.inc(dve.tensor_scalar(block_, block_, rinv[:, g % 2, i:i + 1], None, ALU.mult))

                def task(what, key):
                    if what == "o":
                        kv, i = key
                        n = plan.number[what, key]
                        pp_ready.wait(dve, b, n + 1)
                        if kv:
                            pp_free["dve"].wait(dve, b, plan.count(what, (kv - 1, i)))
                        else:
                            x2_in.wait(dve, b, 16)
                        pp_free["dve"].inc(dve.tensor_tensor(hid[:, i, :], hid[:, i, :], pp[n % 2][:, :], ALU.add))
                    elif what == "q":
                        rope_queries(b, plan, key)
                    elif what == "k":
                        rope(b, plan, "k", key, key, QM + key, HK, 2)

                for s in range(SLOTS + 1):
                    if s < SN:
                        row_max(*divmod(s, ST))
                    if s % ST == EXP and ST <= s <= SN + EXP:
                        normalise(s // ST - 1)
                    if plan is inner and s == SQUARE + ST:
                        sum_up(b)
                    if plan is inner and s == SQUARE + ST + 2:
                        norm_rows(b)
                    if s - 1 in plan.tasks:
                        task(*plan.tasks[s - 1][:2])
                    if plan is inner and s == SN + ST + 2:
                        norm_keys(b, QM, HK)

            for i in range(ST):
                rope(None, first, "k", i, i, i, 0, 2)
            norm_keys(None, 0, 0)
            run_batches(dve, batch)

        @block.gpsimd
        def _(pool):
            pool.wait_ge(consts_ready.sem, 1)

            def invert_rows(b):
                eps_added.wait(pool, b, 1)
                hr_ready.inc(pool.tensor_tensor(hr[:, :], ssv[:, :], mhalf[:, 0:ST], ALU.pow))

            def add_parts(b, plan, what, key, i, m):
                pp_free["dve"].wait(pool, b, plan.count(what, key))
                roped_ready.inc(pool.tensor_tensor(roped[:, i], part[:, m % 2], cross[:, m % 2], ALU.add))

            def invert_heads(b, group, place):
                hsum_ready.wait(pool, b, group + 1)
                hinv_ready.inc(pool.tensor_tensor(hinv[:, place].rearrange("p t h -> p (t h)"),
                                                  heps[:, place].rearrange("p t h -> p (t h)"), mhalf[:, :], ALU.pow))

            def batch(b, plan):
                for kv in range(HK):
                    pp_ready.wait(pool, b, plan.number[("qT", (kv - 1, QH - 1)) if kv else ("kT", HK - 1)] + 1)
                    for i in range(ST):
                        add_parts(b, plan, "q", (kv, i), i, ST * kv + i)
                    invert_heads(b, kv, kv % 2)
                if plan is inner:
                    invert_rows(b)
                    pp_ready.wait(pool, b, plan.number["qT", (HK - 1, QH - 1)] + 1)
                    for i in range(ST):
                        add_parts(b, plan, "k", i, i, QM + i)
                    invert_heads(b, HK, 2)

            invert_rows(None)
            for i in range(ST):
                add_parts(None, first, "k", i, i, i)
            invert_heads(None, 0, 2)
            run_batches(pool, batch)


def mixture_of_experts(nc, io, x2_dram, hidden_dram, out):
    B, S, F = io["x"].shape
    E = io["gate_wT"].shape[1]
    I = io["wgT"].shape[2]
    FT, ST = F // P, S // P
    NT = B * ST
    J = 2 * NT
    NP = -(-(J * P + E * (P - 1)) // P)
    NP += NP % 2
    IT = -(-I // P)
    IL = I - (IT - 1) * P
    EPS = 1e-6
    AHEAD = 1
    RING = 8
    U32, F16 = mybir.dt.uint32, mybir.dt.float16
    assert E == 8 and I <= 512 and NP <= P and B * S <= 2048

    hn_dram = nc.dram_tensor("hn_rows", (B * S, F), F32, kind="Internal").ap()
    y_dram = nc.dram_tensor("expert_rows", (NP * P, F), F32, kind="Internal").ap()

    with ExitStack() as ctx:
        def sb(name, shape, dt=F32):
            return ctx.enter_context(nc.sbuf_tensor("p3_" + name, shape, dt))

        def sig(name, per=0, primed=False):
            return Signal(ctx.enter_context(nc.semaphore("p3_" + name)), per, primed)

        gate_w = sb("gate_w", [P, FT, E])
        norm_col = sb("norm_col3", [P, FT])
        ident = sb("ident3", [P, P])
        before = sb("before", [P, P])
        ones = sb("ones", [P, P])
        expert_no = sb("expert_no", [P, E])
        place_no = sb("place_no", [P, P])
        token_no = sb("token_no", [P, J])
        new_expert = sb("new_expert", [P, E * J])
        mhalf = sb("mhalf3", [P, NT])
        wg = sb("wg_sb", [P, E * FT * I])
        wu = sb("wu_sb", [P, E * FT * I])
        wd = sb("wd_sb", [P, E * IT * F])
        hbuf = sb("hbuf3", [P, 2, ST, F])
        hn = sb("hn3", [P, ST, F])
        acc = sb("acc", [P, NT, F])
        hT = sb("hT3", [P, FT, S])
        ss = sb("ss3", [P, NT])
        ssv = sb("ssv3", [P, NT])
        hr = sb("hr3", [P, NT])
        logits = sb("logits", [P, NT, E])
        top = sb("top", [P, NT, 8])
        topi = sb("topi", [P, NT, 8], U32)
        topf = sb("topf", [P, 2, NT])
        small = sb("small", [P, 8, NT])
        per_expert = sb("per_expert", [P, 4, E])
        pos = sb("pos", [P, J])
        pos_u = sb("pos_u", [P, J], U32)
        pos_hi = sb("pos_hi", [P, J], U32)
        pos_lo = sb("pos_lo", [P, J], U32)
        tile_of = sb("tile_of", [P, J])
        row_of = sb("row_of", [P, J])
        expert_f = sb("expert_f", [1, NP])
        expert_of = sb("expert_of", [1, NP], U32)
        token_of = sb("token_of", [P, NP], U32)
        rows_of = [sb(f"rows_of{i}", [P, 1], U32) for i in range(2)]
        stats = sb("stats3", [P, ST, 6])
        mv = sb("mv3", [P, NT, 2])
        veps = sb("veps3", [P, NT])
        rstd = sb("rstd3", [P, NT])
        spare = {"hbuf": hbuf[:].rearrange("p a t f -> p (a t f)"), "hT": hT[:].rearrange("p k s -> p (k s)"),
                 "hn": hn[:].rearrange("p t f -> p (t f)")}

        def carved(name, n, width):
            got, spare[name] = spare[name][:, 0:n * width], spare[name][:, n * width:]
            return got.rearrange("p (n w) -> p n w", w=width)

        row_hot = spare["hbuf"].bitcast(F16)[:, 0:J * P].rearrange("p (j r) -> p j r", r=P)
        tile_hot = spare["hT"].bitcast(F16)[:, 0:J * NP].rearrange("p (j t) -> p j t", t=NP)
        xg = carved("hbuf", 2, F)
        xT = carved("hbuf", 2, F)
        y_row = carved("hbuf", 2, F)
        silu = carved("hbuf", 2, I)
        chosen = carved("hn", E, J)
        upto = carved("hn", E, J)
        shifted = carved("hn", NT, E)
        begun = carved("hn", E, NT)
        ended = carved("hn", NP, E)[0:1]
        act_row = carved("hT", 2, I)
        actT = carved("hT", 2, IT * P)
        results = hbuf[:].rearrange("p a t f -> p (a t) f")
        assert 2 * ST == RING and J * P <= 2 * ST * F and J * NP <= FT * S

        ps_g = [ctx.enter_context(nc.psum_tensor(f"p3_ps_g{i}", [P, 512], F32)) for i in range(2)]
        ps_u = [ctx.enter_context(nc.psum_tensor(f"p3_ps_u{i}", [P, 512], F32)) for i in range(2)]
        ps_x = ctx.enter_context(nc.psum_tensor("p3_ps_x", [P, 512], F32))
        ps_l = ps_g + ps_u
        assert B == len(ps_l)
        square = ps_x
        ps_a = ctx.enter_context(nc.psum_tensor("p3_ps_a", [P, 512], F32))
        ps_d = [ctx.enter_context(nc.psum_tensor(f"p3_ps_d{i}", [P, 512], F32)) for i in range(2)]

        small_in = sig("small_in")
        weights_in = sig("weights_in3")
        down_in = sig("down_in")
        hidden_in = [sig(f"hidden_in{i}") for i in range(2)]
        acc_in = [sig(f"acc_in{c}") for c in range(B)]
        hn_stored = [sig(f"hn_stored{i}") for i in range(2)]
        consts_ready = sig("consts_ready3")
        squared = sig("squared3")
        eps_added = sig("eps_added3")
        hr_ready = sig("hr_ready3")
        acc_begun = sig("acc_begun")
        hn_ready = sig("hn_ready3")
        turned_in = sig("turned_in")
        hT_ready = sig("hT_ready")
        logits_made = sig("logits_made")
        logits_ready = sig("logits_ready")
        exp_ready = sig("exp_ready3")
        route = sig("route")
        chosen_ready = sig("chosen_ready")
        counted = sig("counted")
        hots_ready = sig("hots_ready")
        placed = sig("placed")
        table_ready = sig("table_ready")
        rows_copied = sig("rows_copied", 2)
        rows_seen = sig("rows_seen", 2)
        gathered = [sig(f"gathered{i}", 16) for i in range(2)]
        x_turned = sig("x_turned", 2)
        xT_ready = sig("xT_ready3", 2)
        gate_made = sig("gate_made", 2)
        up_made = sig("up_made", 2)
        silu_ready = sig("silu_ready", 2)
        row_ready = sig("row_ready", 2)
        act_turned = sig("act_turned", 2)
        actT_ready = sig("actT_ready", 4)
        down_made = sig("down_made", 2)
        y_ready = sig("y_ready", 2)
        y_stored = [sig(f"y_stored{i}", 16) for i in range(2)]
        result_in = [sig(f"result_in{i}") for i in range(RING)]
        added = sig("added3")
        ln_step = sig("ln_step3")
        rstd_ready = sig("rstd_ready3")
        out_ready = sig("out_ready")
        out_stored = sig("out_stored")

        def tile_done(engine, signal, turn, k):
            value = (k + 1) * signal.per // 2
            if isinstance(turn, int) and turn * signal.per + value <= 0:
                return
            engine.wait_ge(signal.sem, turn * signal.per + value)

        def ring_done(engine, signals, turn, k):
            value = (k // 2 + 1) * 16
            if isinstance(turn, int) and turn * 16 + value <= 0:
                return
            engine.wait_ge(signals[k % 2].sem, turn * 16 + value)

        def run_tiles(engine, turn):
            turn(0, True, False)
            with engine.Fori(1, NP // 2 - 1) as ee:
                turn(ee, False, False)
            turn(NP // 2 - 1, False, True)

        def at(turn, k, width=1):
            if isinstance(turn, int):
                return slice((2 * turn + k) * width, (2 * turn + k + 1) * width)
            return bass.ds(turn * (2 * width) + k * width, width)

        block = ctx.enter_context(nc.Block())

        @block.sync
        def _(sp):
            def load_hidden(c):
                if c >= 2:
                    sp.wait_ge(hn_ready.sem, ST * (c - 1))
                    sp.wait_ge(acc_begun.sem, c - 1)
                hidden_in[c % 2].inc(sp.dma_start(hbuf[:, c % 2], hidden_dram[c].rearrange("(t p) f -> p t f", p=P)), 16)

            def load_x2(c):
                acc_in[c].inc(sp.dma_start(acc[:, ST * c:ST * (c + 1), :], x2_dram[c].rearrange("(t p) f -> p t f", p=P)), 16)

            def load_in(w, name, e):
                weights_in.inc(sp.dma_start(w[:, e * FT * I:(e + 1) * FT * I].rearrange("p (t i) -> p t i", i=I),
                                            io[name][e].rearrange("(t p) i -> p t i", p=P)), 16)

            load_hidden(0)
            for dst, src in ((gate_w[:], io["gate_wT"].rearrange("(t p) e -> p t e", p=P)), (norm_col[:], io["ffn_norm"]),
                             (ident[:], io["ident"]), (before[:], io["before"]), (token_no[:], io["token_no"]),
                             (expert_no[:], io["place_no"][:, 0:E].to_broadcast([P, E])),
                             (place_no[:], io["place_no"].to_broadcast([P, P])),
                             (new_expert[:], io["new_expert"].to_broadcast([P, E * J]))):
                small_in.inc(sp.dma_start(dst, src), 16)
            load_x2(0)
            load_hidden(1)
            load_x2(1)
            rest = [(w, name, e) for w, name in ((wg, "wgT"), (wu, "wuT")) for e in range(E)]
            for c in range(2, B):
                load_hidden(c)
                load_x2(c)
                for _ in range(AHEAD):
                    load_in(*rest.pop(0))
            sp.wait_ge(hn_ready.sem, B * ST)
            while rest:
                load_in(*rest.pop(0))
            for e in range(E):
                if e == 0:
                    sp.wait_ge(weights_in.sem, weights_in.n)
                wd_e = wd[:, e * IT * F:(e + 1) * IT * F].rearrange("p (t f) -> p t f", f=F)
                down_in.inc(sp.dma_start(wd_e[:, 0:IT - 1], io["wdT"][e, 0:(IT - 1) * P].rearrange("(t p) f -> p t f", p=P)), 16)
                down_in.inc(sp.dma_start(wd_e[0:IL, IT - 1], io["wdT"][e, (IT - 1) * P:]), 16)

            def turn(ee, first, last):
                for q in range(2):
                    tile_done(sp, y_ready, ee, q)
                    sp.dma_start(y_dram[at(ee, q, P)], y_row[:, q, :]).then_inc(y_stored[q].sem, 16)

            run_tiles(sp, turn)
            for c in range(B):
                sp.wait_ge(out_ready.sem, ST * (c + 1))
                out_stored.inc(sp.dma_start(out[c].rearrange("(t p) f -> p t f", p=P), acc[:, ST * c:ST * (c + 1), :]), 16)
            sp.wait_ge(out_stored.sem, out_stored.n)

        @block.tensor
        def _(pe):
            pe.wait_ge(small_in.sem, small_in.n)
            for c in range(B):
                pe.wait_ge(hn_ready.sem, ST * (c + 1))
                for k in range(FT):
                    n = FT * c + k
                    if n >= 2:
                        pe.wait_ge(hT_ready.sem, n - 1)
                    for i in range(ST):
                        mm = pe.transpose(ps_d[n % 2][:, i * P:(i + 1) * P], hn[:, i, k * P:(k + 1) * P], ident[:, :])
                    turned_in.inc(mm)
                pe.wait_ge(hT_ready.sem, FT * (c + 1))
                for i in range(ST):
                    t = ST * c + i
                    for k in range(FT):
                        mm = pe.matmul(ps_l[c][:, i * E:(i + 1) * E], hT[:, k, i * P:(i + 1) * P], gate_w[:, k, :],
                                       start=(k == 0), stop=(k == FT - 1))
                logits_made.inc(mm)
            pe.wait_ge(chosen_ready.sem, 1)
            flat = chosen[:].rearrange("p e j -> p (e j)")
            pe.matmul(ps_u[0][:, 0:E * J], before[:, :], flat, start=True, stop=True)
            counted.inc(pe.matmul(ps_u[1][:, 0:E * J], ones[:, :], flat, start=True, stop=True))
            for j in range(J):
                if j % NT == 0:
                    pe.wait_ge(hots_ready.sem, 2 + j // NT)
                mm = pe.matmul(ps_d[0][:, 0:NP], row_hot[:, j, :], tile_hot[:, j, :], start=(j == 0), stop=(j == J - 1))
            placed.inc(mm)
            pe.wait_ge(weights_in.sem, weights_in.n)
            pe.wait_ge(table_ready.sem, 2)

            def expert(ee, k):
                return pe.value_load(expert_of[0:1, at(ee, k)], min_val=0, max_val=E - 1)

            def turn_x(ee, k):
                ring_done(pe, gathered, ee, k)
                tile_done(pe, xT_ready, ee, k - 1)
                for j in range(FT):
                    mm = pe.transpose(ps_x[:, j * P:(j + 1) * P], xg[:, k % 2, j * P:(j + 1) * P], ident[:, :])
                mm.then_inc(x_turned.sem, 1)

            def project(bank, w, e, q):
                for j in range(FT):
                    mm = pe.matmul(bank[:, 0:I], xT[:, q, j * P:(j + 1) * P], w[:, bass.ds(e * (FT * I) + j * I, I)],
                                   start=(j == 0), stop=(j == FT - 1))
                return mm

            def turn_act(ee, k):
                tile_done(pe, row_ready, ee, k)
                tile_done(pe, actT_ready, ee, k - 1)
                for j in range(IT):
                    w = P if j < IT - 1 else IL
                    mm = pe.transpose(ps_a[0:w, j * P:(j + 1) * P], act_row[:, k % 2, j * P:j * P + w], ident[:, :])
                mm.then_inc(act_turned.sem, 1)

            def down(ee, k, e):
                tile_done(pe, actT_ready, ee, k)
                tile_done(pe, y_ready, ee, k - 2)
                for j in range(IT):
                    w = P if j < IT - 1 else IL
                    mm = pe.matmul(ps_d[k % 2][:, :], actT[0:w, k % 2, j * P:(j + 1) * P], wd[0:w, bass.ds(e * (IT * F) + j * F, F)],
                                   start=(j == 0), stop=(j == IT - 1))
                mm.then_inc(down_made.sem, 1)

            def turn(ee, first, last):
                for q in range(2):
                    e = expert(ee, q)
                    e_last = None if first and q == 0 else expert(ee, q - 1)
                    tile_done(pe, xT_ready, ee, q)
                    tile_done(pe, silu_ready, ee, q - 2)
                    project(ps_g[q], wg, e, q).then_inc(gate_made.sem, 1)
                    if e_last is not None:
                        turn_act(ee, q - 1)
                    if not (last and q == 1):
                        turn_x(ee, q + 1)
                    tile_done(pe, row_ready, ee, q - 2)
                    project(ps_u[q], wu, e, q).then_inc(up_made.sem, 1)
                    if first and q:
                        pe.wait_ge(down_in.sem, down_in.n)
                    if e_last is not None:
                        down(ee, q - 1, e_last)
                if last:
                    turn_act(ee, 1)
                    down(ee, 1, e)

            turn_x(0, 0)
            run_tiles(pe, turn)

        @block.scalar
        def _(act):
            def square_rows(c):
                act.wait_ge(hidden_in[c % 2].sem, 16 * (c // 2 + 1))
                for i in range(ST):
                    if squared.n:
                        act.wait_ge(squared.sem, squared.n)
                    squared.inc(act.activation(square[:, :], hbuf[:, c % 2, i, :], ACT.Square, accum_out=ss[:, ST * c + i:ST * c + i + 1]))

            square_rows(0)
            act.wait_ge(small_in.sem, small_in.n)
            for c in range(B):
                if c + 1 < B:
                    square_rows(c + 1)
                act.wait_ge(hn_ready.sem, ST * (c + 1))
                hn_stored[c % 2].inc(act.dma_start(hn_dram[S * c:S * (c + 1)].rearrange("(t p) f -> p t f", p=P), hn[:]), 16)
                if c:
                    act.wait_ge(logits_made.sem, c)
                for k in range(FT):
                    n = FT * c + k
                    act.wait_ge(turned_in.sem, n + 1)
                    hT_ready.inc(act.activation(hT[:, k, :], ps_d[n % 2][:, :], ACT.Copy, scale=norm_col[:, k:k + 1]))
            act.wait_ge(route.sem, 1)
            exp_ready.inc(act.activation(small[:, 1, :], small[:, 0, :], ACT.Exp))
            exp_ready.inc(act.activation(shifted[:], shifted[:], ACT.Exp))

            def keep_y(ee, k):
                tile_done(act, down_made, ee, k)
                ring_done(act, y_stored, ee, k - 2)
                act.activation(y_row[:, k % 2, :], ps_d[k % 2][:, :], ACT.Copy).then_inc(y_ready.sem, 1)

            def keep_actT(ee, k):
                q = k % 2
                tile_done(act, act_turned, ee, k)
                tile_done(act, down_made, ee, k - 2)
                act.activation(actT[:, q, 0:(IT - 1) * P], ps_a[:, 0:(IT - 1) * P], ACT.Copy).then_inc(actT_ready.sem, 1)
                act.activation(actT[0:IL, q, (IT - 1) * P:], ps_a[0:IL, (IT - 1) * P:IT * P], ACT.Copy).then_inc(actT_ready.sem, 1)

            def turn(ee, first, last):
                for q in range(2):
                    if not first:
                        keep_y(ee, q - 2)
                    tile_done(act, gate_made, ee, q)
                    tile_done(act, row_ready, ee, q - 2)
                    act.activation(silu[:, q, :], ps_g[q][:, 0:I], ACT.Silu).then_inc(silu_ready.sem, 1)
                    if not (first and q == 0):
                        keep_actT(ee, q - 1)
                if last:
                    keep_y(ee, 0)
                    keep_actT(ee, 1)
                    keep_y(ee, 1)

            run_tiles(act, turn)

        @block.vector
        def _(dve):
            consts_ready.inc(dve.memset(mhalf[:], -0.5))
            consts_ready.inc(dve.memset(ones[:], 1.0))

            def step(signal, instruction):
                signal.inc(instruction)
                dve.wait_ge(signal.sem, signal.n)

            def best_two(c):
                own = slice(ST * c, ST * (c + 1))
                dve.wait_ge(logits_made.sem, c + 1)
                step(logits_ready, dve.tensor_copy(logits[:, own].rearrange("p t e -> p (t e)"), ps_l[c][:, 0:ST * E]))
                for t in range(ST * c, ST * (c + 1)):
                    logits_ready.inc(dve.max(top[:, t, :], logits[:, t, :]))
                dve.wait_ge(logits_ready.sem, logits_ready.n)
                for t in range(ST * c, ST * (c + 1)):
                    logits_ready.inc(dve.max_index(topi[:, t, :], top[:, t, :], logits[:, t, :]))
                dve.wait_ge(logits_ready.sem, logits_ready.n)

            for c in range(B):
                own = slice(ST * c, ST * (c + 1))
                dve.wait_ge(squared.sem, ST * (c + 1))
                eps_added.inc(dve.tensor_scalar(ssv[:, own], ss[:, own], 1.0 / F, EPS, ALU.mult, ALU.add))
                if c:
                    dve.wait_ge(turned_in.sem, FT * c)
                    dve.wait_ge(hn_stored[(c - 1) % 2].sem, 16 * ((c - 1) // 2 + 1))
                dve.wait_ge(hr_ready.sem, c + 1)
                for i in range(ST):
                    hn_ready.inc(dve.tensor_scalar(hn[:, i, :], hbuf[:, c % 2, i, :], hr[:, ST * c + i:ST * c + i + 1], None, ALU.mult))
                if c:
                    best_two(c - 1)
            best_two(B - 1)
            dve.wait_ge(small_in.sem, small_in.n)

            def wide(ap, n):
                return ap.rearrange("p (t o) -> p t o", o=1).to_broadcast([ap.shape[0], ap.shape[1], n])

            def tall(ap, n):
                return ap.rearrange("p (o t) -> p o t", o=1).to_broadcast([ap.shape[0], n, ap.shape[1]])

            for stored in hn_stored:
                dve.wait_ge(stored.sem, 16 * (B // 2))
            step(logits_ready, dve.tensor_copy(topf[:], topi[:, :, 0:2].rearrange("p t k -> p k t")))
            chosen_ready.inc(dve.tensor_tensor(chosen[:], wide(expert_no[:, :], J), tall(topf[:].rearrange("p k t -> p (k t)"), E), ALU.is_equal))

            def row(k):
                return small[:, k, :]

            step(logits_ready, dve.tensor_tensor(shifted[:], logits[:], wide(top[:, :, 0], E), ALU.subtract))
            step(route, dve.tensor_tensor(row(0), top[:, :, 1], top[:, :, 0], ALU.subtract))
            dve.wait_ge(counted.sem, 1)
            ranks = ps_u[0][:, 0:E * J].rearrange("p (e j) -> p e j", j=J)
            counts = ps_u[1][:, 0:E * J].rearrange("p (e j) -> p e j", j=J)
            step(route, dve.tensor_tensor_scan(upto[:].rearrange("p e j -> p (e j)"), new_expert[:], ps_u[1][:, 0:E * J], 0.0, ALU.mult, ALU.add))
            step(route, dve.tensor_scalar(per_expert[:, 0, :], upto[:, :, J - 1], 1.0 / P, None, ALU.mult))
            step(route, dve.tensor_tensor(begun[:], wide(per_expert[:, 0, :], NT), tall(place_no[:, 0:NT], E), ALU.is_gt))
            step(route, dve.tensor_reduce(per_expert[:, 1, :], begun[:], AX.X, ALU.add))
            step(route, dve.tensor_tensor_scan(per_expert[:, 2, :], new_expert[:, 0:E], per_expert[:, 1, :], 0.0, ALU.mult, ALU.add))
            step(route, dve.tensor_tensor(per_expert[:, 3, :], per_expert[:, 2, :], per_expert[:, 1, :], ALU.subtract))
            step(route, dve.tensor_scalar(per_expert[:, 3, :], per_expert[:, 3, :], float(P), None, ALU.mult))
            step(route, dve.tensor_tensor(upto[:], upto[:], counts, ALU.subtract))
            step(route, dve.tensor_tensor(upto[:], upto[:], ranks, ALU.add))
            step(route, dve.tensor_tensor(upto[:], upto[:], wide(per_expert[:, 3, :], J), ALU.add))
            step(route, dve.tensor_tensor(upto[:], upto[:], chosen[:], ALU.mult))
            step(route, dve.tensor_reduce(pos[:], upto[:].rearrange("p e j -> p j e"), AX.X, ALU.add))
            step(route, dve.tensor_copy(pos_u[:], pos[:]))
            route.inc(dve.tensor_scalar(pos_hi[:], pos_u[:], P.bit_length() - 1, None, ALU.logical_shift_right))
            step(route, dve.tensor_scalar(pos_lo[:], pos_u[:], P - 1, None, ALU.bitwise_and))
            route.inc(dve.tensor_copy(tile_of[:], pos_hi[:]))
            step(route, dve.tensor_copy(row_of[:], pos_lo[:]))
            step(route, dve.tensor_tensor(tile_hot, tall(place_no[:, 0:NP], J), wide(tile_of[:], NP), ALU.is_equal))
            hots_ready.inc(dve.tensor_tensor(tile_hot, tile_hot, wide(token_no[:], NP), ALU.mult))
            dve.wait_ge(acc_begun.sem, B)
            for k in range(2):
                half = slice(k * NT, (k + 1) * NT)
                hots_ready.inc(dve.tensor_tensor(row_hot[:, half], tall(place_no[:], NT), wide(row_of[:, half], P), ALU.is_equal))
            step(route, dve.tensor_tensor(ended[:], wide(place_no[0:1, 0:NP], E), tall(per_expert[0:1, 2, :], NP), ALU.is_ge))
            step(route, dve.tensor_reduce(expert_f[:], ended[:], AX.X, ALU.add))
            step(route, dve.tensor_scalar(expert_f[:], expert_f[:], float(E - 1), None, ALU.min))
            table_ready.inc(dve.tensor_copy(expert_of[:], expert_f[:]))
            dve.wait_ge(placed.sem, 1)
            table_ready.inc(dve.tensor_copy(token_of[:], ps_d[0][:, 0:NP]))
            dve.wait_ge(exp_ready.sem, 2)
            step(route, dve.tensor_reduce(row(2), shifted[:], AX.X, ALU.add))
            step(route, dve.reciprocal(row(3), row(2)))
            step(route, dve.tensor_tensor(row(4), row(1), row(3), ALU.mult))
            step(route, dve.scalar_tensor_tensor(row(5), row(3), 1e-9, row(4), ALU.add, ALU.add))
            step(route, dve.reciprocal(row(6), row(5)))
            step(route, dve.tensor_tensor(row(3), row(3), row(6), ALU.mult))
            step(route, dve.tensor_tensor(row(4), row(4), row(6), ALU.mult))

            def keep_xT(ee, k):
                tile_done(dve, x_turned, ee, k)
                tile_done(dve, up_made, ee, k - 2)
                dve.tensor_tensor(xT[:, k % 2, :].rearrange("p (t o) -> p t o", o=P), ps_x[:, :].rearrange("p (t o) -> p t o", o=P),
                                  wide(norm_col[:], P), ALU.mult).then_inc(xT_ready.sem, 1)

            def turn(ee, first, last):
                for q in range(2):
                    if not (last and q == 1):
                        keep_xT(ee, q + 1)
                    tile_done(dve, up_made, ee, q)
                    tile_done(dve, silu_ready, ee, q)
                    tile_done(dve, act_turned, ee, q - 2)
                    dve.tensor_tensor(act_row[:, q, :], ps_u[q][:, 0:I], silu[:, q, :], ALU.mult).then_inc(row_ready.sem, 1)

            keep_xT(0, 0)
            run_tiles(dve, turn)

            def normed(c):
                dve.wait_ge(rstd_ready.sem, c + 1)
                for i in range(ST):
                    t = ST * c + i
                    out_ready.inc(dve.tensor_scalar(acc[:, t, :], acc[:, t, :], mv[:, t, 0:1], rstd[:, t:t + 1], ALU.subtract, ALU.mult))

            for c in range(B):
                for k in range(2):
                    for i in range(ST):
                        t = ST * c + i
                        n = 2 * ST * c + ST * k + i
                        dve.wait_ge(result_in[n % RING].sem, 16 * (n // RING + 1))
                        if k:
                            dve.wait_ge(added.sem, n - ST + 1)
                        added.inc(dve.scalar_tensor_tensor(acc[:, t, :], results[:, n % RING, :], small[:, 3 + k, t:t + 1],
                                                           acc[:, t, :], ALU.mult, ALU.add))
                for i in range(ST):
                    dve.wait_ge(added.sem, 2 * ST * (c + 1) - ST + i + 1)
                    ln_step.inc(dve.bn_stats(stats[:, i, :], acc[:, ST * c + i, :]))
                dve.wait_ge(ln_step.sem, ln_step.n)
                for i in range(ST):
                    ln_step.inc(dve.bn_aggr(mv[:, ST * c + i, :], stats[:, i, :]))
                dve.wait_ge(ln_step.sem, ln_step.n)
                step(ln_step, dve.tensor_scalar(veps[:, ST * c:ST * (c + 1)], mv[:, ST * c:ST * (c + 1), 1], 1e-5, None, ALU.add))
                assert ln_step.n == (2 * ST + 1) * (c + 1)
                if c:
                    normed(c - 1)
            normed(B - 1)

        @block.gpsimd
        def _(pool):
            pool.wait_ge(consts_ready.sem, 2)
            for c in range(B):
                own = slice(ST * c, ST * (c + 1))
                pool.wait_ge(eps_added.sem, c + 1)
                hr_ready.inc(pool.tensor_tensor(hr[:, own], ssv[:, own], mhalf[:, own], ALU.pow))
                pool.wait_ge(acc_in[c].sem, 16)
                acc_begun.inc(pool.tensor_tensor(acc[:, own, :], acc[:, own, :], hbuf[:, c % 2], ALU.add))
            pool.wait_ge(table_ready.sem, 2)
            for stored in hn_stored:
                pool.wait_ge(stored.sem, stored.n)

            def turn(ee, first, last):
                for q in range(2):
                    tile_done(pool, x_turned, ee, q - 2)
                    pool.tensor_copy(rows_of[q][:, :], token_of[:, at(ee, q)]).then_inc(rows_copied.sem, 1)
                    tile_done(pool, rows_copied, ee, q)
                    pool.sem_inc(rows_seen.sem, 1)
                    pool.indirect_dma_start(xg[:, q, :], None, hn_dram,
                                            bass.IndirectOffsetOnAxis(ap=rows_of[q][:, :], axis=0)).then_inc(gathered[q].sem, 16)

            def rsqrt(c):
                own = slice(ST * c, ST * (c + 1))
                pool.wait_ge(ln_step.sem, (2 * ST + 1) * (c + 1))
                rstd_ready.inc(pool.tensor_tensor(rstd[:, own], veps[:, own], mhalf[:, own], ALU.pow))

            run_tiles(pool, turn)
            for q in range(2):
                pool.wait_ge(y_stored[q].sem, 16 * (NP // 2))
            for c in range(B):
                for k in range(2):
                    for i in range(ST):
                        t = ST * c + i
                        n = 2 * ST * c + ST * k + i
                        if n >= RING:
                            pool.wait_ge(added.sem, n - RING + 1)
                        result_in[n % RING].inc(pool.indirect_dma_start(
                            results[:, n % RING, :], None, y_dram,
                            bass.IndirectOffsetOnAxis(ap=pos_u[:, k * NT + t:k * NT + t + 1], axis=0)), 16)
                if c:
                    rsqrt(c - 1)
            rsqrt(B - 1)


def build(nc, io, out):
    B, S, F = io["x"].shape
    x2 = nc.dram_tensor("x2", (B, S, F), F32, kind="Internal").ap()
    bc_dram = nc.dram_tensor("bc_rows", (2 * io["A_log"].shape[1], S), F32, kind="Internal").ap()
    hidden = nc.dram_tensor("hidden", (B, S, F), F32, kind="Internal").ap()
    attention_and_scan(nc, io, x2, bc_dram)
    grouped_attention(nc, io, x2, hidden)
    mixture_of_experts(nc, io, x2, hidden, out)


def shape_constants(length, width):
    freqs = (1.0 / np.float32(1000000.0) ** (np.arange(0, width, 2, dtype=np.float32) / np.float32(width))).astype(np.float32)
    angle = np.outer(np.arange(length, dtype=np.float32), freqs).astype(np.float32)
    cos, sin = np.cos(angle), np.sin(angle)
    return {"cos": np.concatenate([cos, cos], 1), "sin": np.concatenate([-sin, sin], 1),
            "mask": np.triu(np.ones((P, P), np.float32), 1) * np.float32(-1e30)}


def laid_out(inputs):
    i = {k: np.asarray(a) for k, a in inputs.items()}

    def T(a):
        return np.ascontiguousarray(np.swapaxes(a, -1, -2))

    def columns(a):
        return np.ascontiguousarray(a.reshape(-1, P).T)

    a, s = "L0_attn_", "L0_xattn_"
    got = {"x": i["x"], "xT": T(i["x"]), "ctxT": T(i["ctx_1024"])}
    for w in "qkvo":
        got["W" + w] = i[a + "W" + w]
    got |= {"bq": columns(i[a + "bq"]), "bk": columns(i[a + "bk"]), "bv": i[a + "bv"][None], "bo": i[a + "bo"][None]}
    got |= {"in_wT": T(i[s + "in_proj_w"]), "conv_w": i[s + "conv_w"][:, 0, :], "conv_b": columns(i[s + "conv_b"]),
            "x_wT": T(i[s + "x_proj_w"]), "dt_wT": T(i[s + "dt_proj_w"]), "dt_b": columns(i[s + "dt_proj_b"]),
            "A_log": i[s + "A_log"], "Dskip": columns(i[s + "D"])}
    f = "L0_ffn_"
    got |= {"q_wT": T(i[f + "q_w"]), "k_wT": T(i[f + "k_w"]), "v_wT": T(i[f + "v_w"]), "o_wT": T(i[f + "o_w"]),
            "attn_norm": columns(i[f + "attn_norm_w"]), "q_norm": i[f + "q_norm_w"][None], "k_norm": i[f + "k_norm_w"][None]}
    got |= shape_constants(i["x"].shape[1], i[f + "q_norm_w"].shape[0])
    got |= {"gate_wT": T(i[f + "gate_w"]), "ffn_norm": columns(i[f + "ffn_norm_w"]),
            "wgT": T(i[f + "wg"]), "wuT": T(i[f + "wu"]), "wdT": T(i[f + "wd"]),
            "before": np.triu(np.ones((P, P), np.float32), 1)}
    tokens, experts = i["x"].shape[0] * i["x"].shape[1], i[f + "gate_w"].shape[0]
    number = np.arange(tokens, dtype=np.float32).reshape(-1, P).T
    first = np.ones((experts, 2 * tokens // P), np.float32)
    first[:, 0] = 0
    got |= {"place_no": np.arange(P, dtype=np.float32)[None], "token_no": np.concatenate([number, number], 1), "new_expert": first.reshape(1, -1)}
    got["ident"] = np.eye(P, dtype=np.float32)
    return {k: np.ascontiguousarray(v) for k, v in got.items()}


def kernel(**inputs):
    import concourse.bacc as bacc
    from concourse.bass_utils import run_bass_kernel_spmd

    data = laid_out(inputs)
    nc = bacc.Bacc("TRN2", target_bir_lowering=False, num_devices=1)
    arrays, io = {}, {}
    for name, a in data.items():
        arrays["in_" + name] = a
        io[name] = nc.dram_tensor("in_" + name, a.shape, mybir.dt.from_np(a.dtype), kind="ExternalInput").ap()
    out = nc.dram_tensor("out", inputs["x"].shape, F32, kind="ExternalOutput").ap()
    build(nc, io, out)
    return run_bass_kernel_spmd(nc, [arrays], core_ids=[0]).results[0]["out"]
```
